# Optimizing a Trainium2 kernel written in Bass

```python
import numpy as np
import jax
import jax.numpy as jnp

def _softmax(x, axis=-1):
    return jax.nn.softmax(x, axis=axis)

def _gelu(x):
    return jax.nn.gelu(x, approximate=True)

def _silu(x):
    return jax.nn.silu(x)

def _sigmoid(x):
    return jax.nn.sigmoid(x)

def _layernorm(x, axis=-1, eps=1e-05):
    m = jnp.mean(x, axis=axis, keepdims=True)
    v = jnp.var(x, axis=axis, keepdims=True)
    return (x - m) / jnp.sqrt(v + eps)

def _scatter_add(tgt, idx, src, axis=0):
    return tgt.at[idx].add(src)

def _segment_sum(src, seg, n):
    return jax.ops.segment_sum(src, seg, n)
kernel_name = 'mk_seq_postln_d2_jaxref_r4_b85cca'

def setup_inputs(seed: int=0):
    np.random.seed(seed)
    _w = jnp.asarray

    def _L0_attn_setup():
        import jax, jax.numpy as jnp
        import numpy as np
        D_IN = 256
        D_ATT = 256
        D_OUT = 256
        N, S = (8, 1024)
        key = jax.random.key(seed)
        ks = jax.random.split(key, 5)
        sc_in = 1.0 / np.sqrt(D_IN)
        sc_att = 1.0 / np.sqrt(D_ATT)
        return {'x': jax.random.normal(ks[0], (N, S, D_IN), dtype=jnp.float32), 'Wq': jax.random.normal(ks[1], (D_IN, D_ATT), dtype=jnp.float32) * sc_in, 'bq': jnp.zeros((D_ATT,), dtype=jnp.float32), 'Wk': jax.random.normal(ks[2], (D_IN, D_ATT), dtype=jnp.float32) * sc_in, 'bk': jnp.zeros((D_ATT,), dtype=jnp.float32), 'Wv': jax.random.normal(ks[3], (D_IN, D_ATT), dtype=jnp.float32) * sc_in, 'bv': jnp.zeros((D_ATT,), dtype=jnp.float32), 'Wo': jax.random.normal(ks[4], (D_ATT, D_OUT), dtype=jnp.float32) * sc_att, 'bo': jnp.zeros((D_OUT,), dtype=jnp.float32)}
    _L0_attn_in = _L0_attn_setup()

    def _L0_ffn_setup():
        import jax, jax.numpy as jnp
        import numpy as np
        B, N, D = (4, 512, 256)
        SPARSITY = 0.01
        key = jax.random.key(seed)
        k1, k2, k3 = jax.random.split(key, 3)
        x = jax.random.normal(k1, (B, N, D), dtype=jnp.float32)
        spatial = jax.random.normal(k2, (D, D), dtype=jnp.float32) * 0.02
        freq = jnp.fft.fft(spatial, axis=-1)
        k = int(D * SPARSITY)
        mag = jnp.abs(freq)
        kth = jax.lax.top_k(mag, k)[0][:, -1:]
        w_sparse = jnp.where(mag >= kth, freq, 0.0 + 0j)
        bias = jax.random.normal(k3, (D,), dtype=jnp.float32) * 0.01
        return {'x': x, 'w_freq_real': jnp.real(w_sparse).astype(jnp.float32), 'w_freq_imag': jnp.imag(w_sparse).astype(jnp.float32), 'bias': bias}
    _L0_ffn_in = _L0_ffn_setup()

    def _L1_attn_setup():
        import jax, jax.numpy as jnp
        import numpy as np
        import math
        D_MODEL = 256
        NUM_HEADS = 16
        key = jax.random.key(seed)
        k1, k2, k3 = jax.random.split(key, 3)
        B, S = (2, 512)
        x = jax.random.normal(k1, (B, S, D_MODEL), dtype=jnp.float32)
        W_kqv = jax.random.normal(k2, (D_MODEL, 3 * D_MODEL), dtype=jnp.float32) * (1.0 / math.sqrt(D_MODEL))
        m = jax.random.normal(k3, (NUM_HEADS, 1, 1), dtype=jnp.float32)
        return {'x': x, 'W_kqv': W_kqv, 'm': m}
    _L1_attn_in = _L1_attn_setup()

    def _L1_ffn_setup():
        import jax, jax.numpy as jnp
        import numpy as np
        S_LEN, BATCH, HIDDEN = (512, 2, 256)
        N_HEADS, N_KV = (16, 8)
        N_EXP, TOP_K, CAP_F = (8, 2, 1.25)
        FFN = 1024
        HEAD_DIM = HIDDEN // N_HEADS
        Q_PER_KV = N_HEADS // N_KV
        EPS = 1e-05
        NEG = -1000000000.0

        def _ln(x, w, b):
            mu = jnp.mean(x, -1, keepdims=True)
            var = jnp.var(x, -1, keepdims=True)
            return (x - mu) * jax.lax.rsqrt(var + EPS) * w + b

        def _forward(hidden_states, ln1_weight, ln1_bias, ln2_weight, ln2_bias, qkv_weight, proj_weight, router_weight, moe_w1, moe_w2):
            S, B, H = hidden_states.shape
            ln1 = _ln(hidden_states, ln1_weight, ln1_bias)
            qkv = (ln1 @ qkv_weight.T).reshape(S, B, N_KV, (Q_PER_KV + 2) * HEAD_DIM)
            q_dim = Q_PER_KV * HEAD_DIM
            q = qkv[..., :q_dim].reshape(S, B, N_HEADS, HEAD_DIM)
            k = jnp.repeat(qkv[..., q_dim:q_dim + HEAD_DIM], Q_PER_KV, axis=2)
            v = jnp.repeat(qkv[..., q_dim + HEAD_DIM:], Q_PER_KV, axis=2)
            scores = jnp.einsum('sbhd,tbhd->bhst', q, k) / jnp.sqrt(jnp.float32(HEAD_DIM))
            causal = jnp.tril(jnp.ones((S, S), bool))
            attn = jax.nn.softmax(jnp.where(causal[None, None], scores, NEG), axis=-1)
            attn_out = jnp.einsum('bhst,tbhd->sbhd', attn, v).reshape(S, B, H)
            hidden_after_attn = hidden_states + attn_out @ proj_weight.T
            x = _ln(hidden_after_attn, ln2_weight, ln2_bias).reshape(-1, H)
            N = S * B
            probs = jax.nn.softmax(x.astype(jnp.float32) @ router_weight, axis=-1)
            top_p, top_i = jax.lax.top_k(probs, TOP_K)
            top_p = top_p / jnp.sum(top_p, -1, keepdims=True)
            flat_exp = top_i.reshape(-1)
            order = jnp.argsort(flat_exp)
            sorted_exp = flat_exp[order]
            counts = jnp.bincount(sorted_exp, length=N_EXP)
            offsets = jnp.concatenate([jnp.zeros((1,), counts.dtype), jnp.cumsum(counts)])
            within = jnp.arange(N * TOP_K) - offsets[sorted_exp]
            cap = int(np.ceil(N * TOP_K / N_EXP * CAP_F))
            keep = within < cap
            slot = jnp.where(keep, sorted_exp * cap + within, N_EXP * cap)
            tok_id = order // TOP_K
            padded_tokens = jnp.zeros((N_EXP * cap + 1, H), x.dtype).at[slot].set(x[tok_id])[:-1]
            padded_probs = jnp.zeros((N_EXP * cap + 1,), jnp.float32).at[slot].set(top_p.reshape(-1)[order])[:-1]
            padded_ids = jnp.zeros((N_EXP * cap + 1,), jnp.int32).at[slot].set(tok_id.astype(jnp.int32))[:-1]
            exp_in = padded_tokens.reshape(N_EXP, cap, H)
            act = jax.nn.gelu(jnp.einsum('ech,ehf->ecf', exp_in, moe_w1), approximate=False)
            exp_out = jnp.einsum('ecf,efh->ech', act, moe_w2).reshape(N_EXP * cap, H)
            weighted = exp_out * padded_probs[:, None].astype(exp_out.dtype)
            moe = jnp.zeros((N, H), exp_out.dtype).at[padded_ids].add(weighted)
            return hidden_after_attn + moe.reshape(S, B, H)
        ks = jax.random.split(jax.random.key(seed), 6)
        qkv_out = N_KV * (Q_PER_KV + 2) * HEAD_DIM
        sc = 0.02
        return {'hidden_states': jax.random.normal(ks[0], (S_LEN, BATCH, HIDDEN), jnp.float32), 'ln1_weight': jnp.ones((HIDDEN,), jnp.float32), 'ln1_bias': jnp.zeros((HIDDEN,), jnp.float32), 'ln2_weight': jnp.ones((HIDDEN,), jnp.float32), 'ln2_bias': jnp.zeros((HIDDEN,), jnp.float32), 'qkv_weight': jax.random.normal(ks[1], (qkv_out, HIDDEN), jnp.float32) * sc, 'proj_weight': jax.random.normal(ks[2], (HIDDEN, HIDDEN), jnp.float32) * sc, 'router_weight': jax.random.normal(ks[3], (HIDDEN, N_EXP), jnp.float32) * sc, 'moe_w1': jax.random.normal(ks[4], (N_EXP, HIDDEN, FFN), jnp.float32) * sc, 'moe_w2': jax.random.normal(ks[5], (N_EXP, FFN, HIDDEN), jnp.float32) * sc}
    _L1_ffn_in = _L1_ffn_setup()
    _d = {'L0_attn_x': _L0_attn_in['x'], 'L0_attn_Wq': _L0_attn_in['Wq'], 'L0_attn_bq': _L0_attn_in['bq'], 'L0_attn_Wk': _L0_attn_in['Wk'], 'L0_attn_bk': _L0_attn_in['bk'], 'L0_attn_Wv': _L0_attn_in['Wv'], 'L0_attn_bv': _L0_attn_in['bv'], 'L0_attn_Wo': _L0_attn_in['Wo'], 'L0_attn_bo': _L0_attn_in['bo'], 'L0_ffn_w_freq_real': _L0_ffn_in['w_freq_real'], 'L0_ffn_w_freq_imag': _L0_ffn_in['w_freq_imag'], 'L0_ffn_bias': _L0_ffn_in['bias'], 'L1_attn_W_kqv': _L1_attn_in['W_kqv'], 'L1_attn_m': _L1_attn_in['m'], 'L1_ffn_ln1_weight': _L1_ffn_in['ln1_weight'], 'L1_ffn_ln1_bias': _L1_ffn_in['ln1_bias'], 'L1_ffn_ln2_weight': _L1_ffn_in['ln2_weight'], 'L1_ffn_ln2_bias': _L1_ffn_in['ln2_bias'], 'L1_ffn_qkv_weight': _L1_ffn_in['qkv_weight'], 'L1_ffn_proj_weight': _L1_ffn_in['proj_weight'], 'L1_ffn_router_weight': _L1_ffn_in['router_weight'], 'L1_ffn_moe_w1': _L1_ffn_in['moe_w1'], 'L1_ffn_moe_w2': _L1_ffn_in['moe_w2']}
    _x0 = _d['L0_attn_x']
    _d['L0_attn_x'] = jax.random.normal(jax.random.fold_in(jax.random.key(seed), 1), (8, 1024, 256), dtype=_x0.dtype)
    del _x0
    return _d

def reference(L0_attn_x, L0_attn_Wq, L0_attn_bq, L0_attn_Wk, L0_attn_bk, L0_attn_Wv, L0_attn_bv, L0_attn_Wo, L0_attn_bo, L0_ffn_w_freq_real, L0_ffn_w_freq_imag, L0_ffn_bias, L1_attn_W_kqv, L1_attn_m, L1_ffn_ln1_weight, L1_ffn_ln1_bias, L1_ffn_ln2_weight, L1_ffn_ln2_bias, L1_ffn_qkv_weight, L1_ffn_proj_weight, L1_ffn_router_weight, L1_ffn_moe_w1, L1_ffn_moe_w2):

    def _L0_attn_ref(x, Wq, bq, Wk, bk, Wv, bv, Wo, bo):
        import jax, jax.numpy as jnp
        import numpy as np
        D_IN = 256
        D_ATT = 256
        D_OUT = 256
        N, S = (8, 1024)
        query = jnp.einsum('nsd,dh->nsh', x, Wq) + bq
        keyp = jnp.einsum('nsd,dh->nsh', x, Wk) + bk
        value = jnp.einsum('nsd,dh->nsh', x, Wv) + bv
        fmap = lambda t: jax.nn.elu(t) + 1.0
        Q = fmap(query)
        K = fmap(keyp)
        KV = jnp.sum(K * value, axis=1)
        Ksum = jnp.sum(K, axis=1)
        Z = 1.0 / (Q * Ksum[:, None, :] + 1e-06)
        V = Q * KV[:, None, :] * Z
        out = jnp.einsum('nsh,ho->nso', V, Wo) + bo
        return jax.nn.gelu(out)

    def _L0_ffn_ref(x, w_freq_real, w_freq_imag, bias):
        import jax, jax.numpy as jnp
        import numpy as np
        B, N, D = (4, 512, 256)
        SPARSITY = 0.01
        w = jax.lax.complex(w_freq_real, w_freq_imag)
        x_freq = jnp.fft.fft(x, axis=-1)
        y_freq = jnp.einsum('bnd,do->bno', x_freq, w)
        y = jnp.real(jnp.fft.ifft(y_freq, axis=-1))
        return y + bias

    def _L1_attn_ref(x, W_kqv, m):
        import jax, jax.numpy as jnp
        import numpy as np
        import math
        D_MODEL = 256
        NUM_HEADS = 16
        B, S, D = x.shape
        H = NUM_HEADS
        hd = D // H
        scale = math.sqrt(D)
        kqv = x @ W_kqv
        k, q, v = jnp.split(kqv, 3, axis=-1)
        q = q.reshape(B, S, H, hd)
        k = k.reshape(B, S, H, hd)
        v = v.reshape(B, S, H, hd)
        rel = (jnp.arange(S)[None, :] - jnp.arange(S)[:, None]).astype(x.dtype)
        bias = m[None, :, :, :] * rel[None, None, :, :]
        score = jnp.einsum('bqhd,bkhd->bhqk', q, k) / scale + bias
        causal = jnp.tril(jnp.ones((S, S), dtype=bool))
        score = jnp.where(causal[None, None, :, :], score, -jnp.inf)
        attn = jax.nn.softmax(score, axis=-1)
        out = jnp.einsum('bhqk,bkhd->bqhd', attn, v).reshape(B, S, D)
        return out

    def _L1_ffn_ref(hidden_states, ln1_weight, ln1_bias, ln2_weight, ln2_bias, qkv_weight, proj_weight, router_weight, moe_w1, moe_w2):
        import jax, jax.numpy as jnp
        import numpy as np
        S_LEN, BATCH, HIDDEN = (512, 2, 256)
        N_HEADS, N_KV = (16, 8)
        N_EXP, TOP_K, CAP_F = (8, 2, 1.25)
        FFN = 1024
        HEAD_DIM = HIDDEN // N_HEADS
        Q_PER_KV = N_HEADS // N_KV
        EPS = 1e-05
        NEG = -1000000000.0

        def _ln(x, w, b):
            mu = jnp.mean(x, -1, keepdims=True)
            var = jnp.var(x, -1, keepdims=True)
            return (x - mu) * jax.lax.rsqrt(var + EPS) * w + b

        def _forward(hidden_states, ln1_weight, ln1_bias, ln2_weight, ln2_bias, qkv_weight, proj_weight, router_weight, moe_w1, moe_w2):
            S, B, H = hidden_states.shape
            ln1 = _ln(hidden_states, ln1_weight, ln1_bias)
            qkv = (ln1 @ qkv_weight.T).reshape(S, B, N_KV, (Q_PER_KV + 2) * HEAD_DIM)
            q_dim = Q_PER_KV * HEAD_DIM
            q = qkv[..., :q_dim].reshape(S, B, N_HEADS, HEAD_DIM)
            k = jnp.repeat(qkv[..., q_dim:q_dim + HEAD_DIM], Q_PER_KV, axis=2)
            v = jnp.repeat(qkv[..., q_dim + HEAD_DIM:], Q_PER_KV, axis=2)
            scores = jnp.einsum('sbhd,tbhd->bhst', q, k) / jnp.sqrt(jnp.float32(HEAD_DIM))
            causal = jnp.tril(jnp.ones((S, S), bool))
            attn = jax.nn.softmax(jnp.where(causal[None, None], scores, NEG), axis=-1)
            attn_out = jnp.einsum('bhst,tbhd->sbhd', attn, v).reshape(S, B, H)
            hidden_after_attn = hidden_states + attn_out @ proj_weight.T
            x = _ln(hidden_after_attn, ln2_weight, ln2_bias).reshape(-1, H)
            N = S * B
            probs = jax.nn.softmax(x.astype(jnp.float32) @ router_weight, axis=-1)
            top_p, top_i = jax.lax.top_k(probs, TOP_K)
            top_p = top_p / jnp.sum(top_p, -1, keepdims=True)
            flat_exp = top_i.reshape(-1)
            order = jnp.argsort(flat_exp)
            sorted_exp = flat_exp[order]
            counts = jnp.bincount(sorted_exp, length=N_EXP)
            offsets = jnp.concatenate([jnp.zeros((1,), counts.dtype), jnp.cumsum(counts)])
            within = jnp.arange(N * TOP_K) - offsets[sorted_exp]
            cap = int(np.ceil(N * TOP_K / N_EXP * CAP_F))
            keep = within < cap
            slot = jnp.where(keep, sorted_exp * cap + within, N_EXP * cap)
            tok_id = order // TOP_K
            padded_tokens = jnp.zeros((N_EXP * cap + 1, H), x.dtype).at[slot].set(x[tok_id])[:-1]
            padded_probs = jnp.zeros((N_EXP * cap + 1,), jnp.float32).at[slot].set(top_p.reshape(-1)[order])[:-1]
            padded_ids = jnp.zeros((N_EXP * cap + 1,), jnp.int32).at[slot].set(tok_id.astype(jnp.int32))[:-1]
            exp_in = padded_tokens.reshape(N_EXP, cap, H)
            act = jax.nn.gelu(jnp.einsum('ech,ehf->ecf', exp_in, moe_w1), approximate=False)
            exp_out = jnp.einsum('ecf,efh->ech', act, moe_w2).reshape(N_EXP * cap, H)
            weighted = exp_out * padded_probs[:, None].astype(exp_out.dtype)
            moe = jnp.zeros((N, H), exp_out.dtype).at[padded_ids].add(weighted)
            return hidden_after_attn + moe.reshape(S, B, H)
        return _forward(hidden_states, ln1_weight, ln1_bias, ln2_weight, ln2_bias, qkv_weight, proj_weight, router_weight, moe_w1, moe_w2)
    x = L0_attn_x
    x = _layernorm(x + _L0_attn_ref(x, L0_attn_Wq, L0_attn_bq, L0_attn_Wk, L0_attn_bk, L0_attn_Wv, L0_attn_bv, L0_attn_Wo, L0_attn_bo), axis=-1)
    x = _layernorm(x + _L0_ffn_ref(x, L0_ffn_w_freq_real, L0_ffn_w_freq_imag, L0_ffn_bias), axis=-1)
    x = _layernorm(x + _L1_attn_ref(x, L1_attn_W_kqv, L1_attn_m), axis=-1)
    x = _layernorm(x + _L1_ffn_ref(x, L1_ffn_ln1_weight, L1_ffn_ln1_bias, L1_ffn_ln2_weight, L1_ffn_ln2_bias, L1_ffn_qkv_weight, L1_ffn_proj_weight, L1_ffn_router_weight, L1_ffn_moe_w1, L1_ffn_moe_w2), axis=-1)
    return x

_drawn_inputs = setup_inputs


def setup_inputs(seed=0):
    import zlib

    import numpy as np

    out = dict(_drawn_inputs(seed))
    spreads = {'L0_attn_bq': (0.0, 2.0),
     'L0_attn_bk': (0.0, 2.0),
     'L0_attn_bv': (0.0, 0.1),
     'L0_attn_bo': (0.0, 0.1),
     'L1_ffn_ln1_weight': (1.0, 0.6),
     'L1_ffn_ln1_bias': (0.0, 0.8),
     'L1_ffn_ln2_weight': (1.0, 0.6),
     'L1_ffn_ln2_bias': (0.0, 0.66)}
    factors = {'L0_attn_Wq': 54.256, 'L0_ffn_bias': 5.2}
    for name, (base, spread) in spreads.items():
        noise = np.random.default_rng([zlib.crc32(name.encode()), seed]).standard_normal(out[name].shape)
        drawn = base * np.exp(spread * noise) if base else spread * noise
        out[name] = jnp.asarray(drawn.astype(out[name].dtype))
    for name, factor in factors.items():
        out[name] = (out[name] * factor).astype(out[name].dtype)
    return out
```

```python
from contextlib import ExitStack

import numpy as np
import concourse.bass as bass
from concourse import mybir

F32 = mybir.dt.float32
BF16 = mybir.dt.bfloat16
U32 = mybir.dt.uint32
ALU = mybir.AluOpType
ACT = mybir.ActivationFunctionType
AX = mybir.AxisListType

P = 128
N, S, D = 8, 1024, 256
DC = D // P
NT = S // P
NPAIR = NT // 2
T = N * S
EPS = 1e-5
BIG = 1e30


class Signal:

    def __init__(self, ctx, nc, name, per, prime=0, unit=1):
        self.sem = ctx.enter_context(nc.semaphore(name))
        self.per, self.prime, self.unit = per, prime, unit
        self.start = prime * unit

    def at(self, i, k=0):
        return i * (self.per * self.unit) + (k + 1 + self.prime) * self.unit


def spectral_matrix(nc, w_real, w_imag, cos, nsin, cos_n, nsin_n, spectral):
    with ExitStack() as ctx:
        def sb(name, shape, dt=F32):
            return ctx.enter_context(nc.sbuf_tensor("m_" + name, shape, dt))

        wr = sb("wr", [P, DC, D])
        wi = sb("wi", [P, DC, D])
        c = sb("c", [P, DC, D])
        ns = sb("ns", [P, DC, D])
        ps = sb("ps", [P, DC, D])
        cn = sb("cn", [P, DC, D])
        nsn = sb("nsn", [P, DC, D])
        re_t = sb("re_t", [P, DC, D])
        im_t = sb("im_t", [P, DC, D])
        m = sb("m", [P, DC, D])
        bank = [ctx.enter_context(nc.psum_tensor(f"m_bank{i}", [P, 512], F32)) for i in range(6)]
        loaded = ctx.enter_context(nc.semaphore("m_loaded"))
        sin_ready = ctx.enter_context(nc.semaphore("m_sin_ready"))
        product = ctx.enter_context(nc.semaphore("m_product"))
        copied = ctx.enter_context(nc.semaphore("m_copied"))
        stored = ctx.enter_context(nc.semaphore("m_stored"))
        block = ctx.enter_context(nc.Block())

        @block.sync
        def _(sp):
            for dst, src in ((wr, w_real), (wi, w_imag), (c, cos), (ns, nsin), (cn, cos_n), (nsn, nsin_n)):
                sp.dma_start(dst[:], src.rearrange("(c p) n -> p c n", p=P)).then_inc(loaded, 16)
            sp.wait_ge(copied, 6)
            sp.dma_start(spectral.rearrange("(c p) n -> p c n", p=P), m[:]).then_inc(stored, 16)
            sp.wait_ge(stored, 16)

        @block.tensor
        def _(pe):
            pe.wait_ge(loaded, 6 * 16)
            pe.wait_ge(sin_ready, 1)
            for oc in range(DC):
                cols = slice(oc * P, oc * P + P)
                for n, (a, b) in enumerate(((wi, ps), (wr, ns))):
                    main = wr if n == 0 else wi
                    out = bank[2 * oc + n][:, 0:D]
                    for k in range(DC):
                        pe.matmul(out, main[:, k, cols], c[:, k, :], start=(k == 0), stop=False)
                    for k in range(DC):
                        mm = pe.matmul(out, a[:, k, cols], b[:, k, :], start=False, stop=(k == DC - 1))
                    mm.then_inc(product, 1)
            pe.wait_ge(copied, 4)
            for dc in range(DC):
                cols = slice(dc * P, dc * P + P)
                out = bank[4 + dc][:, 0:D]
                for k in range(DC):
                    pe.matmul(out, re_t[:, k, cols], cn[:, k, :], start=(k == 0), stop=False)
                for k in range(DC):
                    mm = pe.matmul(out, im_t[:, k, cols], nsn[:, k, :], start=False, stop=(k == DC - 1))
                mm.then_inc(product, 1)

        @block.vector
        def _(dve):
            dve.wait_ge(loaded, 6 * 16)
            dve.tensor_scalar(ps[:], ns[:], -1.0, None, ALU.mult).then_inc(sin_ready, 1)
            for n, dst in enumerate((re_t[:, 0, :], im_t[:, 0, :], re_t[:, 1, :], im_t[:, 1, :], m[:, 0, :], m[:, 1, :])):
                dve.wait_ge(product, n + 1)
                dve.tensor_copy(dst, bank[n][:, 0:D]).then_inc(copied, 1)


def linear_attention_and_spectral(nc, xT, x, wq, bq, wk, bk, wv, bv, wo, bo2, bias2, ident, spectral, x2, x2T):
    KQ = 8
    with ExitStack() as ctx:
        def sb(name, shape, dt=F32):
            return ctx.enter_context(nc.sbuf_tensor("a_" + name, shape, dt))

        def sig(name, per, prime=0, unit=1):
            return Signal(ctx, nc, "a_" + name, per, prime, unit)

        w = {k: sb("w" + k, [P, DC, D]) for k in "qkvom"}
        b = {k: sb("b" + k, [P, DC]) for k in "qkv"}
        nb = {k: sb("nb" + k, [P, DC]) for k in "qk"}
        n_t = sb("n_t", [P, 2, 512])
        bo_b = sb("bo_b", [P, 2, D])
        bias_b = sb("bias_b", [P, 2, D])
        eye = sb("eye", [P, P])
        neg_half = sb("neg_half", [P, 2])
        xt = sb("xt", [P, DC, S])
        xs = sb("xs", [P, NT, D])
        e_t = sb("e_t", [P, 2, 512])
        r_t = sb("r_t", [P, 2, 512])
        keys = sb("keys", [P, DC, S])
        q_t = sb("q_t", [P, 512])
        z_t = sb("z_t", [P, 512])
        junk = sb("junk", [P, 512])
        ksum2 = sb("ksum2", [P, DC, 2])
        kv2 = sb("kv2", [P, DC, 2])
        ksum = sb("ksum", [P, DC])
        kv = sb("kv", [P, DC])
        vp = sb("vp", [P, DC, S])
        pre = sb("pre", [P, 2, 2, D])
        g = sb("g", [P, 2, 2, D])
        h = sb("h", [P, NT, D])
        x1 = sb("x1", [P, NT, D])
        x1b = sb("x1b", [P, NT, D])
        h2 = sb("h2", [P, NT, D])
        x2s = sb("x2s", [P, NT, D])
        st = sb("st", [P, NT, 2, 6])
        mv = sb("mv", [P, 2, NT, 2])
        var = sb("var", [P, 2, NT])
        rstd = sb("rstd", [P, 2, NT])
        x1t = sb("x1t", [P, 2, DC, 2 * P])
        x2t = sb("x2t", [P, DC, S])
        act_bank = [ctx.enter_context(nc.psum_tensor(f"a_act{i}", [P, 512], F32)) for i in range(2)]
        v_bank = [ctx.enter_context(nc.psum_tensor(f"a_v{i}", [P, 512], F32)) for i in range(2)]
        o_bank = ctx.enter_context(nc.psum_tensor("a_o", [P, 512], F32))
        t1_bank = ctx.enter_context(nc.psum_tensor("a_t1", [P, 512], F32))
        m_bank = ctx.enter_context(nc.psum_tensor("a_mb", [P, 512], F32))
        t2_bank = ctx.enter_context(nc.psum_tensor("a_t2", [P, 512], F32))

        consts = sig("consts", 1, 0, 16)
        xt_in = sig("xt_in", 1, 0, 16)
        xs_in = sig("xs_in", 1, 0, 16)
        kq_ready = sig("kq_ready", KQ)
        v_ready = sig("v_ready", 4)
        er_ready = sig("er_ready", KQ, 2)
        k_done = sig("k_done", 4)
        er_read = sig("er_read", KQ, 2)
        v_done = sig("v_done", 4, 2)
        vp_done = sig("vp_done", 4)
        o_ready = sig("o_ready", NPAIR)
        o_added = sig("o_added", NPAIR, 1)
        gelu_done = sig("gelu_done", NPAIR, 2)
        h_done = sig("h_done", NPAIR, 2)
        mv1_done = sig("mv1_done", NPAIR)
        rstd1_done = sig("rstd1_done", NPAIR)
        x1_done = sig("x1_done", NPAIR)
        x1b_done = sig("x1b_done", NPAIR)
        t1_ready = sig("t1_ready", NPAIR)
        t1_copied = sig("t1_copied", NPAIR, 1)
        m_ready = sig("m_ready", NPAIR, 2)
        h2_done = sig("h2_done", NPAIR, 1)
        mv2_done = sig("mv2_done", NPAIR)
        rstd2_done = sig("rstd2_done", NPAIR)
        x2_done = sig("x2_done", NPAIR)
        t2_ready = sig("t2_ready", NPAIR)
        t2_copied = sig("t2_copied", NPAIR, 1)
        x2_out = sig("x2_out", 1, 1, 16)
        x2t_out = sig("x2t_out", 1, 1, 16)
        turns = sig("turns", 4)
        pool_turns = sig("pool_turns", 2 * NPAIR)
        eps_added = sig("eps_added", 2 * NPAIR)
        SLOTS = NPAIR + 4
        block = ctx.enter_context(nc.Block())

        @block.sync
        def _(sp):
            for k, src in zip("qkvom", (wq, wk, wv, wo, spectral)):
                sp.dma_start(w[k][:], src.rearrange("(c p) n -> p c n", p=P)).then_inc(consts.sem, 16)
            for k, src in zip("qkv", (bq, bk, bv)):
                sp.dma_start(b[k][:], src).then_inc(consts.sem, 16)
            sp.dma_start(bo_b[:], bo2).then_inc(consts.sem, 16)
            sp.dma_start(bias_b[:], bias2).then_inc(consts.sem, 16)
            sp.dma_start(eye[:], ident).then_inc(consts.sem, 16)
            sp.sem_inc(x2_out.sem, x2_out.start)
            sp.sem_inc(x2t_out.sem, x2t_out.start)
            sp.dma_start(xt[:], xT[0].rearrange("(c p) s -> p c s", p=P)).then_inc(xt_in.sem, 16)
            sp.dma_start(xs[:], x[0].rearrange("(t p) d -> p t d", p=P)).then_inc(xs_in.sem, 16)
            def turn(i, last):
                sp.wait_ge(kq_ready.sem, kq_ready.at(i, KQ - 1))
                sp.wait_ge(v_ready.sem, v_ready.at(i, 3))
                sp.sem_inc(turns.sem, 1)
                if not last:
                    sp.dma_start(xt[:], xT[bass.ds(i + 1, 1)].rearrange("o (c p) s -> p (o c) s", p=P)).then_inc(xt_in.sem, 16)
                sp.wait_ge(h_done.sem, h_done.at(i, NPAIR - 1))
                sp.sem_inc(turns.sem, 1)
                if not last:
                    sp.dma_start(xs[:], x[bass.ds(i + 1, 1)].rearrange("o (t p) d -> p (o t) d", p=P)).then_inc(xs_in.sem, 16)
                sp.wait_ge(x2_done.sem, x2_done.at(i, NPAIR - 1))
                sp.sem_inc(turns.sem, 1)
                sp.dma_start(x2[bass.ds(i, 1)].rearrange("o (t p) d -> p (o t) d", p=P), x2s[:]).then_inc(x2_out.sem, 16)
                sp.wait_ge(t2_copied.sem, t2_copied.at(i, NPAIR - 1))
                sp.sem_inc(turns.sem, 1)
                sp.dma_start(x2T[bass.ds(i, 1)].rearrange("o (c p) s -> p (o c) s", p=P), x2t[:]).then_inc(x2t_out.sem, 16)

            with sp.Fori(0, N - 1) as i:
                turn(i, False)
            turn(N - 1, True)
            sp.wait_ge(x2_out.sem, x2_out.at(N - 1))
            sp.wait_ge(x2t_out.sem, x2t_out.at(N - 1))

        @block.tensor
        def _(pe):
            pe.wait_ge(consts.sem, consts.at(0, 10))
            with pe.Fori(0, N) as i:
                pe.wait_ge(xt_in.sem, xt_in.at(i))
                kq = v = 0

                def project(kind, hc, c):
                    nonlocal kq, v
                    if kind == "v":
                        pe.wait_ge(v_done.sem, v_done.at(i, v - 2))
                        bank = v_bank[v % 2]
                    else:
                        pe.wait_ge(er_ready.sem, er_ready.at(i, kq - 2))
                        bank = act_bank[kq % 2]
                    for k in range(DC):
                        mm = pe.matmul(bank[:, :], w[kind][:, k, hc * P:hc * P + P], xt[:, k, c * 512:c * 512 + 512],
                                       start=(k == 0), stop=(k == DC - 1))
                    if kind == "v":
                        mm.then_inc(v_ready.sem, 1)
                        v += 1
                    else:
                        mm.then_inc(kq_ready.sem, 1)
                        kq += 1

                for hc in range(DC):
                    for c in range(2):
                        project("k", hc, c)
                        project("v", hc, c)
                for c in range(2):
                    for hc in range(DC):
                        project("q", hc, c)
                for s in range(SLOTS):
                    if s < NPAIR:
                        p = s
                        pe.wait_ge(vp_done.sem, vp_done.at(i, (2 * p // 4) * 2 + 1))
                        pe.wait_ge(o_added.sem, o_added.at(i, p - 1))
                        for t in (2 * p, 2 * p + 1):
                            for k in range(DC):
                                mm = pe.matmul(o_bank[:, (t % 2) * D:(t % 2) * D + D], vp[:, k, t * P:t * P + P],
                                               w["o"][:, k, :], start=(k == 0), stop=(k == DC - 1))
                        mm.then_inc(o_ready.sem, 1)
                    if 0 <= s - 2 < NPAIR:
                        p = s - 2
                        pe.wait_ge(x1_done.sem, x1_done.at(i, p))
                        pe.wait_ge(t1_copied.sem, t1_copied.at(i, p - 1))
                        for k in range(DC):
                            for t in (2 * p, 2 * p + 1):
                                c0 = k * 256 + (t % 2) * P
                                mm = pe.transpose(t1_bank[:, c0:c0 + P], x1[:, t, k * P:k * P + P], eye[:, :])
                        mm.then_inc(t1_ready.sem, 1)
                    if 0 <= s - 3 < NPAIR:
                        p = s - 3
                        pe.wait_ge(t1_copied.sem, t1_copied.at(i, p))
                        pe.wait_ge(h2_done.sem, h2_done.at(i, p - 1))
                        for t in (2 * p, 2 * p + 1):
                            for k in range(DC):
                                mm = pe.matmul(m_bank[:, (t % 2) * D:(t % 2) * D + D],
                                               x1t[:, p % 2, k, (t % 2) * P:(t % 2) * P + P], w["m"][:, k, :],
                                               start=(k == 0), stop=(k == DC - 1))
                        mm.then_inc(m_ready.sem, 1)
                    if 0 <= s - 4 < NPAIR:
                        p = s - 4
                        pe.wait_ge(x2_done.sem, x2_done.at(i, p))
                        pe.wait_ge(t2_copied.sem, t2_copied.at(i, p - 1))
                        for k in range(DC):
                            for t in (2 * p, 2 * p + 1):
                                c0 = k * 256 + (t % 2) * P
                                mm = pe.transpose(t2_bank[:, c0:c0 + P], x2s[:, t, k * P:k * P + P], eye[:, :])
                        mm.then_inc(t2_ready.sem, 1)

        @block.scalar
        def _(act):
            act.sem_inc(er_ready.sem, er_ready.start)
            act.sem_inc(gelu_done.sem, gelu_done.start)
            act.sem_inc(t1_copied.sem, t1_copied.start)
            act.sem_inc(t2_copied.sem, t2_copied.start)
            act.sem_inc(m_ready.sem, m_ready.start)
            act.wait_ge(consts.sem, consts.at(0, 10))
            for kind in "kq":
                act.activation(nb[kind][:, :], b[kind][:, :], ACT.Copy, scale=-1.0)
            act.drain()
            with act.Fori(0, N) as i:
                for n in range(KQ):
                    kind = "k" if n < 4 else "q"
                    hc = n // 2 if n < 4 else n % 2
                    act.wait_ge(kq_ready.sem, kq_ready.at(i, n))
                    act.wait_ge(er_read.sem, er_read.at(i, n - 2))
                    act.activation(n_t[:, n % 2, :], act_bank[n % 2][:, :], ACT.Relu, scale=-1.0, bias=nb[kind][:, hc:hc + 1])
                    act.activation(r_t[:, n % 2, :], act_bank[n % 2][:, :], ACT.Relu, bias=b[kind][:, hc:hc + 1])
                    act.drain()
                    act.activation(e_t[:, n % 2, :], n_t[:, n % 2, :], ACT.Exp, scale=-1.0).then_inc(er_ready.sem, 1)
                for s in range(SLOTS):
                    if s < NPAIR:
                        p = s
                        act.wait_ge(o_added.sem, o_added.at(i, p))
                        act.wait_ge(h_done.sem, h_done.at(i, p - 2))
                        act.activation(g[:, p % 2], pre[:, p % 2], ACT.Gelu_apprx_tanh).then_inc(gelu_done.sem, 1)
                    if 0 <= s - 2 < NPAIR:
                        p = s - 2
                        act.wait_ge(t1_ready.sem, t1_ready.at(i, p))
                        act.wait_ge(m_ready.sem, m_ready.at(i, p - 2))
                        act.activation(x1t[:, p % 2].rearrange("p c t -> p (c t)"), t1_bank[:, :],
                                       ACT.Copy).then_inc(t1_copied.sem, 1)
                    if 0 <= s - 4 < NPAIR:
                        p = s - 4
                        act.wait_ge(t2_ready.sem, t2_ready.at(i, p))
                        if p == 0:
                            act.wait_ge(x2t_out.sem, x2t_out.at(i, -1))
                        act.activation(x2t[:, :, 2 * p * P:2 * p * P + 2 * P],
                                       t2_bank[:, :].rearrange("p (c t) -> p c t", c=DC),
                                       ACT.Copy).then_inc(t2_copied.sem, 1)

        @block.vector
        def _(dve):
            dve.sem_inc(er_read.sem, er_read.start)
            dve.sem_inc(v_done.sem, v_done.start)
            dve.sem_inc(h_done.sem, h_done.start)
            dve.sem_inc(o_added.sem, o_added.start)
            dve.sem_inc(h2_done.sem, h2_done.start)
            dve.wait_ge(consts.sem, consts.at(0, 10))
            with dve.Fori(0, N) as i:
                def feature_map(n, out, **more):
                    dve.wait_ge(er_ready.sem, er_ready.at(i, n))
                    dve.tensor_scalar(e_t[:, n % 2, :], e_t[:, n % 2, :], -1.0, None, ALU.add)
                    dve.drain()
                    dve.scalar_tensor_tensor(out, e_t[:, n % 2, :], 1.0, r_t[:, n % 2, :], ALU.add, ALU.add,
                                             **more).then_inc(er_read.sem, 1)

                for n in range(4):
                    hc, c = n // 2, n % 2
                    chunk = keys[:, hc, c * 512:c * 512 + 512]
                    feature_map(n, chunk, accum_out=ksum2[:, hc, c:c + 1])
                    dve.drain()
                    dve.wait_ge(v_ready.sem, v_ready.at(i, n))
                    dve.scalar_tensor_tensor(junk[:, :], v_bank[n % 2][:, :], b["v"][:, hc:hc + 1], chunk, ALU.add,
                                             ALU.mult, accum_out=kv2[:, hc, c:c + 1]).then_inc(v_done.sem, 1)
                dve.drain()
                dve.tensor_tensor(ksum[:, :], ksum2[:, :, 0], ksum2[:, :, 1], ALU.add)
                dve.tensor_tensor(kv[:, :], kv2[:, :, 0], kv2[:, :, 1], ALU.add)
                for n in range(4, KQ):
                    hc, c = n % 2, (n - 4) // 2
                    feature_map(n, q_t[:, :])
                    dve.drain()
                    dve.tensor_scalar(z_t[:, :], q_t[:, :], ksum[:, hc:hc + 1], 1e-6, ALU.mult, ALU.add)
                    dve.drain()
                    dve.reciprocal(z_t[:, :], z_t[:, :])
                    dve.drain()
                    dve.scalar_tensor_tensor(vp[:, hc, c * 512:c * 512 + 512], q_t[:, :], kv[:, hc:hc + 1], z_t[:, :],
                                             ALU.mult, ALU.mult).then_inc(vp_done.sem, 1)
                dve.wait_ge(xs_in.sem, xs_in.at(i))
                for s in range(SLOTS):
                    if s < NPAIR:
                        p = s
                        dve.wait_ge(o_ready.sem, o_ready.at(i, p))
                        dve.wait_ge(gelu_done.sem, gelu_done.at(i, p - 2))
                        dve.tensor_tensor(pre[:, p % 2].rearrange("p t d -> p (t d)"), o_bank[:, :],
                                          bo_b[:].rearrange("p t d -> p (t d)"), ALU.add).then_inc(o_added.sem, 1)
                    if 0 <= s - 2 < NPAIR:
                        p = s - 2
                        dve.wait_ge(rstd1_done.sem, rstd1_done.at(i, p))
                        for t in (2 * p, 2 * p + 1):
                            ins = dve.tensor_scalar(x1[:, t, :], h[:, t, :], mv[:, 0, t, 0:1], rstd[:, 0, t:t + 1],
                                                    ALU.subtract, ALU.mult)
                        ins.then_inc(x1_done.sem, 1)
                    if 0 <= s - 4 < NPAIR:
                        p = s - 4
                        dve.wait_ge(rstd2_done.sem, rstd2_done.at(i, p))
                        if p == 0:
                            dve.wait_ge(x2_out.sem, x2_out.at(i, -1))
                        for t in (2 * p, 2 * p + 1):
                            ins = dve.tensor_scalar(x2s[:, t, :], h2[:, t, :], mv[:, 1, t, 0:1], rstd[:, 1, t:t + 1],
                                                    ALU.subtract, ALU.mult)
                        ins.then_inc(x2_done.sem, 1)
                    if 0 <= s - 1 < NPAIR:
                        p = s - 1
                        dve.wait_ge(gelu_done.sem, gelu_done.at(i, p))
                        hp = slice(2 * p, 2 * p + 2)
                        dve.tensor_tensor(h[:, hp, :], g[:, p % 2], xs[:, hp, :], ALU.add).then_inc(h_done.sem, 1)
                        dve.drain()
                        for t in (2 * p, 2 * p + 1):
                            dve.bn_stats(st[:, t, 0, :], h[:, t, :])
                        dve.drain()
                        for t in (2 * p, 2 * p + 1):
                            ins = dve.bn_aggr(mv[:, 0, t, :], st[:, t, 0, :])
                        ins.then_inc(mv1_done.sem, 1)
                    if 0 <= s - 3 < NPAIR:
                        p = s - 3
                        dve.wait_ge(m_ready.sem, m_ready.at(i, p))
                        dve.wait_ge(x1b_done.sem, x1b_done.at(i, p))
                        hp = slice(2 * p, 2 * p + 2)
                        dve.tensor_tensor(h2[:, hp, :], m_bank[:, :].rearrange("p (t d) -> p t d", t=2), x1b[:, hp, :],
                                          ALU.add).then_inc(h2_done.sem, 1)
                        dve.drain()
                        for t in (2 * p, 2 * p + 1):
                            dve.bn_stats(st[:, t, 1, :], h2[:, t, :])
                        dve.drain()
                        for t in (2 * p, 2 * p + 1):
                            ins = dve.bn_aggr(mv[:, 1, t, :], st[:, t, 1, :])
                        ins.then_inc(mv2_done.sem, 1)

        @block.gpsimd
        def _(pool):
            pool.memset(neg_half[:, :], -0.5)
            pool.drain()
            with pool.Fori(0, N) as i:
                def rstd_of(which, p):
                    c = slice(2 * p, 2 * p + 2)
                    pool.tensor_scalar(var[:, which, c], mv[:, which, c, 1], EPS, None, ALU.add).then_inc(
                        eps_added.sem, 1)
                    pool.wait_ge(eps_added.sem, eps_added.at(i, rstd_of.n))
                    rstd_of.n += 1
                    return pool.tensor_tensor(rstd[:, which, c], var[:, which, c], neg_half[:, :], ALU.pow)
                rstd_of.n = 0
                for s in range(SLOTS):
                    if 0 <= s - 2 < NPAIR:
                        p = s - 2
                        pool.wait_ge(x1_done.sem, x1_done.at(i, p))
                        hp = slice(2 * p, 2 * p + 2)
                        pool.tensor_tensor(x1b[:, hp, :], x1[:, hp, :], bias_b[:], ALU.add).then_inc(x1b_done.sem, 1)
                    if 0 <= s - 1 < NPAIR:
                        pool.wait_ge(mv1_done.sem, mv1_done.at(i, s - 1))
                        pool.sem_inc(pool_turns.sem, 1)
                        rstd_of(0, s - 1).then_inc(rstd1_done.sem, 1)
                    if 0 <= s - 3 < NPAIR:
                        pool.wait_ge(mv2_done.sem, mv2_done.at(i, s - 3))
                        pool.sem_inc(pool_turns.sem, 1)
                        rstd_of(1, s - 3).then_inc(rstd2_done.sem, 1)


def causal_attention(nc, x2, x2T, w_kqv, ident, above, ramp_q, ramp_k, sel_q, sel_k, m_rows, split_q, split_k, guard_d, x3):
    H, HD = 16, 16
    HH = H // 2
    G = HH // 2
    PARTS = 3
    PROD = 6 * HD
    SCORE_ROWS = PROD + 4 * PARTS
    ROWS = SCORE_ROWS + PARTS
    VW = 32
    STEPS = [(g, c, j) for g in range(2) for c in range(2) for j in range(4 * c + 4)]
    NS = len(STEPS)
    MAX_UNITS = [[(hd, t, kc) for hd in range(g * G, g * G + G) for t in range(NT) for kc in range(1 + (t >= 4))]
                 for g in range(2)]
    NM = len(MAX_UNITS[0])
    PREP = {0: ["q0", "q1"], 1: ["k0", "k1"], 2: ["v0", "v1"], 15: ["g0"], 23: ["g1"]}
    for n in range(8):
        PREP.setdefault(6 + n, []).append(("max", 0, n))
        PREP.setdefault(14 + n, []).append(("max", 1, n))
    PREP[15] = [("max", 1, 1), "g0"]
    MISC = ["q0", "q1", "k0", "k1", "v0", "v1", "g0", "g1"]
    PER_STEP = NM // 8

    with ExitStack() as ctx:
        def sb(name, shape, dt=F32):
            return ctx.enter_context(nc.sbuf_tensor("b_" + name, shape, dt))

        def sig(name, per, prime=0, unit=1):
            return Signal(ctx, nc, "b_" + name, per, prime, unit)

        w = sb("w", [P, DC, 3 * D])
        eye = sb("eye", [P, P])
        eye_b = sb("eye_b", [P, P], BF16)
        mask_f = sb("mask_f", [P, 2, P])
        mask = sb("mask", [P, 2, P], BF16)
        ramp = {"q": sb("ramp_q", [P, S]), "k": sb("ramp_k", [P, S])}
        sel = {"q": sb("sel_q", [P, PARTS]), "k": sb("sel_k", [P, PARTS])}
        m_all = sb("m_all", [P, H])
        m_part = sb("m_part", [P, PARTS, H], BF16)
        m_rest = sb("m_rest", [P, 2, H])
        m_sel = {"q": sb("m_sel_q", [P, 3, H]), "k": sb("m_sel_k", [P, 3, H])}
        neg_half = sb("neg_half", [P, NT])
        xt = sb("xt", [P, DC, S])
        xs = sb("xs", [P, NT, D])
        parts = {"q": sb("parts_q", [P, PARTS, S], BF16), "k": sb("parts_k", [P, PARTS, S], BF16)}
        rest = sb("rest", [P, 2, 512])
        aug = {k: [sb(f"aug_{k}{i}", [P, HH, S], BF16) for i in range(2)] for k in "qk"}
        v = [sb(f"v{i}", [P, NT, HH, VW]) for i in range(2)]
        cmax = sb("cmax", [P, 2, G, NT, 2])
        guard = sb("guard", [P, 2, G * NT])
        g_rest = sb("g_rest", [G * NT, 2, P])
        g_part = sb("g_part", [G * NT, 2, PARTS, P], BF16)
        pt = sb("pt", [P, 3, G, 512])
        ot = sb("ot", [P, 512])
        rc = sb("rc", [P, 4, G])
        att = sb("att", [P, 4, G, HD])
        h3 = sb("h3", [P, NT, D])
        st = sb("st", [P, NT, 6])
        mv = sb("mv", [P, NT, 2])
        var = sb("var", [P, NT])
        rstd = sb("rstd", [P, NT])
        x3s = sb("x3s", [P, NT, D])
        s_bank = [ctx.enter_context(nc.psum_tensor(f"b_s{i}", [P, 2, 512], F32)) for i in range(2)]
        max_bank = [ctx.enter_context(nc.psum_tensor(f"b_max{i}", [P, 512], F32)) for i in range(2)]
        av_bank = ctx.enter_context(nc.psum_tensor("b_av", [P, 512], F32))
        misc = ctx.enter_context(nc.psum_tensor("b_misc", [P, 512], F32))

        consts = sig("consts", 1, 0, 16)
        const_cast = sig("const_cast", 1)
        rows_set = sig("rows_set", 1)
        xt_in = sig("xt_in", 1, 0, 16)
        xs_in = sig("xs_in", 1, 0, 16)
        misc_ready = sig("misc_ready", 2 * 8)
        misc_read = sig("misc_read", 2 * 8, 1)
        rest_ready = sig("rest_ready", 2 * 4)
        rest_read = sig("rest_read", 2 * 4, 2)
        parts_out = sig("parts_out", 2 * 2, 0, 16)
        aug_in = sig("aug_in", 2 * 12, 0, 16)
        max_ready = sig("max_ready", 2 * 2 * NM)
        max_read = sig("max_read", 2 * 2 * NM, 2)
        guard_done = sig("guard_done", 2 * 2)
        g_parts_done = sig("g_parts_done", 2 * 2)
        guard_out = sig("guard_out", 2 * 2, 0, 16)
        guard_in = [sig(f"guard_in{g}", 2, 0, 16) for g in range(2)]
        s_ready = sig("s_ready", 2 * NS * 2)
        exp_done = sig("exp_done", 2 * NS * 2, 2)
        av_done = sig("av_done", 2 * NS, 3)
        ot_copied = sig("ot_copied", 2 * 4)
        o_turned = sig("o_turned", 2 * 4, 1)
        o_read = sig("o_read", 2 * 4, 1)
        h3_done = sig("h3_done", 1)
        mv_done = sig("mv_done", 1)
        eps_added = sig("eps_added", 1)
        rstd_done = sig("rstd_done", 1)
        x3_done = sig("x3_done", 1)
        x3_out = sig("x3_out", 1, 1, 16)
        ticks = sig("ticks", 1)
        pool_ticks = sig("pool_ticks", 1)
        block = ctx.enter_context(nc.Block())

        def width(c, j):
            lo = max(512 * c, P * j)
            return lo, 512 * (c + 1) - lo

        def finished(k):
            g, c, j = STEPS[k]
            return g * 2 + c if j == 4 * c + 3 else None

        def turns(eng, half_turn, prologue=None):
            if prologue:
                prologue()
            with eng.Fori(0, N - 1) as i:
                for half in range(2):
                    half_turn(i, half, True)
            half_turn(N - 1, 0, True)
            half_turn(N - 1, 1, False)

        @block.sync
        def _(sp):
            for dst, src in ((w[:], w_kqv.rearrange("(c p) n -> p c n", p=P)), (eye[:], ident),
                             (mask_f[:], above.rearrange("k p n -> p k n")),
                             (ramp["q"][PROD:ROWS, :], ramp_q), (ramp["k"][PROD:ROWS, :], ramp_k),
                             (sel["q"][PROD:ROWS, :], sel_q), (sel["k"][PROD:ROWS, :], sel_k),
                             (m_all[PROD:ROWS, :], m_rows)):
                sp.dma_start(dst, src).then_inc(consts.sem, 16)
            sp.sem_inc(x3_out.sem, x3_out.start)
            sp.dma_start(xt[:], x2T[0].rearrange("(c p) s -> p c s", p=P)).then_inc(xt_in.sem, 16)
            sp.dma_start(xs[:], x2[0].rearrange("(t p) d -> p t d", p=P)).then_inc(xs_in.sem, 16)

            def prepare(i, h, part):
                hb = h % 2
                if part == "qk":
                    for n, kind in enumerate("qk"):
                        dram = (split_q, split_k)[n]
                        sp.wait_ge(rest_read.sem, rest_read.at(i, h * 4 + 2 * n + 1))
                        sp.dma_start(dram.rearrange("r p s -> p r s"), parts[kind][:]).then_inc(parts_out.sem, 16)
                        sp.wait_ge(parts_out.sem, parts_out.at(i, h * 2 + n))
                        sp.sem_inc(ticks.sem, 1)
                        src = dram.rearrange("r (h d) s -> r d h s", d=HD)
                        row = 0
                        for a, count in ((0, 3), (1, 2), (2, 1)):
                            for r in range(count):
                                sp.dma_start(aug[kind][hb][row:row + HD], src[a if kind == "q" else r]).then_inc(
                                    aug_in.sem, 16)
                                row += HD
                else:
                    g = part
                    sp.wait_ge(g_parts_done.sem, g_parts_done.at(i, h * 2 + g))
                    sp.dma_start(guard_d[g].rearrange("r p n -> p r n"), g_part[:, g]).then_inc(guard_out.sem, 16)
                    sp.wait_ge(guard_out.sem, guard_out.at(i, h * 2 + g))
                    sp.sem_inc(ticks.sem, 1)
                    sp.dma_start(aug["q"][hb][SCORE_ROWS:ROWS, g * G:g * G + G, :],
                                 guard_d[g].rearrange("r (h t) n -> r h (t n)", h=G)).then_inc(guard_in[g].sem, 16)

            def half_turn(i, half, more):
                if more:
                    prepare(i, half + 1, "qk")
                if half == 0:
                    sp.wait_ge(misc_ready.sem, misc_ready.at(i, 1 * 8 + 5))
                    sp.sem_inc(ticks.sem, 1)
                    if not isinstance(i, int):
                        sp.dma_start(xt[:], x2T[bass.ds(i + 1, 1)].rearrange("o (c p) s -> p (o c) s", p=P)).then_inc(
                            xt_in.sem, 16)
                if more:
                    prepare(i, half + 1, 0)
                    prepare(i, half + 1, 1)
                if half == 1:
                    sp.wait_ge(h3_done.sem, h3_done.at(i))
                    sp.sem_inc(ticks.sem, 1)
                    if not isinstance(i, int):
                        sp.dma_start(xs[:], x2[bass.ds(i + 1, 1)].rearrange("o (t p) d -> p (o t) d", p=P)).then_inc(
                            xs_in.sem, 16)
                    sp.wait_ge(x3_done.sem, x3_done.at(i))
                    sp.sem_inc(ticks.sem, 1)
                    sp.dma_start(x3[bass.ds(i, 1)].rearrange("o (t p) d -> p (o t) d", p=P), x3s[:]).then_inc(
                        x3_out.sem, 16)

            def prologue():
                for part in ("qk", 0, 1):
                    prepare(0, 0, part)

            turns(sp, half_turn, prologue)
            sp.wait_ge(x3_out.sem, x3_out.at(N - 1))

        @block.tensor
        def _(pe):
            pe.wait_ge(consts.sem, consts.at(0, 7))
            pe.wait_ge(const_cast.sem, const_cast.at(0))
            pe.wait_ge(rows_set.sem, rows_set.at(0))
            pe.sem_inc(av_done.sem, av_done.start)
            pe.sem_inc(o_turned.sem, o_turned.start)

            def prepare(i, h, task):
                hb = h % 2
                if isinstance(task, tuple):
                    _, g, n = task
                    q, k = aug["q"][hb], aug["k"][hb]
                    if (g, n) == (0, 0):
                        pe.wait_ge(aug_in.sem, aug_in.at(i, h * 12 + 11))
                    for u in range(n * PER_STEP, n * PER_STEP + PER_STEP):
                        hd, t, kc = MAX_UNITS[g][u]
                        at = (h * 2 + g) * NM + u
                        pe.wait_ge(max_read.sem, max_read.at(i, at - 2))
                        n_keys = min(512, P * (t + 1) - 512 * kc)
                        diagonal = n_keys == P * (t + 1) - 512 * kc
                        bank = max_bank[u % 2]
                        mm = pe.matmul(bank[:, 0:n_keys], q[0:SCORE_ROWS, hd, t * P:t * P + P],
                                       k[0:SCORE_ROWS, hd, 512 * kc:512 * kc + n_keys], start=True, stop=not diagonal)
                        if diagonal:
                            mm = pe.matmul(bank[:, n_keys - P:n_keys], eye_b[:, :], mask[:, 0, :], start=False, stop=True)
                        mm.then_inc(max_ready.sem, 1)
                    return
                m = MISC.index(task)
                pe.wait_ge(misc_read.sem, misc_read.at(i, h * 8 + m - 1))
                if task == "q0":
                    if h != 1:
                        pe.wait_ge(xt_in.sem, xt_in.at(i, h // 2))
                if task[0] in "qk":
                    c = int(task[1])
                    col = (D if task[0] == "q" else 0) + hb * P
                    for k in range(DC):
                        mm = pe.matmul(misc[:, :], w[:, k, col:col + P], xt[:, k, c * 512:c * 512 + 512],
                                       start=(k == 0), stop=(k == DC - 1))
                elif task[0] == "v":
                    c = int(task[1])
                    col = 2 * D + hb * P
                    for t in range(4):
                        for k in range(DC):
                            at = (4 * c + t) * P
                            mm = pe.matmul(misc[:, t * P:t * P + P], xt[:, k, at:at + P], w[:, k, col:col + P],
                                           start=(k == 0), stop=(k == DC - 1))
                else:
                    g = int(task[1])
                    pe.wait_ge(guard_done.sem, guard_done.at(i, h * 2 + g))
                    mm = pe.transpose(misc[0:G * NT, 0:P], guard[:, g, :], eye[:, :])
                mm.then_inc(misc_ready.sem, 1)

            def scores(i, half, k):
                g, c, j = STEPS[k]
                lo, n = width(c, j)
                if k % 12 == 0:
                    pe.wait_ge(guard_in[g].sem, guard_in[g].at(i, half))
                for pair in range(2):
                    bank = s_bank[pair]
                    pe.wait_ge(exp_done.sem, exp_done.at(i, (half * NS + k - 1) * 2 + pair))
                    for hh in range(2):
                        hd = g * G + pair * 2 + hh
                        diagonal = j >= 4 * c
                        mm = pe.matmul(bank[:, hh, 0:n], aug["k"][half][0:ROWS, hd, j * P:j * P + P],
                                       aug["q"][half][0:ROWS, hd, lo:lo + n], start=True, stop=not diagonal)
                        if diagonal:
                            mm = pe.matmul(bank[:, hh, 0:P], eye_b[:, :], mask[:, 1, :], start=False, stop=True)
                    mm.then_inc(s_ready.sem, 1)

            def values(i, half, k):
                g, c, j = STEPS[k]
                lo, n = width(c, j)
                pe.wait_ge(exp_done.sem, exp_done.at(i, (half * NS + k) * 2 + 1))
                if j == 0:
                    pe.wait_ge(o_read.sem, o_read.at(i, half * 4 + g * 2 + c - 1))
                for hh in range(G):
                    mm = pe.matmul(av_bank[hh * VW:hh * VW + VW, lo - 512 * c:512], v[half][:, j, g * G + hh, :],
                                   pt[:, k % 3, hh, 0:n], start=(j == 0), stop=(j == 4 * c + 3))
                mm.then_inc(av_done.sem, 1)

            def turn_output(i, half, o):
                pe.wait_ge(ot_copied.sem, ot_copied.at(i, half * 4 + o))
                for t in range(4):
                    mm = pe.transpose(av_bank[:, t * P:t * P + P], ot[:, t * P:t * P + P], eye[:, :])
                mm.then_inc(o_turned.sem, 1)

            def half_turn(i, half, more):
                for k in range(NS + 2):
                    if k < NS:
                        scores(i, half, k)
                    if k >= 2 and finished(k - 2) is not None:
                        turn_output(i, half, finished(k - 2))
                    if more and k < NS:
                        for task in PREP.get(k, []):
                            prepare(i, half + 1, task)
                    if 1 <= k <= NS:
                        values(i, half, k - 1)

            def prologue():
                for k in range(NS):
                    for task in PREP.get(k, []):
                        prepare(0, 0, task)

            turns(pe, half_turn, prologue)

        @block.scalar
        def _(act):
            act.sem_inc(exp_done.sem, exp_done.start)

            def half_turn(i, half, more):
                for k in range(NS + 1):
                    if k < NS:
                        g, c, j = STEPS[k]
                        lo, n = width(c, j)
                        for pair in range(2):
                            act.wait_ge(s_ready.sem, s_ready.at(i, (half * NS + k) * 2 + pair))
                            if pair == 0:
                                act.wait_ge(av_done.sem, av_done.at(i, half * NS + k - 3))
                            act.activation(pt[:, k % 3, 2 * pair:2 * pair + 2, 0:n], s_bank[pair][:, :, 0:n],
                                           ACT.Exp).then_inc(exp_done.sem, 1)
                    if k >= 1 and finished(k - 1) is not None:
                        o = finished(k - 1)
                        act.wait_ge(av_done.sem, av_done.at(i, half * NS + k - 1))
                        act.wait_ge(o_turned.sem, o_turned.at(i, half * 4 + o - 1))
                        act.activation(ot[:, :], av_bank[:, :], ACT.Copy).then_inc(ot_copied.sem, 1)

            turns(act, half_turn)

        @block.vector
        def _(dve):
            dve.sem_inc(misc_read.sem, misc_read.start)
            dve.sem_inc(max_read.sem, max_read.start)
            dve.sem_inc(o_read.sem, o_read.start)
            dve.wait_ge(consts.sem, consts.at(0, 7))
            for k in range(2):
                for t in range(2):
                    dve.memset(v[k][:, :, :, :] if t == 0 else v[k][:, :, :, HD:HD + 1], float(t))
                    dve.drain()
            dve.memset(cmax[:], -3e38)
            dve.tensor_copy(eye_b[:], eye[:])
            dve.tensor_copy(mask[:], mask_f[:]).then_inc(const_cast.sem, 1)
            r = slice(PROD, ROWS)
            dve.tensor_copy(m_part[r, 0, :], m_all[r, :])
            dve.drain()
            dve.tensor_tensor(m_rest[r, 0, :], m_all[r, :], m_part[r, 0, :], ALU.subtract)
            dve.drain()
            dve.tensor_copy(m_part[r, 1, :], m_rest[r, 0, :])
            dve.drain()
            dve.tensor_tensor(m_part[r, 2, :], m_rest[r, 0, :], m_part[r, 1, :], ALU.subtract)
            dve.drain()
            for kind in "qk":
                ms = m_sel[kind]
                dve.tensor_scalar(ms[r, 0, :], m_part[r, 0, :], sel[kind][r, 0:1], None, ALU.mult)
                for p in (1, 2):
                    dve.drain()
                    dve.scalar_tensor_tensor(ms[r, p, :], m_part[r, p, :], sel[kind][r, p:p + 1], ms[r, p - 1, :],
                                             ALU.mult, ALU.add)
                dve.drain()
                for half in range(2):
                    for hd in range(HH):
                        ins = dve.tensor_scalar(aug[kind][half][r, hd, :], ramp[kind][r, :],
                                                ms[r, 2, half * HH + hd:half * HH + hd + 1], None, ALU.add)
            ins.then_inc(rows_set.sem, 1)

            def prepare(i, h, task):
                hb = h % 2
                if isinstance(task, tuple):
                    _, g, n = task
                    for u in range(n * PER_STEP, n * PER_STEP + PER_STEP):
                        hd, t, kc = MAX_UNITS[g][u]
                        n_keys = min(512, P * (t + 1) - 512 * kc)
                        dve.wait_ge(max_ready.sem, max_ready.at(i, (h * 2 + g) * NM + u))
                        dve.tensor_reduce(cmax[:, g, hd % G, t, kc:kc + 1], max_bank[u % 2][:, 0:n_keys], AX.X,
                                          ALU.max).then_inc(max_read.sem, 1)
                    if n == 7:
                        dve.drain()
                        flat = cmax[:, g].rearrange("p h t k -> p (h t) k")
                        dve.tensor_tensor(guard[:, g, :], flat[:, :, 0], flat[:, :, 1], ALU.max).then_inc(
                            guard_done.sem, 1)
                    return
                m = MISC.index(task)
                if task[0] in "qk":
                    kind, c = task[0], int(task[1])
                    n = (kind == "k") * 2 + c
                    cols = slice(c * 512, c * 512 + 512)
                    scale = 1.0 / 16 if kind == "q" else 1.0
                    dve.wait_ge(misc_ready.sem, misc_ready.at(i, h * 8 + m))
                    if n == 0:
                        if h:
                            dve.wait_ge(parts_out.sem, parts_out.at(i, h * 2 - 1))
                    dve.tensor_scalar(parts[kind][:, 0, cols], misc[:, :], scale, None, ALU.mult)
                    dve.drain()
                    dve.wait_ge(rest_read.sem, rest_read.at(i, h * 4 + n - 2))
                    dve.scalar_tensor_tensor(rest[:, n % 2, :], misc[:, :], scale, parts[kind][:, 0, cols], ALU.mult,
                                             ALU.subtract).then_inc(misc_read.sem, 1)
                elif task[0] == "v":
                    c = int(task[1])
                    dve.wait_ge(misc_ready.sem, misc_ready.at(i, h * 8 + m))
                    dve.tensor_copy(v[hb][:, 4 * c:4 * c + 4, :, 0:HD].rearrange("p t h d -> p (t h) d"),
                                    misc[:, :].rearrange("p (n d) -> p n d", d=HD)).then_inc(misc_read.sem, 1)
                else:
                    g = int(task[1])
                    dve.wait_ge(misc_ready.sem, misc_ready.at(i, h * 8 + m))
                    turned = misc[0:G * NT, 0:P]
                    dve.tensor_copy(g_part[:, g, 0, :], turned)
                    dve.drain()
                    dve.tensor_tensor(g_rest[:, 0, :], turned, g_part[:, g, 0, :], ALU.subtract).then_inc(
                        misc_read.sem, 1)
                    dve.drain()
                    dve.tensor_copy(g_part[:, g, 1, :], g_rest[:, 0, :])
                    dve.drain()
                    dve.tensor_tensor(g_part[:, g, 2, :], g_rest[:, 0, :], g_part[:, g, 1, :],
                                      ALU.subtract).then_inc(g_parts_done.sem, 1)

            def output(i, half, o):
                g, c = o // 2, o % 2
                dve.wait_ge(o_turned.sem, o_turned.at(i, half * 4 + o))
                turned = av_bank[:, :].rearrange("p (t h d) -> p t h d", t=4, h=G)
                dve.reciprocal(rc[:, :, :], turned[:, :, :, HD])
                dve.drain()
                dve.tensor_tensor(att[:, :, :, :], turned[:, :, :, 0:HD],
                                  rc[:, :, :].unsqueeze(3).broadcast_to([P, 4, G, HD]), ALU.mult).then_inc(o_read.sem, 1)
                dve.drain()
                if half == 0 and o == 0:
                    dve.wait_ge(xs_in.sem, xs_in.at(i))
                d0 = half * P + g * G * HD
                tiles = slice(4 * c, 4 * c + 4)
                ins = dve.tensor_tensor(h3[:, tiles, d0:d0 + G * HD], xs[:, tiles, d0:d0 + G * HD],
                                        att[:].rearrange("p t h d -> p t (h d)"), ALU.add)
                if half == 1 and o == 3:
                    ins.then_inc(h3_done.sem, 1)

            def half_turn(i, half, more):
                for k in range(NS + 2):
                    if k >= 2 and finished(k - 2) is not None:
                        output(i, half, finished(k - 2))
                    if more and k < NS:
                        for task in PREP.get(k, []):
                            prepare(i, half + 1, task)
                if half == 1:
                    dve.drain()
                    for t in range(NT):
                        dve.bn_stats(st[:, t, :], h3[:, t, :])
                    dve.drain()
                    for t in range(NT):
                        ins = dve.bn_aggr(mv[:, t, :], st[:, t, :])
                    ins.then_inc(mv_done.sem, 1)
                    dve.wait_ge(rstd_done.sem, rstd_done.at(i))
                    dve.wait_ge(x3_out.sem, x3_out.at(i, -1))
                    for t in range(NT):
                        ins = dve.tensor_scalar(x3s[:, t, :], h3[:, t, :], mv[:, t, 0:1], rstd[:, t:t + 1],
                                                ALU.subtract, ALU.mult)
                    ins.then_inc(x3_done.sem, 1)
                    dve.drain()

            def prologue():
                for k in range(NS):
                    for task in PREP.get(k, []):
                        prepare(0, 0, task)

            turns(dve, half_turn, prologue)

        @block.gpsimd
        def _(pool):
            pool.sem_inc(rest_read.sem, rest_read.start)
            pool.memset(neg_half[:, :], -0.5)
            pool.drain()

            def prepare(i, h):
                for n in range(4):
                    kind, c = "qk"[n // 2], n % 2
                    cols = slice(c * 512, c * 512 + 512)
                    pool.wait_ge(misc_read.sem, misc_read.at(i, h * 8 + n))
                    pool.sem_inc(pool_ticks.sem, 1)
                    pool.tensor_copy(parts[kind][:, 1, cols], rest[:, n % 2, :])
                    pool.drain()
                    pool.tensor_tensor(parts[kind][:, 2, cols], rest[:, n % 2, :], parts[kind][:, 1, cols],
                                       ALU.subtract).then_inc(rest_read.sem, 1)

            def half_turn(i, half, more):
                if more:
                    prepare(i, half + 1)
                if half == 1:
                    pool.wait_ge(mv_done.sem, mv_done.at(i))
                    pool.sem_inc(pool_ticks.sem, 1)
                    pool.tensor_scalar(var[:, :], mv[:, :, 1], EPS, None, ALU.add).then_inc(eps_added.sem, 1)
                    pool.wait_ge(eps_added.sem, eps_added.at(i))
                    pool.tensor_tensor(rstd[:, :], var[:, :], neg_half[:, :], ALU.pow).then_inc(rstd_done.sem, 1)

            turns(pool, half_turn, lambda: prepare(0, 0))


def position_attention(nc, x3, ln1_w, ln1_b, ln2_w, ln2_b, w_qkv, w_proj, w_router, ident, resid, xn, logits):
    KV, R, HD = 8, 2, 16
    GW = (R + 2) * HD
    E8 = 8
    NP2 = N // 2
    with ExitStack() as ctx:
        def sb(name, shape, dt=F32):
            return ctx.enter_context(nc.sbuf_tensor("c_" + name, shape, dt))

        def sig(name, per, prime=0, unit=1):
            return Signal(ctx, nc, "c_" + name, per, prime, unit)

        wq = sb("wq", [P, DC, KV * GW])
        wp = sb("wp", [P, DC, D])
        wr = sb("wr", [P, DC, E8])
        eye = sb("eye", [P, P])
        ln = [sb(f"ln{k}", [P, 2, D]) for k in range(4)]
        neg_half = sb("neg_half", [P, N])
        x = sb("x", [P, N, D])
        st = sb("st", [P, N, 6])
        mv = sb("mv", [P, 2, N, 2])
        var = sb("var", [P, 2, N])
        rstd = sb("rstd", [P, 2, N])
        n1 = sb("n1", [P, N, D])
        h1 = sb("h1", [P, N, D])
        ht = sb("ht", [P, 2, DC, 2 * P])
        qkv = sb("qkv", [P, N, KV * GW])
        prod = sb("prod", [P, 2, R, N, KV, HD])
        sc = sb("sc", [P, N * R, N, KV])
        mx = sb("mx", [P, N * R, KV])
        sh = sb("sh", [P, N * R, N, KV])
        pe_ = sb("pe", [P, N * R, N, KV])
        sm = sb("sm", [P, N * R, KV])
        rs = sb("rs", [P, N * R, KV])
        pn = sb("pn", [P, N * R, N, KV])
        ao = sb("ao", [P, N, KV, R, HD])
        aot = sb("aot", [P, 2, DC, 2 * P])
        ha = sb("ha", [P, N, D])
        rr = sb("rr", [P, N, D])
        n2 = sb("n2", [P, N, D])
        n2w = sb("n2w", [P, N, D])
        h2 = sb("h2", [P, N, D])
        n1w = sb("n1w", [P, N, D])
        xt = sb("xt", [P, 2, DC, 2 * P])
        lg = sb("lg", [P, N, E8])

        def bank(name):
            return ctx.enter_context(nc.psum_tensor("c_" + name, [P, 512], F32))

        t1_bank, p_bank, t2_bank, t3_bank, l_bank = (bank(k) for k in ("t1", "p", "t2", "t3", "l"))
        q_bank = [bank(f"q{k}") for k in range(2)]

        consts = sig("consts", 1, 0, 16)
        x_in = sig("x_in", 1, 0, 16)
        mv_done = [sig(f"mv_done{k}", 1) for k in range(2)]
        eps_added = [sig(f"eps_added{k}", 1) for k in range(2)]
        rstd_done = [sig(f"rstd_done{k}", 1) for k in range(2)]
        n1_done = sig("n1_done", NP2)
        h1_done = sig("h1_done", NP2)
        t1_ready = sig("t1_ready", NP2)
        t1_copied = sig("t1_copied", NP2, 1)
        q_ready = sig("q_ready", N, 3)
        q_copied = sig("q_copied", N, 2)
        prod_ready = sig("prod_ready", 2 * N)
        prod_read = sig("prod_read", 2 * N, 2)
        sh_done = sig("sh_done", 1)
        exp_done = sig("exp_done", 1)
        pn_done = sig("pn_done", 1)
        t2_ready = sig("t2_ready", NP2)
        t2_copied = sig("t2_copied", NP2, 1)
        p_ready = sig("p_ready", NP2, 2)
        p_read = sig("p_read", NP2, 1)
        rr_done = sig("rr_done", 1)
        n2_done = sig("n2_done", NP2)
        h2_done = sig("h2_done", NP2)
        t3_ready = sig("t3_ready", NP2)
        t3_copied = sig("t3_copied", NP2, 1)
        l_ready = sig("l_ready", NP2, 2)
        l_copied = sig("l_copied", 1, 1)
        rr_out = sig("rr_out", 1, 1, 16)
        xn_out = sig("xn_out", 1, 1, 16)
        lg_out = sig("lg_out", 1, 1, 16)
        ticks = sig("ticks", 1)
        pool_ticks = sig("pool_ticks", 1)
        block = ctx.enter_context(nc.Block())

        def q_of(s, r):
            return qkv[:, s, :].rearrange("p (g w) -> p g w", g=KV)[:, :, r * HD:r * HD + HD]

        def kv_of(s, which):
            at = (R + which) * HD
            return qkv[:, 0:s + 1, :].rearrange("p t (g w) -> p t g w", g=KV)[:, :, :, at:at + HD]

        def score_products(eng, s, r):
            n = s + 1
            return eng.tensor_tensor(prod[:, s % 2, r, 0:n], q_of(s, r).unsqueeze(1).broadcast_to([P, n, KV, HD]),
                                     kv_of(s, 0), ALU.mult)

        def value_products(eng, s, r):
            n = s + 1
            return eng.tensor_tensor(prod[:, s % 2, r, 0:n],
                                     pn[:, s * R + r, 0:n, :].unsqueeze(3).broadcast_to([P, n, KV, HD]),
                                     kv_of(s, 1), ALU.mult)

        @block.sync
        def _(sp):
            for dst, src in ((wq[:], w_qkv.rearrange("(c p) n -> p c n", p=P)),
                             (wp[:], w_proj.rearrange("(c p) n -> p c n", p=P)),
                             (wr[:], w_router.rearrange("(c p) n -> p c n", p=P)), (eye[:], ident),
                             (ln[0][:], ln1_w), (ln[1][:], ln1_b), (ln[2][:], ln2_w), (ln[3][:], ln2_b)):
                sp.dma_start(dst, src).then_inc(consts.sem, 16)
            for s in (rr_out, xn_out, lg_out):
                sp.sem_inc(s.sem, s.start)
            sp.dma_start(x[:], x3[:, 0:P, :].rearrange("s p d -> p s d")).then_inc(x_in.sem, 16)

            def turn(i, last):
                sp.wait_ge(rr_done.sem, rr_done.at(i))
                sp.sem_inc(ticks.sem, 1)
                if not last:
                    sp.dma_start(x[:], x3[:, bass.ds((i + 1) * P, P), :].rearrange("s p d -> p s d")).then_inc(
                        x_in.sem, 16)
                sp.dma_start(resid[:, bass.ds(i * P, P), :].rearrange("s p d -> p s d"), rr[:]).then_inc(rr_out.sem, 16)
                sp.wait_ge(h2_done.sem, h2_done.at(i, NP2 - 1))
                sp.sem_inc(ticks.sem, 1)
                sp.dma_start(xn[:, bass.ds(i * P, P), :].rearrange("s p d -> p s d"), h2[:]).then_inc(xn_out.sem, 16)
                sp.wait_ge(l_copied.sem, l_copied.at(i))
                sp.sem_inc(ticks.sem, 1)
                sp.dma_start(logits[bass.ds(i, 1)].rearrange("o p s e -> p o (s e)"),
                             lg[:].rearrange("p (o s) e -> p o (s e)", o=1)).then_inc(lg_out.sem, 16)

            with sp.Fori(0, NT - 1) as i:
                turn(i, False)
            turn(NT - 1, True)
            for s in (rr_out, xn_out, lg_out):
                sp.wait_ge(s.sem, s.at(NT - 1))

        @block.tensor
        def _(pe):
            pe.wait_ge(consts.sem, consts.at(0, 7))
            pe.sem_inc(q_ready.sem, q_ready.start)
            pe.sem_inc(p_ready.sem, p_ready.start)
            pe.sem_inc(l_ready.sem, l_ready.start)
            with pe.Fori(0, NT) as i:
                def turn_pair(bank_, src, p, ready):
                    for k in range(DC):
                        for s in (2 * p, 2 * p + 1):
                            c0 = k * 256 + (s % 2) * P
                            mm = pe.transpose(bank_[:, c0:c0 + P], src(s, k), eye[:, :])
                    mm.then_inc(ready.sem, 1)

                for p in range(NP2):
                    pe.wait_ge(h1_done.sem, h1_done.at(i, p))
                    pe.wait_ge(t1_copied.sem, t1_copied.at(i, p - 1))
                    turn_pair(t1_bank, lambda s, k: h1[:, s, k * P:k * P + P], p, t1_ready)
                    pe.wait_ge(t1_copied.sem, t1_copied.at(i, p))
                    for s in (2 * p, 2 * p + 1):
                        pe.wait_ge(q_copied.sem, q_copied.at(i, s - 2))
                        for k in range(DC):
                            mm = pe.matmul(q_bank[s % 2][:, :], ht[:, p % 2, k, (s % 2) * P:(s % 2) * P + P],
                                           wq[:, k, :], start=(k == 0), stop=(k == DC - 1))
                        mm.then_inc(q_ready.sem, 1)
                pe.wait_ge(prod_read.sem, prod_read.at(i, 2 * N - 1))
                for p in range(NP2):
                    pe.wait_ge(t2_copied.sem, t2_copied.at(i, p - 1))
                    turn_pair(t2_bank, lambda s, k: ao[:, s].rearrange("p g r d -> p (g r d)")[:, k * P:k * P + P], p,
                              t2_ready)
                    pe.wait_ge(t2_copied.sem, t2_copied.at(i, p))
                    pe.wait_ge(p_read.sem, p_read.at(i, p - 1))
                    for s in (2 * p, 2 * p + 1):
                        for k in range(DC):
                            mm = pe.matmul(p_bank[:, (s % 2) * D:(s % 2) * D + D],
                                           aot[:, p % 2, k, (s % 2) * P:(s % 2) * P + P], wp[:, k, :],
                                           start=(k == 0), stop=(k == DC - 1))
                    mm.then_inc(p_ready.sem, 1)
                for p in range(NP2):
                    pe.wait_ge(h2_done.sem, h2_done.at(i, p))
                    pe.wait_ge(t3_copied.sem, t3_copied.at(i, p - 1))
                    turn_pair(t3_bank, lambda s, k: h2[:, s, k * P:k * P + P], p, t3_ready)
                    pe.wait_ge(t3_copied.sem, t3_copied.at(i, p))
                    if p == 0:
                        pe.wait_ge(l_copied.sem, l_copied.at(i, -1))
                    for s in (2 * p, 2 * p + 1):
                        for k in range(DC):
                            mm = pe.matmul(l_bank[:, s * E8:s * E8 + E8], xt[:, p % 2, k, (s % 2) * P:(s % 2) * P + P],
                                           wr[:, k, :], start=(k == 0), stop=(k == DC - 1))
                    mm.then_inc(l_ready.sem, 1)

        @block.scalar
        def _(act):
            for s in (t1_copied, t2_copied, t3_copied, q_copied):
                act.sem_inc(s.sem, s.start)
            with act.Fori(0, NT) as i:
                for p in range(NP2):
                    act.wait_ge(t1_ready.sem, t1_ready.at(i, p))
                    act.wait_ge(q_ready.sem, q_ready.at(i, 2 * p - 3))
                    act.activation(ht[:, p % 2].rearrange("p c t -> p (c t)"), t1_bank[:, :], ACT.Copy).then_inc(
                        t1_copied.sem, 1)
                    for s in (2 * p, 2 * p + 1):
                        act.wait_ge(q_ready.sem, q_ready.at(i, s))
                        act.activation(qkv[:, s, :], q_bank[s % 2][:, :], ACT.Copy).then_inc(q_copied.sem, 1)
                act.wait_ge(sh_done.sem, sh_done.at(i))
                act.activation(pe_[:], sh[:], ACT.Exp, scale=0.25).then_inc(exp_done.sem, 1)
                for p in range(NP2):
                    act.wait_ge(t2_ready.sem, t2_ready.at(i, p))
                    act.wait_ge(p_ready.sem, p_ready.at(i, p - 2))
                    act.activation(aot[:, p % 2].rearrange("p c t -> p (c t)"), t2_bank[:, :], ACT.Copy).then_inc(
                        t2_copied.sem, 1)
                for p in range(NP2):
                    act.wait_ge(t3_ready.sem, t3_ready.at(i, p))
                    act.wait_ge(l_ready.sem, l_ready.at(i, p - 2))
                    act.activation(xt[:, p % 2].rearrange("p c t -> p (c t)"), t3_bank[:, :], ACT.Copy).then_inc(
                        t3_copied.sem, 1)

        @block.vector
        def _(dve):
            dve.sem_inc(l_copied.sem, l_copied.start)
            dve.sem_inc(p_read.sem, p_read.start)
            dve.sem_inc(prod_read.sem, prod_read.start)
            dve.memset(sc[:], -BIG)
            dve.drain()
            with dve.Fori(0, NT) as i:
                def moments(which, src):
                    for s in range(N):
                        dve.bn_stats(st[:, s, :], src[:, s, :])
                    dve.drain()
                    for s in range(N):
                        ins = dve.bn_aggr(mv[:, which, s, :], st[:, s, :])
                    ins.then_inc(mv_done[which].sem, 1)
                    dve.wait_ge(rstd_done[which].sem, rstd_done[which].at(i))

                def normalise(which, dst, src, done):
                    for s in range(N):
                        ins = dve.tensor_scalar(dst[:, s, :], src[:, s, :], mv[:, which, s, 0:1],
                                                rstd[:, which, s:s + 1], ALU.subtract, ALU.mult)
                        if s % 2:
                            ins.then_inc(done.sem, 1)

                dve.wait_ge(x_in.sem, x_in.at(i))
                moments(0, x)
                normalise(0, n1, x, n1_done)
                dve.wait_ge(q_copied.sem, q_copied.at(i, N - 1))
                for s in range(N):
                    n = s + 1
                    dve.wait_ge(prod_ready.sem, prod_ready.at(i, s))
                    dve.tensor_reduce(sc[:, s * R:s * R + R, 0:n, :].rearrange("p r t g -> p r (t g)"),
                                      prod[:, s % 2, :, 0:n].rearrange("p r t g d -> p r (t g) d"), AX.X,
                                      ALU.add).then_inc(prod_read.sem, 1)
                dve.drain()
                dve.tensor_reduce(mx[:], sc[:].rearrange("p a t g -> p a g t"), AX.X, ALU.max)
                dve.drain()
                dve.tensor_tensor(sh[:], sc[:], mx[:].unsqueeze(2).broadcast_to([P, N * R, N, KV]),
                                  ALU.subtract).then_inc(sh_done.sem, 1)
                dve.wait_ge(exp_done.sem, exp_done.at(i))
                dve.tensor_reduce(sm[:], pe_[:].rearrange("p a t g -> p a g t"), AX.X, ALU.add)
                dve.drain()
                dve.reciprocal(rs[:], sm[:])
                dve.drain()
                dve.tensor_tensor(pn[:], pe_[:], rs[:].unsqueeze(2).broadcast_to([P, N * R, N, KV]),
                                  ALU.mult).then_inc(pn_done.sem, 1)
                for s in range(N):
                    dve.wait_ge(prod_ready.sem, prod_ready.at(i, N + s))
                    for r in range(R):
                        ins = dve.tensor_reduce(ao[:, s, :, r, :],
                                                prod[:, s % 2, r, 0:s + 1].rearrange("p t g d -> p g d t"), AX.X,
                                                ALU.add)
                    ins.then_inc(prod_read.sem, 1)
                for p in range(NP2):
                    hp = slice(2 * p, 2 * p + 2)
                    dve.wait_ge(p_ready.sem, p_ready.at(i, p))
                    dve.tensor_tensor(ha[:, hp, :], p_bank[:, :].rearrange("p (t d) -> p t d", t=2), x[:, hp, :],
                                      ALU.add).then_inc(p_read.sem, 1)
                dve.drain()
                dve.wait_ge(rr_out.sem, rr_out.at(i, -1))
                dve.tensor_tensor(rr[:], ha[:], x[:], ALU.add).then_inc(rr_done.sem, 1)
                dve.drain()
                moments(1, ha)
                normalise(1, n2, ha, n2_done)
                dve.wait_ge(l_ready.sem, l_ready.at(i, NP2 - 1))
                dve.wait_ge(lg_out.sem, lg_out.at(i, -1))
                dve.tensor_copy(lg[:].rearrange("p s e -> p (s e)"), l_bank[:, 0:N * E8]).then_inc(l_copied.sem, 1)

        @block.gpsimd
        def _(pool):
            pool.memset(neg_half[:, :], -0.5)
            pool.drain()
            pool.wait_ge(consts.sem, consts.at(0, 7))
            pool.sem_inc(pool_ticks.sem, 1)
            with pool.Fori(0, NT) as i:
                def inverse_std(which):
                    pool.wait_ge(mv_done[which].sem, mv_done[which].at(i))
                    pool.sem_inc(pool_ticks.sem, 1)
                    pool.tensor_scalar(var[:, which, :], mv[:, which, :, 1], EPS, None, ALU.add).then_inc(
                        eps_added[which].sem, 1)
                    pool.wait_ge(eps_added[which].sem, eps_added[which].at(i))
                    pool.tensor_tensor(rstd[:, which, :], var[:, which, :], neg_half[:, :], ALU.pow).then_inc(
                        rstd_done[which].sem, 1)

                def affine(dst, mid, src, k, ready, done):
                    for p in range(NP2):
                        hp = slice(2 * p, 2 * p + 2)
                        pool.wait_ge(ready.sem, ready.at(i, p))
                        pool.tensor_tensor(mid[:, hp, :], src[:, hp, :], ln[k][:], ALU.mult)
                        pool.drain()
                        pool.tensor_tensor(dst[:, hp, :], mid[:, hp, :], ln[k + 1][:], ALU.add).then_inc(done.sem, 1)

                inverse_std(0)
                affine(h1, n1w, n1, 0, n1_done, h1_done)
                pool.wait_ge(q_copied.sem, q_copied.at(i, N - 1))
                for s in range(2 * N):
                    if s == N:
                        pool.wait_ge(pn_done.sem, pn_done.at(i))
                    pool.wait_ge(prod_read.sem, prod_read.at(i, s - 2))
                    products = score_products if s < N else value_products
                    for r in range(R):
                        ins = products(pool, s % N, r)
                    ins.then_inc(prod_ready.sem, 1)
                inverse_std(1)
                pool.wait_ge(xn_out.sem, xn_out.at(i, -1))
                affine(h2, n2w, n2, 2, n2_done, h2_done)


EXPERTS = 8
FFN = 1024
CAP = -(-(T * 2 * 5) // (EXPERTS * 4))
SLOTS_ALL = EXPERTS * CAP


def route(nc, logits, before, iota, token_ids, gather_d, prob_d, scatter_d, slot_token):
    NTILE = T // P
    E8 = EXPERTS
    with ExitStack() as ctx:
        def sb(name, shape, dt=F32):
            return ctx.enter_context(nc.sbuf_tensor("r_" + name, shape, dt))

        def sem(name):
            return ctx.enter_context(nc.semaphore("r_" + name))

        lg = sb("lg", [P, NTILE, E8])
        tri = sb("tri", [P, P])
        ones = sb("ones", [P, P])
        io = sb("io", [P, NTILE, E8])
        oh = [sb(f"oh{k}", [P, NTILE, E8]) for k in range(2)]
        lg2 = sb("lg2", [P, NTILE, E8])
        eq = [sb(f"eq{k}", [P, NTILE, E8]) for k in range(2)]
        at = [sb(f"at{k}", [P, NTILE, E8]) for k in range(2)]
        best = [sb(f"best{k}", [P, NTILE]) for k in range(2)]
        first = [sb(f"first{k}", [P, NTILE]) for k in range(2)]
        gap = sb("gap", [P, NTILE])
        e2 = sb("e2", [P, NTILE])
        total = sb("total", [P, NTILE])
        prob = sb("prob", [P, 2, NTILE])
        chosen = sb("chosen", [P, NTILE, E8])
        scan = [sb(f"scan{k}", [P, NTILE, E8]) for k in range(7)]
        base = sb("base", [P, NTILE, E8])
        place = sb("place", [P, NTILE, E8])
        keep = sb("keep", [P, NTILE, E8])
        slot = sb("slot", [P, NTILE, E8])
        pick = [sb(f"pick{k}", [P, NTILE, E8]) for k in range(4)]
        slot_k = sb("slot_k", [P, 2, NTILE])
        keep_k = sb("keep_k", [P, 2, NTILE])
        weight = sb("weight", [P, 2, NTILE])
        gat_f = sb("gat_f", [P, 2, NTILE])
        out_f = sb("out_f", [P, 2, NTILE])
        sca_f = sb("sca_f", [P, 2, NTILE])
        gat = sb("gat", [P, 2, NTILE], U32)
        sca = sb("sca", [P, 2, NTILE], U32)
        tok_f = sb("tok_f", [P, NTILE])
        tok = sb("tok", [P, NTILE], U32)
        zero = sb("zero", [P, SLOTS_ALL // P], U32)
        count_bank = [ctx.enter_context(nc.psum_tensor(f"r_count{k}", [P, 512], F32)) for k in range(2)]
        loaded, ones_set, chosen_done, counted = (sem(k) for k in ("loaded", "ones_set", "chosen_done", "counted"))
        gap_done, exp_done, results, stored, zeroed, zero_set = (
            sem(k) for k in ("gap_done", "exp_done", "results", "stored", "zeroed", "zero_set"))
        block = ctx.enter_context(nc.Block())

        @block.sync
        def _(sp):
            lg_v = lg[:].rearrange("p (s t) e -> p s t e", s=N)
            for t in range(NT):
                sp.dma_start(lg_v[:, :, t, :], logits[t]).then_inc(loaded, 16)
            sp.dma_start(tri[:], before).then_inc(loaded, 16)
            sp.dma_start(io[:], iota).then_inc(loaded, 16)
            sp.dma_start(tok_f[:], token_ids).then_inc(loaded, 16)
            sp.wait_ge(zero_set, 1)
            sp.dma_start(slot_token.rearrange("(p n) o -> p (n o)", p=P), zero[:]).then_inc(zeroed, 16)
            sp.wait_ge(results, 4)
            sp.dma_start(gather_d, gat[:]).then_inc(stored, 16)
            sp.dma_start(prob_d, weight[:]).then_inc(stored, 16)
            sp.dma_start(scatter_d[:, 0:2, :], sca[:]).then_inc(stored, 16)
            sp.dma_start(scatter_d[:, 2, :], tok[:]).then_inc(stored, 16)
            sp.wait_ge(stored, 4 * 16)
            sp.wait_ge(zeroed, 16)

        @block.tensor
        def _(pe):
            pe.wait_ge(loaded, (NT + 3) * 16)
            pe.wait_ge(ones_set, 1)
            pe.wait_ge(chosen_done, 1)
            flat = chosen[:].rearrange("p t e -> p (t e)")
            pe.matmul(count_bank[0][:, :], tri[:, :], flat, start=True, stop=True)
            pe.matmul(count_bank[1][:, :], ones[:, :], flat, start=True, stop=True).then_inc(counted, 1)

        @block.scalar
        def _(act):
            act.wait_ge(gap_done, 1)
            act.activation(e2[:], gap[:], ACT.Exp).then_inc(exp_done, 1)

        @block.vector
        def _(dve):
            def step(ins):
                dve.drain()
                return ins

            def wide(a):
                return a.unsqueeze(2).broadcast_to([P, NTILE, E8])

            dve.memset(ones[:], 1.0).then_inc(ones_set, 1)
            dve.memset(zero[:], 0).then_inc(zero_set, 1)
            dve.wait_ge(loaded, (NT + 3) * 16)
            src = lg
            for k in range(2):
                step(dve.tensor_reduce(best[k][:], src[:], AX.X, ALU.max))
                step(dve.tensor_tensor(eq[k][:], src[:], wide(best[k][:]), ALU.is_equal))
                step(dve.tensor_tensor(at[k][:], eq[k][:], io[:], ALU.mult))
                step(dve.tensor_reduce(first[k][:], at[k][:], AX.X, ALU.min))
                step(dve.tensor_tensor(oh[k][:], io[:], wide(first[k][:]), ALU.is_equal))
                if k == 0:
                    step(dve.scalar_tensor_tensor(lg2[:], oh[0][:], -1e38, lg[:], ALU.mult, ALU.add))
                    src = lg2
            dve.tensor_tensor(chosen[:], oh[0][:], oh[1][:], ALU.add).then_inc(chosen_done, 1)
            dve.tensor_tensor(gap[:], best[1][:], best[0][:], ALU.subtract).then_inc(gap_done, 1)
            dve.wait_ge(exp_done, 1)
            step(dve.tensor_scalar(total[:], e2[:], 1.0, None, ALU.add))
            step(dve.reciprocal(prob[:, 0, :], total[:]))
            dve.tensor_tensor(prob[:, 1, :], prob[:, 0, :], e2[:], ALU.mult)
            dve.wait_ge(counted, 1)
            step(dve.tensor_copy(scan[0][:].rearrange("p t e -> p (t e)"), count_bank[1][:, :]))
            for n in range(6):
                d = 1 << n
                dve.tensor_copy(scan[n + 1][:, 0:d, :], scan[n][:, 0:d, :])
                step(dve.tensor_tensor(scan[n + 1][:, d:, :], scan[n][:, d:, :], scan[n][:, :NTILE - d, :], ALU.add))
            step(dve.tensor_tensor(base[:], scan[6][:], scan[0][:], ALU.subtract))
            step(dve.tensor_tensor(place[:].rearrange("p t e -> p (t e)"), count_bank[0][:, :],
                                   base[:].rearrange("p t e -> p (t e)"), ALU.add))
            dve.tensor_scalar(keep[:], place[:], float(CAP), None, ALU.is_lt)
            dve.scalar_tensor_tensor(slot[:], io[:], float(CAP), place[:], ALU.mult, ALU.add)
            dve.drain()
            for k in range(2):
                dve.tensor_tensor(pick[k][:], oh[k][:], slot[:], ALU.mult)
                dve.tensor_tensor(pick[2 + k][:], oh[k][:], keep[:], ALU.mult)
            dve.drain()
            for k in range(2):
                dve.tensor_reduce(slot_k[:, k, :], pick[k][:], AX.X, ALU.add)
                dve.tensor_reduce(keep_k[:, k, :], pick[2 + k][:], AX.X, ALU.add)
            dve.drain()
            dve.tensor_tensor(weight[:], prob[:], keep_k[:], ALU.mult).then_inc(results, 1)
            step(dve.scalar_tensor_tensor(gat_f[:], slot_k[:], float(EXPERTS * CAP), keep_k[:], ALU.add, ALU.mult))
            dve.tensor_copy(gat[:], gat_f[:]).then_inc(results, 1)
            step(dve.tensor_scalar(out_f[:], keep_k[:], -1.0, -float(1 << 20), ALU.add, ALU.mult))
            step(dve.tensor_tensor(sca_f[:], gat_f[:], out_f[:], ALU.add))
            dve.tensor_copy(sca[:], sca_f[:]).then_inc(results, 1)
            dve.tensor_copy(tok[:], tok_f[:]).then_inc(results, 1)


def fill_slots(nc, scatter_d, slot_token):
    PER = 8
    with ExitStack() as ctx:
        table = ctx.enter_context(nc.sbuf_tensor("f_table", [P, 3, T // P], U32))
        cols = ctx.enter_context(nc.sbuf_tensor("f_cols", [P, 3, PER], U32))
        loaded = ctx.enter_context(nc.semaphore("f_loaded"))
        written = Signal(ctx, nc, "f_written", 2 * PER, 0, 16)
        block = ctx.enter_context(nc.Block())

        @block.gpsimd
        def _(pool):
            pool.dma_start(table[:], scatter_d).then_inc(loaded, 16)
            pool.wait_ge(loaded, 16)
            with pool.Fori(0, T // P // PER) as i:
                pool.tensor_copy(cols[:], table[:, :, bass.ds(i * PER, PER)])
                pool.drain()
                for t in range(PER):
                    for k in range(2):
                        pool.indirect_dma_start(slot_token, bass.IndirectOffsetOnAxis(ap=cols[:, k, t:t + 1], axis=0),
                                                cols[:, 2, t:t + 1], None, bounds_check=SLOTS_ALL - 1,
                                                oob_is_err=False).then_inc(written.sem, 16)
                pool.wait_ge(written.sem, written.at(i, 2 * PER - 1))


def experts(nc, slot_token, xn, w1, w2, ident, slot_out):
    NB = 512
    BLOCKS = CAP // NB
    A = NB // P
    FC = FFN // P
    UNITS = 2 * BLOCKS
    H_BANKS = 4
    TURNS = EXPERTS // 2
    with ExitStack() as ctx:
        def sb(name, shape, dt=F32):
            return ctx.enter_context(nc.sbuf_tensor("e_" + name, shape, dt))

        def sig(name, per, prime=0, unit=1):
            return Signal(ctx, nc, "e_" + name, per, prime, unit)

        eye = sb("eye", [P, P])
        w1s = [sb(f"w1{k}", [P, DC, FFN]) for k in range(2)]
        w2s = [sb(f"w2{k}", [P, FC, D]) for k in range(2)]
        ids = sb("ids", [P, 2, A], U32)
        rows = sb("rows", [P, 2, A, D])
        xt = sb("xt", [P, 2, DC, NB])
        hid = sb("hid", [P, 2, FC, NB])
        out = sb("out", [P, 2, A, D])
        t_bank = [ctx.enter_context(nc.psum_tensor(f"e_t{k}", [P, 512], F32)) for k in range(2)]
        h_bank = [ctx.enter_context(nc.psum_tensor(f"e_h{k}", [P, 512], F32)) for k in range(H_BANKS)]
        o_bank = [ctx.enter_context(nc.psum_tensor(f"e_o{k}", [P, 512], F32)) for k in range(2)]
        consts = sig("consts", 1, 0, 16)
        w_in = [sig(f"w_in{k}", 2, 0, 16) for k in range(2)]
        ids_in = [sig(f"ids_in{k}", BLOCKS, 0, 16) for k in range(2)]
        rows_in = [sig(f"rows_in{k}", BLOCKS * A, 0, 16) for k in range(2)]
        t_ready = sig("t_ready", UNITS * 2, 4)
        t_copied = sig("t_copied", UNITS * 2, 2)
        h_ready = sig("h_ready", UNITS * FC, 2 * FC)
        gelu_done = sig("gelu_done", UNITS * FC, H_BANKS)
        o_ready = sig("o_ready", UNITS * 2, 4)
        o_copied = sig("o_copied", UNITS * 2, 2)
        stored = [sig(f"stored{k}", BLOCKS, 1, 16) for k in range(2)]
        ticks = sig("ticks", 1)
        ticks2 = sig("ticks2", 1)
        block = ctx.enter_context(nc.Block())

        def units():
            return [(u, u // BLOCKS, u % BLOCKS) for u in range(UNITS)]

        @block.sync
        def _(sp):
            sp.dma_start(eye[:], ident).then_inc(consts.sem, 16)
            for s in stored:
                sp.sem_inc(s.sem, s.start)

            def weights(e, k):
                a, b = (w1[e], w2[e]) if isinstance(e, int) else (
                    w1[bass.ds(e, 1)].rearrange("o d f -> (o d) f"), w2[bass.ds(e, 1)].rearrange("o f d -> (o f) d"))
                sp.dma_start(w1s[k][:], a.rearrange("(c p) f -> p c f", p=P)).then_inc(w_in[k].sem, 16)
                sp.dma_start(w2s[k][:], b.rearrange("(c p) d -> p c d", p=P)).then_inc(w_in[k].sem, 16)

            def store(i, u):
                sp.wait_ge(o_copied.sem, o_copied.at(i, 2 * u + 1))
                sp.sem_inc(ticks.sem, 1)
                sp.dma_start(slot_out[bass.ds((i * UNITS + u) * NB, NB), :].rearrange("(p a) d -> p (a d)", a=A),
                             out[:, u % 2].rearrange("p a d -> p (a d)")).then_inc(stored[u % 2].sem, 16)

            weights(0, 0)
            weights(1, 1)

            def turn(i, last):
                for u, k, b in units():
                    store(i, u)
                    if b == BLOCKS - 1 and not last:
                        weights(i * 2 + 2 + k, k)
            with sp.Fori(0, TURNS - 1) as i:
                turn(i, False)
            turn(TURNS - 1, True)
            for k in range(2):
                sp.wait_ge(stored[k].sem, stored[k].at(TURNS - 1, BLOCKS - 1))

        @block.gpsimd
        def _(pool):
            pool.sem_inc(t_ready.sem, t_ready.start)

            def gather(i, u):
                n = u // 2
                pool.wait_ge(t_ready.sem, t_ready.at(i, 2 * u - 3))
                pool.sem_inc(ticks2.sem, 1)
                pool.dma_start(ids[:, u % 2, :], slot_token[bass.ds((i * UNITS + u) * NB, NB), :].rearrange(
                    "(p a) o -> p (a o)", a=A)).then_inc(ids_in[u % 2].sem, 16)
                pool.wait_ge(ids_in[u % 2].sem, ids_in[u % 2].at(i, n))
                pool.sem_inc(ticks2.sem, 1)
                for a in range(A):
                    pool.indirect_dma_start(rows[:, u % 2, a, :], None, xn,
                                            bass.IndirectOffsetOnAxis(ap=ids[:, u % 2, a:a + 1], axis=0),
                                            bounds_check=T - 1, oob_is_err=False).then_inc(rows_in[u % 2].sem, 16)

            with pool.Fori(0, TURNS) as i:
                for u, _, _ in units():
                    gather(i, u)

        @block.tensor
        def _(pe):
            pe.wait_ge(consts.sem, consts.at(0))
            pe.sem_inc(h_ready.sem, h_ready.start)
            pe.sem_inc(o_ready.sem, o_ready.start)

            def turned(i, u):
                pe.wait_ge(rows_in[u % 2].sem, rows_in[u % 2].at(i, (u // 2) * A + A - 1))
                for k in range(DC):
                    pe.wait_ge(t_copied.sem, t_copied.at(i, 2 * u + k - 2))
                    for a in range(A):
                        mm = pe.transpose(t_bank[k][:, a * P:a * P + P], rows[:, u % 2, a, k * P:k * P + P], eye[:, :])
                    mm.then_inc(t_ready.sem, 1)

            def up(i, u, e):
                if u % BLOCKS == 0:
                    pe.wait_ge(w_in[e].sem, w_in[e].at(i, 1))
                pe.wait_ge(t_copied.sem, t_copied.at(i, 2 * u + 1))
                for f in range(FC):
                    n = u * FC + f
                    pe.wait_ge(gelu_done.sem, gelu_done.at(i, n - H_BANKS))
                    bank = h_bank[n % H_BANKS]
                    for k in range(DC):
                        mm = pe.matmul(bank[:, :], w1s[e][:, k, f * P:f * P + P], xt[:, u % 2, k, :], start=(k == 0),
                                       stop=(k == DC - 1))
                    mm.then_inc(h_ready.sem, 1)

            def down(i, u, e):
                pe.wait_ge(gelu_done.sem, gelu_done.at(i, u * FC + FC - 1))
                for pair in range(2):
                    pe.wait_ge(o_copied.sem, o_copied.at(i, 2 * u + pair - 2))
                    for a in (2 * pair, 2 * pair + 1):
                        for f in range(FC):
                            mm = pe.matmul(o_bank[pair][:, (a % 2) * D:(a % 2) * D + D],
                                           hid[:, u % 2, f, a * P:a * P + P], w2s[e][:, f, :], start=(f == 0),
                                           stop=(f == FC - 1))
                    mm.then_inc(o_ready.sem, 1)

            with pe.Fori(0, TURNS) as i:
                turned(i, 0)
                for u, e, _ in units():
                    if u + 1 < UNITS:
                        turned(i, u + 1)
                    up(i, u, e)
                    if u:
                        down(i, u - 1, (u - 1) // BLOCKS)
                down(i, UNITS - 1, 1)

        @block.scalar
        def _(act):
            act.sem_inc(gelu_done.sem, gelu_done.start)
            with act.Fori(0, TURNS) as i:
                for u, _, _ in units():
                    for f in range(FC):
                        n = u * FC + f
                        act.wait_ge(h_ready.sem, h_ready.at(i, n))
                        if f == 0:
                            act.wait_ge(o_ready.sem, o_ready.at(i, 2 * u - 3))
                        act.activation(hid[:, u % 2, f, :], h_bank[n % H_BANKS][:, :], ACT.Gelu).then_inc(gelu_done.sem, 1)

        @block.vector
        def _(dve):
            dve.sem_inc(t_copied.sem, t_copied.start)
            dve.sem_inc(o_copied.sem, o_copied.start)

            def copy_turned(i, u):
                for k in range(DC):
                    dve.wait_ge(t_ready.sem, t_ready.at(i, 2 * u + k))
                    if k == 0:
                        dve.wait_ge(h_ready.sem, h_ready.at(i, (u - 1) * FC - 1))
                    dve.tensor_copy(xt[:, u % 2, k, :], t_bank[k][:, :]).then_inc(t_copied.sem, 1)

            def copy_out(i, u):
                for pair in range(2):
                    dve.wait_ge(o_ready.sem, o_ready.at(i, 2 * u + pair))
                    if pair == 0:
                        dve.wait_ge(stored[u % 2].sem, stored[u % 2].at(i, u // 2 - 1))
                    dve.tensor_copy(out[:, u % 2, 2 * pair:2 * pair + 2, :].rearrange("p a d -> p (a d)"),
                                    o_bank[pair][:, :]).then_inc(o_copied.sem, 1)

            with dve.Fori(0, TURNS) as i:
                copy_turned(i, 0)
                for u, _, _ in units():
                    if u + 1 < UNITS:
                        copy_turned(i, u + 1)
                    if u:
                        copy_out(i, u - 1)
                copy_out(i, UNITS - 1)


def combine(nc, resid, slot_out, gather_d, prob_d, out):
    with ExitStack() as ctx:
        def sb(name, shape, dt=F32):
            return ctx.enter_context(nc.sbuf_tensor("o_" + name, shape, dt))

        def sig(name, per, prime=0, unit=1):
            return Signal(ctx, nc, "o_" + name, per, prime, unit)

        idx_all = sb("idx_all", [P, 2, T // P], U32)
        prob_all = sb("prob_all", [P, 2, T // P])
        idx = sb("idx", [P, 2, NT], U32)
        prob = sb("prob", [P, 2, NT])
        neg_half = sb("neg_half", [P, NT])
        r = sb("r", [P, NT, D])
        y = sb("y", [P, NT, 2, D])
        s1 = sb("s1", [P, NT, D])
        s2 = sb("s2", [P, NT, D])
        st = sb("st", [P, NT, 6])
        mv = sb("mv", [P, NT, 2])
        var = sb("var", [P, NT])
        rstd = sb("rstd", [P, NT])
        res = sb("res", [P, NT, D])
        tables = sig("tables", 2, 0, 16)
        r_in = sig("r_in", 1, 0, 16)
        y_in = [sig(f"y_in{t}", 2, 0, 16) for t in range(NT)]
        prob_set = sig("prob_set", 1)
        summed = sig("summed", NT, NT)
        mv_done = sig("mv_done", 1)
        eps_added = sig("eps_added", 1)
        rstd_done = sig("rstd_done", 1)
        res_done = sig("res_done", 1)
        res_out = sig("res_out", 1, 1, 16)
        ticks = sig("ticks", 1)
        pool_ticks = sig("pool_ticks", 1)
        block = ctx.enter_context(nc.Block())

        @block.sync
        def _(sp):
            sp.dma_start(idx_all[:], gather_d).then_inc(tables.sem, 16)
            sp.dma_start(prob_all[:], prob_d).then_inc(tables.sem, 16)
            sp.sem_inc(res_out.sem, res_out.start)
            sp.dma_start(r[:], resid[0].rearrange("(t p) d -> p t d", p=P)).then_inc(r_in.sem, 16)

            def turn(i, last):
                sp.wait_ge(summed.sem, summed.at(i, NT - 1))
                sp.sem_inc(ticks.sem, 1)
                if not last:
                    sp.dma_start(r[:], resid[bass.ds(i + 1, 1)].rearrange("o (t p) d -> p (o t) d", p=P)).then_inc(
                        r_in.sem, 16)
                sp.wait_ge(res_done.sem, res_done.at(i))
                sp.sem_inc(ticks.sem, 1)
                sp.dma_start(out[bass.ds(i, 1)].rearrange("o (t p) d -> p (o t) d", p=P), res[:]).then_inc(
                    res_out.sem, 16)
            with sp.Fori(0, N - 1) as i:
                turn(i, False)
            turn(N - 1, True)
            sp.wait_ge(res_out.sem, res_out.at(N - 1))

        @block.gpsimd
        def _(pool):
            pool.wait_ge(tables.sem, tables.at(0, 1))
            pool.sem_inc(pool_ticks.sem, 1)
            pool.memset(neg_half[:, :], -0.5)
            pool.drain()

            def gathers(i):
                pool.wait_ge(summed.sem, summed.at(i, -1))
                pool.sem_inc(pool_ticks.sem, 1)
                pool.tensor_copy(idx[:], idx_all[:, :, bass.ds(i * NT, NT)])
                pool.tensor_copy(prob[:], prob_all[:, :, bass.ds(i * NT, NT)]).then_inc(prob_set.sem, 1)
                pool.drain()
                for t in range(NT):
                    for k in range(2):
                        pool.indirect_dma_start(y[:, t, k, :], None, slot_out,
                                                bass.IndirectOffsetOnAxis(ap=idx[:, k, t:t + 1], axis=0),
                                                bounds_check=SLOTS_ALL - 1, oob_is_err=False).then_inc(y_in[t].sem, 16)

            with pool.Fori(0, N) as i:
                gathers(i)
                pool.wait_ge(mv_done.sem, mv_done.at(i))
                pool.sem_inc(pool_ticks.sem, 1)
                pool.tensor_scalar(var[:, :], mv[:, :, 1], EPS, None, ALU.add).then_inc(eps_added.sem, 1)
                pool.wait_ge(eps_added.sem, eps_added.at(i))
                pool.tensor_tensor(rstd[:, :], var[:, :], neg_half[:, :], ALU.pow).then_inc(rstd_done.sem, 1)

        @block.vector
        def _(dve):
            dve.sem_inc(summed.sem, summed.start)
            with dve.Fori(0, N) as i:
                dve.wait_ge(r_in.sem, r_in.at(i))
                dve.wait_ge(prob_set.sem, prob_set.at(i))
                for t in range(NT):
                    dve.wait_ge(y_in[t].sem, y_in[t].at(i, 1))
                    dve.scalar_tensor_tensor(s1[:, t, :], y[:, t, 0, :], prob[:, 0, t:t + 1], r[:, t, :], ALU.mult,
                                             ALU.add)
                    dve.drain()
                    dve.scalar_tensor_tensor(s2[:, t, :], y[:, t, 1, :], prob[:, 1, t:t + 1], s1[:, t, :], ALU.mult,
                                             ALU.add).then_inc(summed.sem, 1)
                dve.drain()
                for t in range(NT):
                    dve.bn_stats(st[:, t, :], s2[:, t, :])
                dve.drain()
                for t in range(NT):
                    ins = dve.bn_aggr(mv[:, t, :], st[:, t, :])
                ins.then_inc(mv_done.sem, 1)
                dve.wait_ge(rstd_done.sem, rstd_done.at(i))
                dve.wait_ge(res_out.sem, res_out.at(i, -1))
                for t in range(NT):
                    ins = dve.tensor_scalar(res[:, t, :], s2[:, t, :], mv[:, t, 0:1], rstd[:, t:t + 1], ALU.subtract,
                                            ALU.mult)
                ins.then_inc(res_done.sem, 1)
                dve.drain()


def program(nc, a, out):
    def scratch(name, shape, dt=F32):
        return nc.dram_tensor("d_" + name, shape, dt, kind="Internal").ap()

    spectral = scratch("spectral", [D, D])
    x2 = scratch("x2", [N, S, D])
    x2T = scratch("x2T", [N, D, S])
    x3 = scratch("x3", [N, S, D])
    split_q = scratch("split_q", [3, P, S], BF16)
    split_k = scratch("split_k", [3, P, S], BF16)
    guard_d = scratch("guard_d", [2, 3, 32, P], BF16)
    resid = scratch("resid", [N, S, D])
    xn = scratch("xn", [N, S, D])
    logits = scratch("logits", [NT, P, N, EXPERTS])
    gather_d = scratch("gather_d", [P, 2, T // P], U32)
    prob_d = scratch("prob_d", [P, 2, T // P])
    scatter_d = scratch("scatter_d", [P, 3, T // P], U32)
    slot_token = scratch("slot_token", [SLOTS_ALL, 1], U32)
    slot_out = scratch("slot_out", [SLOTS_ALL, D])

    spectral_matrix(nc, a["w_real"], a["w_imag"], a["cos"], a["nsin"], a["cos_n"], a["nsin_n"], spectral)
    linear_attention_and_spectral(nc, a["xT"], a["x"], a["wq"], a["bq"], a["wk"], a["bk"], a["wv"], a["bv"], a["wo"],
                                  a["bo"], a["ffn_bias"], a["ident"], spectral, x2, x2T)
    causal_attention(nc, x2, x2T, a["w_kqv"], a["ident"], a["above"], a["ramp_q"], a["ramp_k"], a["sel_q"],
                     a["sel_k"], a["m_rows"], split_q, split_k, guard_d, x3)
    position_attention(nc, x3, a["ln1_w"], a["ln1_b"], a["ln2_w"], a["ln2_b"], a["w_qkv"], a["w_proj"],
                       a["w_router"], a["ident"], resid, xn, logits)
    route(nc, logits, a["before"], a["iota"], a["token_ids"], gather_d, prob_d, scatter_d, slot_token)
    fill_slots(nc, scatter_d, slot_token)
    experts(nc, slot_token, xn.rearrange("n s d -> (n s) d"), a["w1"], a["w2"], a["ident"], slot_out)
    combine(nc, resid, slot_out, gather_d, prob_d, out)


def shape_constants():
    d = np.arange(D)
    angle = 2 * np.pi * (np.outer(d, d) % D) / D
    q = np.arange(P)
    pos = np.arange(S)
    high, low, zero, one = ((pos // P) * P, pos % P, 0 * pos, 0 * pos + 1)
    sel_q = np.zeros((15, 3))
    sel_k = np.zeros((15, 3))
    for part in range(3):
        sel_q[4 * part:4 * part + 2, part] = 1
        sel_k[4 * part + 2:4 * part + 4, part] = 1
    c = {
        "cos": np.cos(angle), "nsin": -np.sin(angle), "cos_n": np.cos(angle) / D, "nsin_n": -np.sin(angle) / D,
        "ident": np.eye(P),
        "above": np.stack([np.where(q[None, :] > q[:, None], -BIG, 0), np.where(q[None, :] < q[:, None], -BIG, 0)]),
        "ramp_q": np.stack([zero, zero, -high, -low] * 3 + [zero] * 3),
        "ramp_k": np.stack([high, low, zero, zero] * 3 + [-one] * 3),
        "sel_q": sel_q, "sel_k": sel_k,
        "before": q[:, None] < q[None, :],
        "iota": np.broadcast_to(np.arange(-EXPERTS, 0), (P, T // P, EXPERTS)),
        "token_ids": np.arange(T // P)[None, :] * P + q[:, None],
    }
    return {k: np.ascontiguousarray(v, dtype=np.float32) for k, v in c.items()}


def kernel(**inputs):
    import concourse.bacc as bacc
    from concourse.bass_utils import run_bass_kernel_spmd

    t = {k: np.asarray(v) for k, v in inputs.items()}

    def by_partition(v):
        return v.reshape(DC, P).T

    def on_all(v):
        return np.broadcast_to(v, (P, 2, D))

    arrays = {
        "x": t["L0_attn_x"], "xT": t["L0_attn_x"].transpose(0, 2, 1),
        "wq": t["L0_attn_Wq"], "wk": t["L0_attn_Wk"], "wv": t["L0_attn_Wv"], "wo": t["L0_attn_Wo"],
        "bq": by_partition(t["L0_attn_bq"]), "bk": by_partition(t["L0_attn_bk"]), "bv": by_partition(t["L0_attn_bv"]),
        "bo": on_all(t["L0_attn_bo"]), "ffn_bias": on_all(t["L0_ffn_bias"]),
        "w_real": t["L0_ffn_w_freq_real"], "w_imag": t["L0_ffn_w_freq_imag"],
        "w_kqv": t["L1_attn_W_kqv"], "m_rows": np.broadcast_to(t["L1_attn_m"].reshape(1, 16), (15, 16)),
        "ln1_w": on_all(t["L1_ffn_ln1_weight"]), "ln1_b": on_all(t["L1_ffn_ln1_bias"]),
        "ln2_w": on_all(t["L1_ffn_ln2_weight"]), "ln2_b": on_all(t["L1_ffn_ln2_bias"]),
        "w_qkv": t["L1_ffn_qkv_weight"].T, "w_proj": t["L1_ffn_proj_weight"].T,
        "w_router": t["L1_ffn_router_weight"], "w1": t["L1_ffn_moe_w1"], "w2": t["L1_ffn_moe_w2"],
    }
    arrays = {k: np.ascontiguousarray(v) for k, v in arrays.items()}
    arrays.update(shape_constants())
    nc = bacc.Bacc("TRN2", target_bir_lowering=False, num_devices=1)
    a = {k: nc.dram_tensor("in_" + k, v.shape, mybir.dt.from_np(v.dtype), kind="ExternalInput").ap()
         for k, v in arrays.items()}
    out = nc.dram_tensor("out", (N, S, D), F32, kind="ExternalOutput").ap()
    program(nc, a, out)
    r = run_bass_kernel_spmd(nc, [{"in_" + k: v for k, v in arrays.items()}], core_ids=[0])
    return r.results[0]["out"]
```

```python
from contextlib import ExitStack

import numpy as np
import concourse.bass as bass
from concourse import mybir

F32 = mybir.dt.float32
BF16 = mybir.dt.bfloat16
U32 = mybir.dt.uint32
ALU = mybir.AluOpType
ACT = mybir.ActivationFunctionType
AX = mybir.AxisListType

P = 128
N, S, D = 8, 1024, 256
DC = D // P
NT = S // P
NPAIR = NT // 2
T = N * S
EPS = 1e-5
BIG = 1e30


class Signal:

    def __init__(self, ctx, nc, name, per, prime=0, unit=1):
        self.sem = ctx.enter_context(nc.semaphore(name))
        self.per, self.prime, self.unit = per, prime, unit
        self.start = prime * unit

    def at(self, i, k=0):
        return i * (self.per * self.unit) + (k + 1 + self.prime) * self.unit


def spectral_matrix(nc, w_real, w_imag, cos, nsin, cos_n, nsin_n, spectral):
    with ExitStack() as ctx:
        def sb(name, shape, dt=F32):
            return ctx.enter_context(nc.sbuf_tensor("m_" + name, shape, dt))

        wr = sb("wr", [P, DC, D])
        wi = sb("wi", [P, DC, D])
        c = sb("c", [P, DC, D])
        ns = sb("ns", [P, DC, D])
        ps = sb("ps", [P, DC, D])
        cn = sb("cn", [P, DC, D])
        nsn = sb("nsn", [P, DC, D])
        re_t = sb("re_t", [P, DC, D])
        im_t = sb("im_t", [P, DC, D])
        m = sb("m", [P, DC, D])
        bank = [ctx.enter_context(nc.psum_tensor(f"m_bank{i}", [P, 512], F32)) for i in range(6)]
        loaded = ctx.enter_context(nc.semaphore("m_loaded"))
        sin_ready = ctx.enter_context(nc.semaphore("m_sin_ready"))
        product = ctx.enter_context(nc.semaphore("m_product"))
        copied = ctx.enter_context(nc.semaphore("m_copied"))
        stored = ctx.enter_context(nc.semaphore("m_stored"))
        block = ctx.enter_context(nc.Block())

        @block.sync
        def _(sp):
            for dst, src in ((wr, w_real), (wi, w_imag), (c, cos), (ns, nsin), (cn, cos_n), (nsn, nsin_n)):
                sp.dma_start(dst[:], src.rearrange("(c p) n -> p c n", p=P)).then_inc(loaded, 16)
            sp.wait_ge(copied, 6)
            sp.dma_start(spectral.rearrange("(c p) n -> p c n", p=P), m[:]).then_inc(stored, 16)
            sp.wait_ge(stored, 16)

        @block.tensor
        def _(pe):
            pe.wait_ge(loaded, 6 * 16)
            pe.wait_ge(sin_ready, 1)
            for oc in range(DC):
                cols = slice(oc * P, oc * P + P)
                for n, (a, b) in enumerate(((wi, ps), (wr, ns))):
                    main = wr if n == 0 else wi
                    out = bank[2 * oc + n][:, 0:D]
                    for k in range(DC):
                        pe.matmul(out, main[:, k, cols], c[:, k, :], start=(k == 0), stop=False)
                    for k in range(DC):
                        mm = pe.matmul(out, a[:, k, cols], b[:, k, :], start=False, stop=(k == DC - 1))
                    mm.then_inc(product, 1)
            pe.wait_ge(copied, 4)
            for dc in range(DC):
                cols = slice(dc * P, dc * P + P)
                out = bank[4 + dc][:, 0:D]
                for k in range(DC):
                    pe.matmul(out, re_t[:, k, cols], cn[:, k, :], start=(k == 0), stop=False)
                for k in range(DC):
                    mm = pe.matmul(out, im_t[:, k, cols], nsn[:, k, :], start=False, stop=(k == DC - 1))
                mm.then_inc(product, 1)

        @block.vector
        def _(dve):
            dve.wait_ge(loaded, 6 * 16)
            dve.tensor_scalar(ps[:], ns[:], -1.0, None, ALU.mult).then_inc(sin_ready, 1)
            for n, dst in enumerate((re_t[:, 0, :], im_t[:, 0, :], re_t[:, 1, :], im_t[:, 1, :], m[:, 0, :], m[:, 1, :])):
                dve.wait_ge(product, n + 1)
                dve.tensor_copy(dst, bank[n][:, 0:D]).then_inc(copied, 1)


def linear_attention_and_spectral(nc, xT, x, wq, bq, wk, bk, wv, bv, wo, bo2, bias2, w_kqv, ident, spectral, x2,
                                  split, v_d):
    SLOTS = 10
    FRONT = {0: ("k0", "v0"), 1: ("k1", "v1"), 2: ("k2", "v2"), 3: ("k3", "v3"), 5: ("q4",), 6: ("q5",), 7: ("q6",),
             8: ("q7",)}
    NEXT = {6: ((0, 0, 0), (0, 1, 0), (1, 0, 0)), 7: ((1, 1, 0), ("v", 0), ("v", 1)),
            8: ((0, 0, 1), (0, 1, 1), (1, 0, 1)), 9: ((1, 1, 1), ("v", 2), ("v", 3))}
    NEXT_ORDER = [u for s in sorted(NEXT) for u in NEXT[s]]
    SPLIT_ORDER = [u for u in NEXT_ORDER if u[0] != "v"]
    TURNED = [(w, s - 2 - 2 * w) for s in range(SLOTS) for w in (0, 1) if 0 <= s - 2 - 2 * w < NPAIR]
    HEADS, HD, VW = 16, 16, 32
    HH = HEADS // 2
    with ExitStack() as ctx:
        def sb(name, shape, dt=F32):
            return ctx.enter_context(nc.sbuf_tensor("a_" + name, shape, dt))

        def sig(name, per, prime=0, unit=1):
            return Signal(ctx, nc, "a_" + name, per, prime, unit)

        def psum(name):
            return ctx.enter_context(nc.psum_tensor("a_" + name, [P, 512], F32))

        w = {k: sb("w" + k, [P, DC, D]) for k in "qkvom"}
        w_next = sb("w_next", [P, DC, 3 * D])
        b = {k: sb("b" + k, [P, DC]) for k in "qkv"}
        minus_b = {k: sb("minus_b" + k, [P, DC]) for k in "qk"}
        bo_b = sb("bo_b", [P, 2, D])
        bias_b = sb("bias_b", [P, 2, D])
        eye = sb("eye", [P, P])
        neg_half = sb("neg_half", [P, 2])
        xt = sb("xt", [P, DC, S])
        xs = sb("xs", [P, NT, D])
        n_t = sb("n_t", [P, 2, 512])
        e_t = sb("e_t", [P, 2, 512])
        r_t = sb("r_t", [P, 2, 512])
        keys = sb("keys", [P, DC, S])
        q_t = sb("q_t", [P, 2, 512])
        z_t = sb("z_t", [P, 2, 512])
        junk = sb("junk", [P, 512])
        ksum2 = sb("ksum2", [P, DC, 2])
        kv2 = sb("kv2", [P, DC, 2])
        ksum = sb("ksum", [P, DC])
        kv = sb("kv", [P, DC])
        vp = sb("vp", [P, DC, S])
        pre = sb("pre", [P, 2, 2, D])
        g = sb("g", [P, 2, 2, D])
        h = sb("h", [P, NT, D])
        x1 = sb("x1", [P, NT, D])
        x1b = sb("x1b", [P, NT, D])
        h2 = sb("h2", [P, NT, D])
        x2s = sb("x2s", [P, NT, D])
        st = sb("st", [P, NT, 2, 6])
        mv = sb("mv", [P, 2, NT, 2])
        var = sb("var", [P, 2, NT])
        rstd = sb("rstd", [P, 2, NT])
        x1t = sb("x1t", [P, 2, DC, 2 * P])
        x2t = sb("x2t", [P, DC, S])
        parts = sb("parts", [P, 2, 3, 512], BF16)
        rest = sb("rest", [P, 2, 512])
        vs = sb("vs", [P, 2, NT, HH, VW])
        act_bank = [psum(f"act{k}") for k in range(2)]
        v_bank, o_bank, t_bank, m_bank = (psum(k) for k in ("v", "o", "t", "mb"))
        next_bank = [psum(f"next{k}") for k in range(2)]

        consts = sig("consts", 1, 0, 16)
        xt_in = sig("xt_in", 1, 0, 16)
        xs_in = sig("xs_in", 1, 0, 16)
        kq_ready = sig("kq_ready", 8)
        v_ready = sig("v_ready", 4)
        er_ready = sig("er_ready", 8, 2)
        er_read = sig("er_read", 8, 2)
        v_done = sig("v_done", 4, 1)
        vp_done = sig("vp_done", 4)
        o_ready = sig("o_ready", NPAIR)
        o_added = sig("o_added", NPAIR, 1)
        gelu_done = sig("gelu_done", NPAIR, 2)
        h_done = sig("h_done", NPAIR, 2)
        mv_done = [sig(f"mv_done{k}", NPAIR) for k in range(2)]
        eps_added = [sig(f"eps_added{k}", NPAIR) for k in range(2)]
        rstd_done = [sig(f"rstd_done{k}", NPAIR) for k in range(2)]
        x1_done = sig("x1_done", NPAIR)
        x1b_done = sig("x1b_done", NPAIR)
        turned = sig("turned", 2 * NPAIR)
        turned_read = sig("turned_read", 2 * NPAIR, 1)
        m_ready = sig("m_ready", NPAIR, 2)
        h2_done = sig("h2_done", NPAIR, 1)
        x2_done = sig("x2_done", NPAIR)
        next_ready = sig("next_ready", 12)
        high_done = sig("high_done", 8)
        rest_done = sig("rest_done", 8)
        v_copied = sig("v_copied", 4)
        split_done = sig("split_done", 8, 2)
        split_out = [sig(f"split_out{k}", 4, 1, 16) for k in range(2)]
        v_set = sig("v_set", 1)
        v_out = sig("v_out", 1, 1, 16)
        x2_out = sig("x2_out", 1, 1, 16)
        ticks = sig("ticks", 1)
        pool_ticks = sig("pool_ticks", 1)
        block = ctx.enter_context(nc.Block())

        def turns(eng, turn, front):
            for s in range(SLOTS + 1):
                front(0, s)
            with eng.Fori(0, N - 1) as i:
                turn(i, lambda s: front(i + 1, s))
            turn(N - 1, lambda s: None)

        def front_units(s, kinds):
            return [(u[0], int(u[1])) for u in FRONT.get(s, ()) if u[0] in kinds]

        def bank_read(at):
            u = NEXT_ORDER[at]
            if u[0] == "v":
                return v_copied, u[1]
            return rest_done, SPLIT_ORDER.index(u)

        @block.sync
        def _(sp):
            for k, src in zip("qkvom", (wq, wk, wv, wo, spectral)):
                sp.dma_start(w[k][:], src.rearrange("(c p) n -> p c n", p=P)).then_inc(consts.sem, 16)
            for k, src in zip("qkv", (bq, bk, bv)):
                sp.dma_start(b[k][:], src).then_inc(consts.sem, 16)
            sp.dma_start(w_next[:], w_kqv.rearrange("(c p) n -> p c n", p=P)).then_inc(consts.sem, 16)
            sp.dma_start(bo_b[:], bo2).then_inc(consts.sem, 16)
            sp.dma_start(bias_b[:], bias2).then_inc(consts.sem, 16)
            sp.dma_start(eye[:], ident).then_inc(consts.sem, 16)
            sp.sem_inc(x2_out.sem, x2_out.start)
            sp.sem_inc(v_out.sem, v_out.start)
            for k in range(2):
                sp.sem_inc(split_out[k].sem, split_out[k].start)
            sp.dma_start(xt[:], xT[0].rearrange("(c p) s -> p c s", p=P)).then_inc(xt_in.sem, 16)
            sp.dma_start(xs[:], x[0].rearrange("(t p) d -> p t d", p=P)).then_inc(xs_in.sem, 16)
            sp.wait_ge(kq_ready.sem, kq_ready.at(0, 7))
            sp.wait_ge(v_ready.sem, v_ready.at(0, 3))
            sp.dma_start(xt[:], xT[1].rearrange("(c p) s -> p c s", p=P)).then_inc(xt_in.sem, 16)

            def turn(i, more_x, more_xt):
                sp.wait_ge(h_done.sem, h_done.at(i, NPAIR - 1))
                sp.sem_inc(ticks.sem, 1)
                if more_x:
                    sp.dma_start(xs[:], x[bass.ds(i + 1, 1)].rearrange("o (t p) d -> p (o t) d", p=P)).then_inc(
                        xs_in.sem, 16)
                for n, (kind, half, c) in enumerate(SPLIT_ORDER):
                    if n == 4:
                        sp.wait_ge(x2_done.sem, x2_done.at(i, NPAIR - 1))
                        sp.sem_inc(ticks.sem, 1)
                        sp.dma_start(x2[bass.ds(i, 1)].rearrange("o (t p) d -> p (o t) d", p=P), x2s[:]).then_inc(
                            x2_out.sem, 16)
                        if more_xt:
                            sp.wait_ge(kq_ready.sem, kq_ready.at(i + 1, 7))
                            sp.wait_ge(v_ready.sem, v_ready.at(i + 1, 3))
                            sp.sem_inc(ticks.sem, 1)
                            sp.dma_start(xt[:], xT[bass.ds(i + 2, 1)].rearrange("o (c p) s -> p (o c) s", p=P)
                                         ).then_inc(xt_in.sem, 16)
                    sp.wait_ge(split_done.sem, split_done.at(i, n))
                    sp.sem_inc(ticks.sem, 1)
                    sp.dma_start(split[bass.ds((i * 2 + half) * 2 + kind, 1), :, :, c * 512:c * 512 + 512].rearrange(
                        "o r p s -> p (o r) s"), parts[:, n % 2]).then_inc(split_out[n % 2].sem, 16)
                sp.wait_ge(v_copied.sem, v_copied.at(i, 3))
                sp.sem_inc(ticks.sem, 1)
                sp.dma_start(v_d[bass.ds(i, 1)].rearrange("o p n -> p (o n)"),
                             vs[:].rearrange("p a t h w -> p (a t h w)")).then_inc(v_out.sem, 16)

            with sp.Fori(0, N - 2) as i:
                turn(i, True, True)
            turn(N - 2, True, False)
            turn(N - 1, False, False)
            sp.wait_ge(x2_out.sem, x2_out.at(N - 1))
            sp.wait_ge(v_out.sem, v_out.at(N - 1))
            for k in range(2):
                sp.wait_ge(split_out[k].sem, split_out[k].at(N - 1, 3))

        @block.tensor
        def _(pe):
            pe.wait_ge(consts.sem, 12 * 16)
            pe.sem_inc(m_ready.sem, m_ready.start)

            def front(i, s):
                for kind, n in front_units(s, "kvq"):
                    hc, c = (n % 2, (n - 4) // 2) if kind == "q" else (n // 2, n % 2)
                    if (kind, n) == ("k", 0):
                        pe.wait_ge(xt_in.sem, xt_in.at(i))
                    if kind == "v":
                        pe.wait_ge(v_done.sem, v_done.at(i, n - 1))
                        bank = v_bank
                    else:
                        pe.wait_ge(er_ready.sem, er_ready.at(i, n - 2))
                        bank = act_bank[n % 2]
                    for k in range(DC):
                        mm = pe.matmul(bank[:, :], w[kind][:, k, hc * P:hc * P + P], xt[:, k, c * 512:c * 512 + 512],
                                       start=(k == 0), stop=(k == DC - 1))
                    mm.then_inc(v_ready.sem if kind == "v" else kq_ready.sem, 1)

            def transpose_pair(i, which, p):
                at = TURNED.index((which, p))
                src, done = ((x1, x1_done), (x2s, x2_done))[which]
                pe.wait_ge(done.sem, done.at(i, p))
                pe.wait_ge(turned_read.sem, turned_read.at(i, at - 1))
                for k in range(DC):
                    for t in (2 * p, 2 * p + 1):
                        c0 = k * 256 + (t % 2) * P
                        mm = pe.transpose(t_bank[:, c0:c0 + P], src[:, t, k * P:k * P + P], eye[:, :])
                mm.then_inc(turned.sem, 1)

            def turn(i, next_front):
                for s in range(SLOTS):
                    if s < NPAIR:
                        p = s
                        pe.wait_ge(vp_done.sem, vp_done.at(i, (2 * p // 4) * 2 + 1))
                        pe.wait_ge(o_added.sem, o_added.at(i, p - 1))
                        for t in (2 * p, 2 * p + 1):
                            for k in range(DC):
                                mm = pe.matmul(o_bank[:, (t % 2) * D:(t % 2) * D + D], vp[:, k, t * P:t * P + P],
                                               w["o"][:, k, :], start=(k == 0), stop=(k == DC - 1))
                        mm.then_inc(o_ready.sem, 1)
                    next_front(s)
                    if 0 <= s - 2 < NPAIR:
                        transpose_pair(i, 0, s - 2)
                    if 0 <= s - 3 < NPAIR:
                        p = s - 3
                        pe.wait_ge(turned_read.sem, turned_read.at(i, TURNED.index((0, p))))
                        pe.wait_ge(h2_done.sem, h2_done.at(i, p - 1))
                        for t in (2 * p, 2 * p + 1):
                            for k in range(DC):
                                mm = pe.matmul(m_bank[:, (t % 2) * D:(t % 2) * D + D],
                                               x1t[:, p % 2, k, (t % 2) * P:(t % 2) * P + P], w["m"][:, k, :],
                                               start=(k == 0), stop=(k == DC - 1))
                        mm.then_inc(m_ready.sem, 1)
                    if 0 <= s - 4 < NPAIR:
                        transpose_pair(i, 1, s - 4)
                    for u in NEXT.get(s, ()):
                        at = NEXT_ORDER.index(u)
                        half_of_tokens = u[1] // 2 if u[0] == "v" else u[2]
                        pe.wait_ge(turned_read.sem, turned_read.at(i, TURNED.index((1, 2 * half_of_tokens + 1))))
                        if at >= 2:
                            sig_, n = bank_read(at - 2)
                            pe.wait_ge(sig_.sem, sig_.at(i, n))
                        bank = next_bank[at % 2]
                        if u[0] == "v":
                            for t in (2 * u[1], 2 * u[1] + 1):
                                for k in range(DC):
                                    mm = pe.matmul(bank[:, (t % 2) * D:(t % 2) * D + D], x2t[:, k, t * P:t * P + P],
                                                   w_next[:, k, 2 * D:3 * D], start=(k == 0), stop=(k == DC - 1))
                        else:
                            kind, half, c = u
                            col = (1 - kind) * D + half * P
                            for k in range(DC):
                                mm = pe.matmul(bank[:, :], w_next[:, k, col:col + P], x2t[:, k, c * 512:c * 512 + 512],
                                               start=(k == 0), stop=(k == DC - 1))
                        mm.then_inc(next_ready.sem, 1)

            turns(pe, turn, front)

        @block.scalar
        def _(act):
            act.sem_inc(er_ready.sem, er_ready.start)
            act.sem_inc(gelu_done.sem, gelu_done.start)
            act.sem_inc(turned_read.sem, turned_read.start)
            act.wait_ge(consts.sem, 12 * 16)
            for kind in "kq":
                act.activation(minus_b[kind][:, :], b[kind][:, :], ACT.Copy, scale=-1.0)
            act.drain()

            def front(i, s):
                for kind, n in front_units(s, "kq"):
                    hc = n // 2 if kind == "k" else n % 2
                    act.wait_ge(kq_ready.sem, kq_ready.at(i, n))
                    act.wait_ge(er_read.sem, er_read.at(i, n - 2))
                    act.activation(n_t[:, n % 2, :], act_bank[n % 2][:, :], ACT.Relu, scale=-1.0,
                                   bias=minus_b[kind][:, hc:hc + 1])
                    act.activation(r_t[:, n % 2, :], act_bank[n % 2][:, :], ACT.Relu, bias=b[kind][:, hc:hc + 1])
                    act.drain()
                    act.activation(e_t[:, n % 2, :], n_t[:, n % 2, :], ACT.Exp, scale=-1.0).then_inc(er_ready.sem, 1)

            def copy_turned(i, which, p):
                at = TURNED.index((which, p))
                act.wait_ge(turned.sem, turned.at(i, at))
                if which == 0:
                    act.wait_ge(m_ready.sem, m_ready.at(i, p - 2))
                    dst = x1t[:, p % 2]
                else:
                    dst = x2t[:, :, 2 * p * P:2 * p * P + 2 * P]
                act.activation(dst, t_bank[:, :].rearrange("p (c t) -> p c t", c=DC), ACT.Copy).then_inc(
                    turned_read.sem, 1)

            def turn(i, next_front):
                for s in range(SLOTS):
                    next_front(s)
                    if 0 <= s - 2 < NPAIR:
                        copy_turned(i, 0, s - 2)
                    if 0 <= s - 4 < NPAIR:
                        copy_turned(i, 1, s - 4)
                    if s < NPAIR:
                        p = s
                        act.wait_ge(o_added.sem, o_added.at(i, p))
                        act.wait_ge(h_done.sem, h_done.at(i, p - 2))
                        act.activation(g[:, p % 2], pre[:, p % 2], ACT.Gelu_apprx_tanh).then_inc(gelu_done.sem, 1)
                    for u in NEXT.get(s, ()):
                        at = NEXT_ORDER.index(u)
                        act.wait_ge(next_ready.sem, next_ready.at(i, at))
                        if u[0] == "v":
                            if u[1] == 0:
                                act.wait_ge(v_set.sem, 1)
                                act.wait_ge(v_out.sem, v_out.at(i, -1))
                            for half in range(2):
                                ins = act.activation(
                                    vs[:, half, 2 * u[1]:2 * u[1] + 2, :, 0:HD],
                                    next_bank[at % 2][:, :].rearrange("p (t a h d) -> p a t h d", t=2, a=2, d=HD)[:, half],
                                    ACT.Copy)
                            ins.then_inc(v_copied.sem, 1)
                        else:
                            n = SPLIT_ORDER.index(u)
                            act.wait_ge(split_out[n % 2].sem, split_out[n % 2].at(i, n // 2 - 1))
                            act.activation(parts[:, n % 2, 0, :], next_bank[at % 2][:, :], ACT.Copy,
                                           scale=1.0 if u[0] else 1.0 / 16).then_inc(high_done.sem, 1)

            turns(act, turn, front)

        @block.vector
        def _(dve):
            dve.memset(vs[:], 0.0)
            dve.drain()
            dve.memset(vs[:].rearrange("p a t h w -> p (a t h) w")[:, :, HD:HD + 1], 1.0).then_inc(v_set.sem, 1)
            for s in (er_read, v_done, o_added, h_done, h2_done):
                dve.sem_inc(s.sem, s.start)
            dve.wait_ge(consts.sem, 12 * 16)

            def front(i, s):
                for kind, n in front_units(s - 1, "kq"):
                    hc, c = (n % 2, (n - 4) // 2) if kind == "q" else (n // 2, n % 2)
                    dve.wait_ge(er_ready.sem, er_ready.at(i, n))
                    dve.tensor_scalar(e_t[:, n % 2, :], e_t[:, n % 2, :], -1.0, None, ALU.add)
                    dve.drain()
                    if kind == "k":
                        chunk = keys[:, hc, c * 512:c * 512 + 512]
                        dve.scalar_tensor_tensor(chunk, e_t[:, n % 2, :], 1.0, r_t[:, n % 2, :], ALU.add, ALU.add,
                                                 accum_out=ksum2[:, hc, c:c + 1]).then_inc(er_read.sem, 1)
                        dve.drain()
                        dve.wait_ge(v_ready.sem, v_ready.at(i, n))
                        dve.scalar_tensor_tensor(junk[:, :], v_bank[:, :], b["v"][:, hc:hc + 1], chunk, ALU.add,
                                                 ALU.mult, accum_out=kv2[:, hc, c:c + 1]).then_inc(v_done.sem, 1)
                        if n == 3:
                            dve.drain()
                            dve.tensor_tensor(ksum[:, :], ksum2[:, :, 0], ksum2[:, :, 1], ALU.add)
                            dve.tensor_tensor(kv[:, :], kv2[:, :, 0], kv2[:, :, 1], ALU.add)
                            dve.drain()
                    else:
                        dve.scalar_tensor_tensor(q_t[:, n % 2, :], e_t[:, n % 2, :], 1.0, r_t[:, n % 2, :], ALU.add,
                                                 ALU.add).then_inc(er_read.sem, 1)
                        dve.drain()
                        dve.tensor_scalar(z_t[:, n % 2, :], q_t[:, n % 2, :], ksum[:, hc:hc + 1], 1e-6, ALU.mult,
                                          ALU.add)
                        dve.drain()
                        dve.reciprocal(z_t[:, n % 2, :], z_t[:, n % 2, :])
                        dve.drain()
                        dve.scalar_tensor_tensor(vp[:, hc, c * 512:c * 512 + 512], q_t[:, n % 2, :], kv[:, hc:hc + 1],
                                                 z_t[:, n % 2, :], ALU.mult, ALU.mult).then_inc(vp_done.sem, 1)

            def residual_stats(which, p, dst, a, c, done):
                hp = slice(2 * p, 2 * p + 2)
                dve.tensor_tensor(dst[:, hp, :], a, c[:, hp, :], ALU.add).then_inc(done.sem, 1)
                dve.drain()
                for t in (2 * p, 2 * p + 1):
                    dve.bn_stats(st[:, t, which, :], dst[:, t, :])
                dve.drain()
                for t in (2 * p, 2 * p + 1):
                    ins = dve.bn_aggr(mv[:, which, t, :], st[:, t, which, :])
                ins.then_inc(mv_done[which].sem, 1)

            def turn(i, next_front):
                for s in range(SLOTS):
                    if s < NPAIR:
                        p = s
                        dve.wait_ge(o_ready.sem, o_ready.at(i, p))
                        dve.wait_ge(gelu_done.sem, gelu_done.at(i, p - 2))
                        dve.tensor_tensor(pre[:, p % 2].rearrange("p t d -> p (t d)"), o_bank[:, :],
                                          bo_b[:].rearrange("p t d -> p (t d)"), ALU.add).then_inc(o_added.sem, 1)
                    if 0 <= s - 2 < NPAIR:
                        p = s - 2
                        dve.wait_ge(rstd_done[0].sem, rstd_done[0].at(i, p))
                        for t in (2 * p, 2 * p + 1):
                            ins = dve.tensor_scalar(x1[:, t, :], h[:, t, :], mv[:, 0, t, 0:1], rstd[:, 0, t:t + 1],
                                                    ALU.subtract, ALU.mult)
                        ins.then_inc(x1_done.sem, 1)
                    if 0 <= s - 4 < NPAIR:
                        p = s - 4
                        dve.wait_ge(rstd_done[1].sem, rstd_done[1].at(i, p))
                        if p == 0:
                            dve.wait_ge(x2_out.sem, x2_out.at(i, -1))
                        for t in (2 * p, 2 * p + 1):
                            ins = dve.tensor_scalar(x2s[:, t, :], h2[:, t, :], mv[:, 1, t, 0:1], rstd[:, 1, t:t + 1],
                                                    ALU.subtract, ALU.mult)
                        ins.then_inc(x2_done.sem, 1)
                    next_front(s)
                    if 0 <= s - 1 < NPAIR:
                        p = s - 1
                        if p == 0:
                            dve.wait_ge(xs_in.sem, xs_in.at(i))
                        dve.wait_ge(gelu_done.sem, gelu_done.at(i, p))
                        residual_stats(0, p, h, g[:, p % 2], xs, h_done)
                    if 0 <= s - 3 < NPAIR:
                        p = s - 3
                        dve.wait_ge(m_ready.sem, m_ready.at(i, p))
                        dve.wait_ge(x1b_done.sem, x1b_done.at(i, p))
                        residual_stats(1, p, h2, m_bank[:, :].rearrange("p (t d) -> p t d", t=2), x1b, h2_done)
                    for u in NEXT.get(s, ()):
                        if u[0] == "v":
                            continue
                        at, n = NEXT_ORDER.index(u), SPLIT_ORDER.index(u)
                        dve.wait_ge(high_done.sem, high_done.at(i, n))
                        dve.wait_ge(split_done.sem, split_done.at(i, n - 2))
                        dve.scalar_tensor_tensor(rest[:, n % 2, :], next_bank[at % 2][:, :], 1.0 if u[0] else 1.0 / 16,
                                                 parts[:, n % 2, 0, :], ALU.mult, ALU.subtract).then_inc(
                                                     rest_done.sem, 1)
                next_front(SLOTS)

            turns(dve, turn, front)

        @block.gpsimd
        def _(pool):
            pool.sem_inc(split_done.sem, split_done.start)
            pool.memset(neg_half[:, :], -0.5)
            pool.wait_ge(consts.sem, 12 * 16)
            pool.sem_inc(pool_ticks.sem, 1)
            pool.drain()

            def inverse_std(i, which, p):
                c = slice(2 * p, 2 * p + 2)
                pool.wait_ge(mv_done[which].sem, mv_done[which].at(i, p))
                pool.sem_inc(pool_ticks.sem, 1)
                pool.tensor_scalar(var[:, which, c], mv[:, which, c, 1], EPS, None, ALU.add).then_inc(
                    eps_added[which].sem, 1)
                pool.wait_ge(eps_added[which].sem, eps_added[which].at(i, p))
                pool.tensor_tensor(rstd[:, which, c], var[:, which, c], neg_half[:, :], ALU.pow).then_inc(
                    rstd_done[which].sem, 1)

            def turn(i, next_front):
                for s in range(SLOTS):
                    if 0 <= s - 2 < NPAIR:
                        p = s - 2
                        pool.wait_ge(x1_done.sem, x1_done.at(i, p))
                        hp = slice(2 * p, 2 * p + 2)
                        pool.tensor_tensor(x1b[:, hp, :], x1[:, hp, :], bias_b[:], ALU.add).then_inc(x1b_done.sem, 1)
                    if 0 <= s - 1 < NPAIR:
                        inverse_std(i, 0, s - 1)
                    if 0 <= s - 3 < NPAIR:
                        inverse_std(i, 1, s - 3)
                    for u in NEXT.get(s, ()):
                        if u[0] == "v":
                            continue
                        n = SPLIT_ORDER.index(u)
                        pool.wait_ge(rest_done.sem, rest_done.at(i, n))
                        pool.sem_inc(pool_ticks.sem, 1)
                        pool.tensor_copy(parts[:, n % 2, 1, :], rest[:, n % 2, :])
                        pool.drain()
                        pool.tensor_tensor(parts[:, n % 2, 2, :], rest[:, n % 2, :], parts[:, n % 2, 1, :],
                                           ALU.subtract).then_inc(split_done.sem, 1)

            turns(pool, turn, lambda i, s: None)


def causal_attention(nc, x2, split, v_d, ident, above, ramp_q, ramp_k, sel_q, sel_k, m_rows, guard_d, x3):
    H, HD = 16, 16
    HH = H // 2
    G = HH // 2
    PARTS = 3
    PROD = 6 * HD
    SCORE_ROWS = PROD + 4 * PARTS
    ROWS = SCORE_ROWS + PARTS
    VW = 32
    VH = NT * HH * VW
    STEPS = [(g, c, j) for g in range(2) for c in range(2) for j in range(4 * c + 4)]
    NS = len(STEPS)
    MAX_UNITS = [[(hd, t, kc) for hd in range(g * G, g * G + G) for t in range(NT) for kc in range(1 + (t >= 4))]
                 for g in range(2)]
    NM = len(MAX_UNITS[0])
    def ring_uses(more):
        steps, n = [], 0
        for k in range(NS + 2):
            gaps = [[] for _ in range(5)]
            if more:
                for gap in range(MAX_COUNTS[k]):
                    gaps[gap].append(("max", n))
                    n += 1
            if k == 1:
                gaps[0].insert(0, ("guard", 0, 1))
            if k == 14 and more:
                gaps[0].insert(0, ("guard", 1, 0))
            if k >= 2 and STEPS[k - 2][2] == 4 * STEPS[k - 2][1] + 3:
                gaps[2].insert(0, ("out", STEPS[k - 2][0] * 2 + STEPS[k - 2][1]))
            steps.append(gaps)
        return steps

    MAX_COUNTS = [4] * (NS - 2) + [2] * 4
    RING_USES = [ring_uses(more) for more in (False, True)]
    PROLOGUE_ORDER = [("max", n) for n in range(NM + 1)] + [("guard", 1, 0)] + [("max", n) for n in range(NM + 1, 2 * NM)]
    ORDER = [[use for gaps in steps for gap in gaps for use in gap] for steps in RING_USES]
    PROLOGUE_USES, USES = len(PROLOGUE_ORDER), len(ORDER[1])
    assert USES % 3 == 0

    with ExitStack() as ctx:
        def sb(name, shape, dt=F32):
            return ctx.enter_context(nc.sbuf_tensor("b_" + name, shape, dt))

        def sig(name, per, prime=0, unit=1):
            return Signal(ctx, nc, "b_" + name, per, prime, unit)

        eye = sb("eye", [P, P])
        eye_b = sb("eye_b", [P, P], BF16)
        mask_f = sb("mask_f", [P, 2, P])
        mask = sb("mask", [P, 2, P], BF16)
        ramp = {"q": sb("ramp_q", [P, S]), "k": sb("ramp_k", [P, S])}
        sel = {"q": sb("sel_q", [P, PARTS]), "k": sb("sel_k", [P, PARTS])}
        m_all = sb("m_all", [P, H])
        m_part = sb("m_part", [P, PARTS, H], BF16)
        m_rest = sb("m_rest", [P, 2, H])
        m_sel = {"q": sb("m_sel_q", [P, 3, H]), "k": sb("m_sel_k", [P, 3, H])}
        neg_half = sb("neg_half", [P, NT])
        xs = sb("xs", [P, NT, D])
        aug = {k: [sb(f"aug_{k}{i}", [P, HH, S], BF16) for i in range(2)] for k in "qk"}
        v = [sb(f"v{i}", [P, NT, HH, VW]) for i in range(2)]
        cmax = sb("cmax", [P, 2, G, NT, 2])
        guard = sb("guard", [P, 2, G * NT])
        g_full = sb("g_full", [G * NT, 2, P])
        g_rest = sb("g_rest", [G * NT, 2, P])
        g_part = sb("g_part", [G * NT, 2, PARTS, P], BF16)
        pt = sb("pt", [P, 3, G, 512])
        ot = sb("ot", [P, 512])
        rc = sb("rc", [P, 4, G])
        att = sb("att", [P, 2, 4, G, HD])
        h3 = sb("h3", [P, NT, D])
        st = sb("st", [P, NT, 6])
        mv = sb("mv", [P, NT, 2])
        var = sb("var", [P, NT])
        rstd = sb("rstd", [P, NT])
        x3s = sb("x3s", [P, NT, D])
        s_bank = [ctx.enter_context(nc.psum_tensor(f"b_s{i}", [P, 2, 512], F32)) for i in range(2)]
        ring_bank = [ctx.enter_context(nc.psum_tensor(f"b_ring{i}", [P, 512], F32)) for i in range(3)]
        av_bank = ctx.enter_context(nc.psum_tensor("b_av", [P, 512], F32))

        consts = sig("consts", 1, 0, 16)
        const_cast = sig("const_cast", 1)
        rows_set = sig("rows_set", 2)
        xs_in = sig("xs_in", 1, 0, 16)
        aug_in = [[sig(f"aug_in{g}{half}", 12, 0, 16) for half in range(2)] for g in range(2)]
        v_in = sig("v_in", 2, 0, 16)
        ring_ready = sig("ring_ready", 2 * USES)
        ring_read = sig("ring_read", 2 * USES, 3)
        guard_done = sig("guard_done", 2 * 2)
        guard_copied = sig("guard_copied", 2 * 2)
        g_parts_done = sig("g_parts_done", 2 * 2)
        guard_out = sig("guard_out", 2 * 2, 0, 16)
        guard_in = [sig(f"guard_in{g}", 2, 0, 16) for g in range(2)]
        s_ready = sig("s_ready", 2 * NS * 2, 1)
        exp_done = sig("exp_done", 2 * NS * 2, 2)
        av_done = sig("av_done", 2 * NS, 3)
        ot_copied = sig("ot_copied", 2 * 4, 1)
        att_done = sig("att_done", 2 * 4, 1)
        h3_added = sig("h3_added", 2 * 4, 2)
        mv_done = sig("mv_done", 2)
        eps_added = sig("eps_added", 2)
        rstd_done = sig("rstd_done", 2)
        x3_done = sig("x3_done", 2)
        x3_out = sig("x3_out", 1, 1, 16)
        ticks = sig("ticks", 1)
        pool_ticks = sig("pool_ticks", 1)
        block = ctx.enter_context(nc.Block())

        def width(c, j):
            lo = max(512 * c, P * j)
            return lo, 512 * (c + 1) - lo

        def finished(k):
            g, c, j = STEPS[k]
            return g * 2 + c if j == 4 * c + 3 else None

        def turns(eng, half_turn, prologue=None):
            if prologue:
                prologue()
            with eng.Fori(0, N - 1) as i:
                for half in range(2):
                    half_turn(i, half, True)
            half_turn(N - 1, 0, True)
            half_turn(N - 1, 1, False)

        def number(half, more, use):
            return PROLOGUE_USES + half * USES + ORDER[more].index(use)

        @block.sync
        def _(sp):
            for dst, src in ((eye[:], ident), (mask_f[:], above.rearrange("k p n -> p k n")),
                             (ramp["q"][PROD:ROWS, :], ramp_q), (ramp["k"][PROD:ROWS, :], ramp_k),
                             (sel["q"][PROD:ROWS, :], sel_q), (sel["k"][PROD:ROWS, :], sel_k),
                             (m_all[PROD:ROWS, :], m_rows)):
                sp.dma_start(dst, src).then_inc(consts.sem, 16)

            sp.sem_inc(x3_out.sem, x3_out.start)

            def load_operands(h, hb, g):
                for kind in range(2):
                    dst = aug["qk"[kind]][hb]
                    row = 0
                    for a, count in ((0, 3), (1, 2), (2, 1)):
                        for r in range(count):
                            part = a if kind == 0 else r
                            src = split[bass.ds(h * 2 + kind, 1), part, g * G * HD:g * G * HD + G * HD]
                            sp.dma_start(dst[row:row + HD, g * G:g * G + G, :],
                                         src.rearrange("o (h d) s -> d (o h) s", d=HD)).then_inc(aug_in[g][hb].sem, 16)
                            row += HD

            def load_values(i, half):
                sp.dma_start(v[half][:].rearrange("p t h w -> p (t h w)"),
                             v_d[bass.ds(i, 1), :, half * VH:half * VH + VH].rearrange("o p n -> p (o n)")).then_inc(
                    v_in.sem, 16)

            def guard_rows(i, h, g):
                sp.wait_ge(g_parts_done.sem, g_parts_done.at(i, h * 2 + g))
                sp.dma_start(guard_d[g].rearrange("r p n -> p r n"), g_part[:, g]).then_inc(guard_out.sem, 16)
                sp.wait_ge(guard_out.sem, guard_out.at(i, h * 2 + g))
                sp.sem_inc(ticks.sem, 1)
                sp.dma_start(aug["q"][h % 2][SCORE_ROWS:ROWS, g * G:g * G + G, :],
                             guard_d[g].rearrange("r (h t) n -> r h (t n)", h=G)).then_inc(guard_in[g].sem, 16)

            def half_turn(i, half, more):
                if more:
                    sp.wait_ge(s_ready.sem, s_ready.at(i, half * NS * 2 - 1))
                    sp.sem_inc(ticks.sem, 1)
                    load_operands(i * 2 + half + 1, 1 - half, 1)
                guard_rows(i, half, 1)
                if more:
                    sp.wait_ge(av_done.sem, av_done.at(i, half * NS - 1))
                    sp.sem_inc(ticks.sem, 1)
                    load_values(i + half, 1 - half)
                if not isinstance(i, int):
                    sp.wait_ge(s_ready.sem, s_ready.at(i, half * NS * 2 + NS - 1))
                    sp.sem_inc(ticks.sem, 1)
                    load_operands(i * 2 + half + 2, half, 0)
                if more:
                    guard_rows(i, half + 1, 0)
                if half == 1:
                    sp.wait_ge(x3_done.sem, x3_done.at(i, 1))
                    sp.sem_inc(ticks.sem, 1)
                    sp.dma_start(x3[bass.ds(i, 1)].rearrange("o (t p) d -> p (o t) d", p=P), x3s[:]).then_inc(
                        x3_out.sem, 16)

            def prologue():
                load_operands(0, 0, 0)
                load_operands(0, 0, 1)
                load_values(0, 0)
                load_operands(1, 1, 0)
                guard_rows(0, 0, 0)

            turns(sp, half_turn, prologue)
            sp.wait_ge(x3_out.sem, x3_out.at(N - 1))

        @block.tensor
        def _(pe):
            pe.wait_ge(consts.sem, consts.at(0, 6))
            pe.wait_ge(const_cast.sem, const_cast.at(0))
            pe.wait_ge(rows_set.sem, rows_set.at(0))
            pe.sem_inc(av_done.sem, av_done.start)
            pe.sem_inc(s_ready.sem, s_ready.start)

            def row_max(i, at, hb, n):
                g, u = n // NM, n % NM
                q, k = aug["q"][hb], aug["k"][hb]
                hd, t, kc = MAX_UNITS[g][u]
                n_keys = min(512, P * (t + 1) - 512 * kc)
                diagonal = n_keys == P * (t + 1) - 512 * kc
                bank = ring_bank[at % 3]
                pe.wait_ge(ring_read.sem, ring_read.at(i, at - 3))
                mm = pe.matmul(bank[:, 0:n_keys], q[0:SCORE_ROWS, hd, t * P:t * P + P],
                               k[0:SCORE_ROWS, hd, 512 * kc:512 * kc + n_keys], start=True, stop=not diagonal)
                if diagonal:
                    mm = pe.matmul(bank[:, n_keys - P:n_keys], eye_b[:, :], mask[:, 0, :], start=False, stop=True)
                mm.then_inc(ring_ready.sem, 1)

            def turn_guard(i, at, h, g):
                pe.wait_ge(guard_done.sem, guard_done.at(i, h * 2 + g))
                pe.wait_ge(ring_read.sem, ring_read.at(i, at - 3))
                pe.transpose(ring_bank[at % 3][0:G * NT, 0:P], guard[:, g, :], eye[:, :]).then_inc(ring_ready.sem, 1)

            def turn_output(i, at, half, o):
                pe.wait_ge(ot_copied.sem, ot_copied.at(i, half * 4 + o))
                pe.wait_ge(ring_read.sem, ring_read.at(i, at - 3))
                for t in range(4):
                    mm = pe.transpose(ring_bank[at % 3][:, t * P:t * P + P], ot[:, t * P:t * P + P], eye[:, :])
                mm.then_inc(ring_ready.sem, 1)

            def scores(i, half, k, head):
                g, c, j = STEPS[k]
                lo, n = width(c, j)
                pair, hh = head // 2, head % 2
                hd = g * G + head
                diagonal = j >= 4 * c
                if k % 12 == 0 and head == 0:
                    pe.wait_ge(guard_in[g].sem, guard_in[g].at(i, half))
                bank = s_bank[pair]
                if hh == 0:
                    pe.wait_ge(exp_done.sem, exp_done.at(i, (half * NS + k - 1) * 2 + pair))
                mm = pe.matmul(bank[:, hh, 0:n], aug["k"][half][0:ROWS, hd, j * P:j * P + P],
                               aug["q"][half][0:ROWS, hd, lo:lo + n], start=True, stop=not diagonal)
                if diagonal:
                    mm = pe.matmul(bank[:, hh, 0:P], eye_b[:, :], mask[:, 1, :], start=False, stop=True)
                if hh == 1:
                    mm.then_inc(s_ready.sem, 1)

            def values(i, half, k):
                g, c, j = STEPS[k]
                lo, n = width(c, j)
                if k == 0:
                    pe.wait_ge(v_in.sem, v_in.at(i, half))
                pe.wait_ge(exp_done.sem, exp_done.at(i, (half * NS + k) * 2 + 1))
                if j == 0:
                    pe.wait_ge(ot_copied.sem, ot_copied.at(i, half * 4 + g * 2 + c - 1))
                for hh in range(G):
                    mm = pe.matmul(av_bank[hh * VW:hh * VW + VW, lo - 512 * c:512], v[half][:, j, g * G + hh, :],
                                   pt[:, k % 3, hh, 0:n], start=(j == 0), stop=(j == 4 * c + 3))
                mm.then_inc(av_done.sem, 1)

            def half_turn(i, half, more):
                for k in range(NS + 2):
                    for gap, uses in enumerate(RING_USES[more][k]):
                        if gap < 4 and k < NS:
                            scores(i, half, k, gap)
                        for use in uses:
                            at = number(half, more, use)
                            if use[0] == "max":
                                h, g = half + 1, use[1] // NM
                                if use[1] % NM == 0:
                                    pe.wait_ge(aug_in[g][h % 2].sem, aug_in[g][h % 2].at(i, h // 2 * 12 + 11))
                                row_max(i, at, h % 2, use[1])
                            elif use[0] == "guard":
                                turn_guard(i, at, half + use[1], use[2])
                            else:
                                turn_output(i, at, half, use[1])
                    if 1 <= k <= NS:
                        values(i, half, k - 1)

            def prologue():
                for at, use in enumerate(PROLOGUE_ORDER):
                    if use[0] == "guard":
                        turn_guard(0, at, 0, 0)
                    else:
                        if use[1] % NM == 0:
                            g = use[1] // NM
                            pe.wait_ge(aug_in[g][0].sem, aug_in[g][0].at(0, 11))
                        row_max(0, at, 0, use[1])
                pe.wait_ge(rows_set.sem, rows_set.at(0, 1))

            turns(pe, half_turn, prologue)

        @block.scalar
        def _(act):
            act.sem_inc(exp_done.sem, exp_done.start)
            act.sem_inc(ot_copied.sem, ot_copied.start)

            def half_turn(i, half, more):
                for k in range(NS + 1):
                    if k < NS:
                        g, c, j = STEPS[k]
                        lo, n = width(c, j)
                        for pair in range(2):
                            act.wait_ge(s_ready.sem, s_ready.at(i, (half * NS + k) * 2 + pair))
                            if pair == 0:
                                act.wait_ge(av_done.sem, av_done.at(i, half * NS + k - 3))
                            act.activation(pt[:, k % 3, 2 * pair:2 * pair + 2, 0:n], s_bank[pair][:, :, 0:n],
                                           ACT.Exp).then_inc(exp_done.sem, 1)
                    if k >= 1 and finished(k - 1) is not None:
                        o = finished(k - 1)
                        act.wait_ge(av_done.sem, av_done.at(i, half * NS + k - 1))
                        act.wait_ge(att_done.sem, att_done.at(i, half * 4 + o - 1))
                        act.activation(ot[:, :], av_bank[:, :], ACT.Copy).then_inc(ot_copied.sem, 1)

            turns(act, half_turn)

        @block.vector
        def _(dve):
            dve.sem_inc(ring_read.sem, ring_read.start)
            dve.sem_inc(att_done.sem, att_done.start)
            dve.wait_ge(consts.sem, consts.at(0, 6))
            dve.memset(cmax[:], -3e38)
            dve.tensor_copy(eye_b[:], eye[:])
            dve.tensor_copy(mask[:], mask_f[:]).then_inc(const_cast.sem, 1)
            r = slice(PROD, ROWS)
            dve.tensor_copy(m_part[r, 0, :], m_all[r, :])
            dve.drain()
            dve.tensor_tensor(m_rest[r, 0, :], m_all[r, :], m_part[r, 0, :], ALU.subtract)
            dve.drain()
            dve.tensor_copy(m_part[r, 1, :], m_rest[r, 0, :])
            dve.drain()
            dve.tensor_tensor(m_part[r, 2, :], m_rest[r, 0, :], m_part[r, 1, :], ALU.subtract)
            dve.drain()
            for kind in "qk":
                ms = m_sel[kind]
                dve.tensor_scalar(ms[r, 0, :], m_part[r, 0, :], sel[kind][r, 0:1], None, ALU.mult)
                for p in (1, 2):
                    dve.drain()
                    dve.scalar_tensor_tensor(ms[r, p, :], m_part[r, p, :], sel[kind][r, p:p + 1], ms[r, p - 1, :],
                                             ALU.mult, ALU.add)
                dve.drain()
            for half in range(2):
                for kind in "qk":
                    for hd in range(HH):
                        ins = dve.tensor_scalar(aug[kind][half][r, hd, :], ramp[kind][r, :],
                                                m_sel[kind][r, 2, half * HH + hd:half * HH + hd + 1], None, ALU.add)
                ins.then_inc(rows_set.sem, 1)

            def row_max(i, at, n):
                g, u = n // NM, n % NM
                hd, t, kc = MAX_UNITS[g][u]
                n_keys = min(512, P * (t + 1) - 512 * kc)
                dve.wait_ge(ring_ready.sem, ring_ready.at(i, at))
                dve.tensor_reduce(cmax[:, g, hd % G, t, kc:kc + 1], ring_bank[at % 3][:, 0:n_keys], AX.X,
                                  ALU.max).then_inc(ring_read.sem, 1)
                if u == NM - 1:
                    dve.drain()
                    flat = cmax[:, g].rearrange("p h t k -> p (h t) k")
                    dve.tensor_tensor(guard[:, g, :], flat[:, :, 0], flat[:, :, 1], ALU.max).then_inc(
                        guard_done.sem, 1)

            def copy_guard(i, at, h, g):
                dve.wait_ge(ring_ready.sem, ring_ready.at(i, at))
                dve.tensor_copy(g_full[:, g, :], ring_bank[at % 3][0:G * NT, 0:P]).then_inc(ring_read.sem, 1)
                dve.drain()
                dve.sem_inc(guard_copied.sem, 1)

            def output(i, at, half, o):
                dve.wait_ge(ring_ready.sem, ring_ready.at(i, at))
                turned = ring_bank[at % 3][:, :].rearrange("p (t h d) -> p t h d", t=4, h=G)
                dve.reciprocal(rc[:, :, :], turned[:, :, :, HD])
                dve.drain()
                dve.wait_ge(h3_added.sem, h3_added.at(i, half * 4 + o - 2))
                dve.tensor_tensor(att[:, o % 2], turned[:, :, :, 0:HD],
                                  rc[:, :, :].unsqueeze(3).broadcast_to([P, 4, G, HD]), ALU.mult).then_inc(
                    ring_read.sem, 1)
                dve.drain()
                dve.sem_inc(att_done.sem, 1)

            def statistics(i, c):
                dve.wait_ge(h3_added.sem, h3_added.at(i, 6 + c))
                for t in range(4 * c, 4 * c + 4):
                    dve.bn_stats(st[:, t, :], h3[:, t, :])
                dve.drain()
                for t in range(4 * c, 4 * c + 4):
                    ins = dve.bn_aggr(mv[:, t, :], st[:, t, :])
                ins.then_inc(mv_done.sem, 1)

            def half_turn(i, half, more):
                for k in range(NS + 2):
                    for uses in RING_USES[more][k]:
                        for use in uses:
                            at = number(half, more, use)
                            if use[0] == "max":
                                row_max(i, at, use[1])
                            elif use[0] == "guard":
                                copy_guard(i, at, half + use[1], use[2])
                            else:
                                output(i, at, half, use[1])
                    if half == 1 and k in (19, NS + 1):
                        statistics(i, int(k == NS + 1))

            def prologue():
                for at, use in enumerate(PROLOGUE_ORDER):
                    if use[0] == "guard":
                        copy_guard(0, at, 0, 0)
                    else:
                        row_max(0, at, use[1])

            turns(dve, half_turn, prologue)

        @block.gpsimd
        def _(pool):
            pool.sem_inc(h3_added.sem, h3_added.start)
            pool.memset(neg_half[:, :], -0.5)
            pool.drain()
            pool.dma_start(xs[:], x2[0].rearrange("(t p) d -> p t d", p=P)).then_inc(xs_in.sem, 16)

            def split_guard(i, h, g):
                full, rest, part = g_full[:, g, :], g_rest[:, g, :], g_part[:, g]
                pool.wait_ge(guard_copied.sem, guard_copied.at(i, h * 2 + g))
                pool.sem_inc(pool_ticks.sem, 1)
                pool.tensor_copy(part[:, 0, :], full)
                pool.drain()
                pool.tensor_tensor(rest, full, part[:, 0, :], ALU.subtract)
                pool.drain()
                pool.tensor_copy(part[:, 1, :], rest)
                pool.drain()
                pool.tensor_tensor(part[:, 2, :], rest, part[:, 1, :], ALU.subtract).then_inc(g_parts_done.sem, 1)

            def add_residual(i, half, o):
                g, c = o // 2, o % 2
                if half == 0 and o == 0:
                    pool.wait_ge(xs_in.sem, xs_in.at(i))
                pool.wait_ge(att_done.sem, att_done.at(i, half * 4 + o))
                pool.sem_inc(pool_ticks.sem, 1)
                d0 = half * P + g * G * HD
                tiles = slice(4 * c, 4 * c + 4)
                pool.tensor_tensor(h3[:, tiles, d0:d0 + G * HD], xs[:, tiles, d0:d0 + G * HD],
                                   att[:, o % 2].rearrange("p t h d -> p t (h d)"), ALU.add).then_inc(h3_added.sem, 1)

            def normalise(i, c):
                tiles = slice(4 * c, 4 * c + 4)
                if c == 0:
                    pool.wait_ge(x3_out.sem, x3_out.at(i, -1))
                pool.wait_ge(mv_done.sem, mv_done.at(i, c))
                pool.sem_inc(pool_ticks.sem, 1)
                pool.tensor_scalar(var[:, tiles], mv[:, tiles, 1], EPS, None, ALU.add).then_inc(eps_added.sem, 1)
                pool.wait_ge(eps_added.sem, eps_added.at(i, c))
                pool.tensor_tensor(rstd[:, tiles], var[:, tiles], neg_half[:, tiles], ALU.pow).then_inc(
                    rstd_done.sem, 1)
                pool.wait_ge(rstd_done.sem, rstd_done.at(i, c))
                pool.sem_inc(pool_ticks.sem, 1)
                for t in range(4 * c, 4 * c + 4):
                    ins = pool.tensor_scalar(x3s[:, t, :], h3[:, t, :], mv[:, t, 0:1], rstd[:, t:t + 1],
                                             ALU.subtract, ALU.mult)
                ins.then_inc(x3_done.sem, 1)

            def turn(i, more):
                for half in range(2):
                    split_guard(i, half, 1)
                    add_residual(i, half, 0)
                    add_residual(i, half, 1)
                    if more or half == 0:
                        split_guard(i, half + 1, 0)
                    add_residual(i, half, 2)
                    if half == 1:
                        normalise(i, 0)
                    add_residual(i, half, 3)
                if more:
                    pool.wait_ge(h3_added.sem, h3_added.at(i, 7))
                    pool.sem_inc(pool_ticks.sem, 1)
                    pool.dma_start(xs[:], x2[bass.ds(i + 1, 1)].rearrange("o (t p) d -> p (o t) d", p=P)).then_inc(
                        xs_in.sem, 16)
                normalise(i, 1)

            split_guard(0, 0, 0)
            with pool.Fori(0, N - 1) as i:
                turn(i, True)
            turn(N - 1, False)


def position_attention(nc, x3, ln1_w, ln1_b, ln2_w, ln2_b, w_qkv, w_proj, w_router, ident, resid, xn, logits):
    KV, R, HD = 8, 2, 16
    GW = (R + 2) * HD
    E8 = 8
    NP2 = N // 2
    with ExitStack() as ctx:
        def sb(name, shape, dt=F32):
            return ctx.enter_context(nc.sbuf_tensor("c_" + name, shape, dt))

        def sig(name, per, prime=0, unit=1):
            return Signal(ctx, nc, "c_" + name, per, prime, unit)

        wq = sb("wq", [P, DC, KV * GW])
        wp = sb("wp", [P, DC, D])
        wr = sb("wr", [P, DC, E8])
        eye = sb("eye", [P, P])
        ln = [sb(f"ln{k}", [P, 2, D]) for k in range(4)]
        neg_half = sb("neg_half", [P, N])
        x = sb("x", [P, N, D])
        st = sb("st", [P, N, 6])
        mv = sb("mv", [P, 2, N, 2])
        var = sb("var", [P, 2, N])
        rstd = sb("rstd", [P, 2, N])
        n1 = sb("n1", [P, N, D])
        h1 = sb("h1", [P, N, D])
        ht = sb("ht", [P, 2, DC, 2 * P])
        qkv = sb("qkv", [P, N, KV * GW])
        prod = sb("prod", [P, 2, R, N, KV, HD])
        sc = sb("sc", [P, N * R, N, KV])
        mx = sb("mx", [P, N * R, KV])
        sh = sb("sh", [P, N * R, N, KV])
        pe_ = sb("pe", [P, N * R, N, KV])
        sm = sb("sm", [P, N * R, KV])
        rs = sb("rs", [P, N * R, KV])
        pn = sb("pn", [P, N * R, N, KV])
        ao = sb("ao", [P, N, KV, R, HD])
        aot = sb("aot", [P, 2, DC, 2 * P])
        ha = sb("ha", [P, N, D])
        rr = sb("rr", [P, N, D])
        n2 = sb("n2", [P, N, D])
        n2w = sb("n2w", [P, N, D])
        h2 = sb("h2", [P, N, D])
        n1w = sb("n1w", [P, N, D])
        xt = sb("xt", [P, 2, DC, 2 * P])
        lg = sb("lg", [P, N, E8])

        def bank(name):
            return ctx.enter_context(nc.psum_tensor("c_" + name, [P, 512], F32))

        t1_bank, p_bank, t2_bank, t3_bank, l_bank = (bank(k) for k in ("t1", "p", "t2", "t3", "l"))
        q_bank = [bank(f"q{k}") for k in range(2)]

        consts = sig("consts", 1, 0, 16)
        x_in = sig("x_in", 1, 0, 16)
        mv_done = [sig(f"mv_done{k}", 1) for k in range(2)]
        eps_added = [sig(f"eps_added{k}", 1) for k in range(2)]
        rstd_done = [sig(f"rstd_done{k}", 1) for k in range(2)]
        n1_done = sig("n1_done", NP2)
        h1_done = sig("h1_done", NP2)
        t1_ready = sig("t1_ready", NP2)
        t1_copied = sig("t1_copied", NP2, 1)
        q_ready = sig("q_ready", N, 3)
        q_copied = sig("q_copied", N, 2)
        prod_ready = sig("prod_ready", 2 * N)
        prod_read = sig("prod_read", 2 * N, 2)
        sh_done = sig("sh_done", 1)
        exp_done = sig("exp_done", 1)
        pn_done = sig("pn_done", 1)
        t2_ready = sig("t2_ready", NP2)
        t2_copied = sig("t2_copied", NP2, 1)
        p_ready = sig("p_ready", NP2, 2)
        p_read = sig("p_read", NP2, 1)
        rr_done = sig("rr_done", 1)
        n2_done = sig("n2_done", NP2)
        h2_done = sig("h2_done", NP2)
        t3_ready = sig("t3_ready", NP2)
        t3_copied = sig("t3_copied", NP2, 1)
        l_ready = sig("l_ready", NP2, 2)
        l_copied = sig("l_copied", 1, 1)
        rr_out = sig("rr_out", 1, 1, 16)
        xn_out = sig("xn_out", 1, 1, 16)
        lg_out = sig("lg_out", 1, 1, 16)
        ticks = sig("ticks", 1)
        pool_ticks = sig("pool_ticks", 1)
        block = ctx.enter_context(nc.Block())

        def q_of(s, r):
            return qkv[:, s, :].rearrange("p (g w) -> p g w", g=KV)[:, :, r * HD:r * HD + HD]

        def kv_of(s, which):
            at = (R + which) * HD
            return qkv[:, 0:s + 1, :].rearrange("p t (g w) -> p t g w", g=KV)[:, :, :, at:at + HD]

        def score_products(eng, s, r):
            n = s + 1
            return eng.tensor_tensor(prod[:, s % 2, r, 0:n], q_of(s, r).unsqueeze(1).broadcast_to([P, n, KV, HD]),
                                     kv_of(s, 0), ALU.mult)

        def value_products(eng, s, r):
            n = s + 1
            return eng.tensor_tensor(prod[:, s % 2, r, 0:n],
                                     pn[:, s * R + r, 0:n, :].unsqueeze(3).broadcast_to([P, n, KV, HD]),
                                     kv_of(s, 1), ALU.mult)

        @block.sync
        def _(sp):
            for dst, src in ((wq[:], w_qkv.rearrange("(c p) n -> p c n", p=P)),
                             (wp[:], w_proj.rearrange("(c p) n -> p c n", p=P)),
                             (wr[:], w_router.rearrange("(c p) n -> p c n", p=P)), (eye[:], ident),
                             (ln[0][:], ln1_w), (ln[1][:], ln1_b), (ln[2][:], ln2_w), (ln[3][:], ln2_b)):
                sp.dma_start(dst, src).then_inc(consts.sem, 16)
            for s in (rr_out, xn_out, lg_out):
                sp.sem_inc(s.sem, s.start)
            sp.dma_start(x[:], x3[:, 0:P, :].rearrange("s p d -> p s d")).then_inc(x_in.sem, 16)

            def turn(i, last):
                sp.wait_ge(rr_done.sem, rr_done.at(i))
                sp.sem_inc(ticks.sem, 1)
                if not last:
                    sp.dma_start(x[:], x3[:, bass.ds((i + 1) * P, P), :].rearrange("s p d -> p s d")).then_inc(
                        x_in.sem, 16)
                sp.dma_start(resid[:, bass.ds(i * P, P), :].rearrange("s p d -> p s d"), rr[:]).then_inc(rr_out.sem, 16)
                sp.wait_ge(h2_done.sem, h2_done.at(i, NP2 - 1))
                sp.sem_inc(ticks.sem, 1)
                sp.dma_start(xn[:, bass.ds(i * P, P), :].rearrange("s p d -> p s d"), h2[:]).then_inc(xn_out.sem, 16)
                sp.wait_ge(l_copied.sem, l_copied.at(i))
                sp.sem_inc(ticks.sem, 1)
                sp.dma_start(logits[bass.ds(i, 1)].rearrange("o p s e -> p o (s e)"),
                             lg[:].rearrange("p (o s) e -> p o (s e)", o=1)).then_inc(lg_out.sem, 16)

            with sp.Fori(0, NT - 1) as i:
                turn(i, False)
            turn(NT - 1, True)
            for s in (rr_out, xn_out, lg_out):
                sp.wait_ge(s.sem, s.at(NT - 1))

        @block.tensor
        def _(pe):
            pe.wait_ge(consts.sem, consts.at(0, 7))
            pe.sem_inc(q_ready.sem, q_ready.start)
            pe.sem_inc(p_ready.sem, p_ready.start)
            pe.sem_inc(l_ready.sem, l_ready.start)
            with pe.Fori(0, NT) as i:
                def turn_pair(bank_, src, p, ready):
                    for k in range(DC):
                        for s in (2 * p, 2 * p + 1):
                            c0 = k * 256 + (s % 2) * P
                            mm = pe.transpose(bank_[:, c0:c0 + P], src(s, k), eye[:, :])
                    mm.then_inc(ready.sem, 1)

                for p in range(NP2):
                    pe.wait_ge(h1_done.sem, h1_done.at(i, p))
                    pe.wait_ge(t1_copied.sem, t1_copied.at(i, p - 1))
                    turn_pair(t1_bank, lambda s, k: h1[:, s, k * P:k * P + P], p, t1_ready)
                    pe.wait_ge(t1_copied.sem, t1_copied.at(i, p))
                    for s in (2 * p, 2 * p + 1):
                        pe.wait_ge(q_copied.sem, q_copied.at(i, s - 2))
                        for k in range(DC):
                            mm = pe.matmul(q_bank[s % 2][:, :], ht[:, p % 2, k, (s % 2) * P:(s % 2) * P + P],
                                           wq[:, k, :], start=(k == 0), stop=(k == DC - 1))
                        mm.then_inc(q_ready.sem, 1)
                pe.wait_ge(prod_read.sem, prod_read.at(i, 2 * N - 1))
                for p in range(NP2):
                    pe.wait_ge(t2_copied.sem, t2_copied.at(i, p - 1))
                    turn_pair(t2_bank, lambda s, k: ao[:, s].rearrange("p g r d -> p (g r d)")[:, k * P:k * P + P], p,
                              t2_ready)
                    pe.wait_ge(t2_copied.sem, t2_copied.at(i, p))
                    pe.wait_ge(p_read.sem, p_read.at(i, p - 1))
                    for s in (2 * p, 2 * p + 1):
                        for k in range(DC):
                            mm = pe.matmul(p_bank[:, (s % 2) * D:(s % 2) * D + D],
                                           aot[:, p % 2, k, (s % 2) * P:(s % 2) * P + P], wp[:, k, :],
                                           start=(k == 0), stop=(k == DC - 1))
                    mm.then_inc(p_ready.sem, 1)
                for p in range(NP2):
                    pe.wait_ge(h2_done.sem, h2_done.at(i, p))
                    pe.wait_ge(t3_copied.sem, t3_copied.at(i, p - 1))
                    turn_pair(t3_bank, lambda s, k: h2[:, s, k * P:k * P + P], p, t3_ready)
                    pe.wait_ge(t3_copied.sem, t3_copied.at(i, p))
                    if p == 0:
                        pe.wait_ge(l_copied.sem, l_copied.at(i, -1))
                    for s in (2 * p, 2 * p + 1):
                        for k in range(DC):
                            mm = pe.matmul(l_bank[:, s * E8:s * E8 + E8], xt[:, p % 2, k, (s % 2) * P:(s % 2) * P + P],
                                           wr[:, k, :], start=(k == 0), stop=(k == DC - 1))
                    mm.then_inc(l_ready.sem, 1)

        @block.scalar
        def _(act):
            for s in (t1_copied, t2_copied, t3_copied, q_copied):
                act.sem_inc(s.sem, s.start)
            with act.Fori(0, NT) as i:
                for p in range(NP2):
                    act.wait_ge(t1_ready.sem, t1_ready.at(i, p))
                    act.wait_ge(q_ready.sem, q_ready.at(i, 2 * p - 3))
                    act.activation(ht[:, p % 2].rearrange("p c t -> p (c t)"), t1_bank[:, :], ACT.Copy).then_inc(
                        t1_copied.sem, 1)
                    for s in (2 * p, 2 * p + 1):
                        act.wait_ge(q_ready.sem, q_ready.at(i, s))
                        act.activation(qkv[:, s, :], q_bank[s % 2][:, :], ACT.Copy).then_inc(q_copied.sem, 1)
                act.wait_ge(sh_done.sem, sh_done.at(i))
                act.activation(pe_[:], sh[:], ACT.Exp, scale=0.25).then_inc(exp_done.sem, 1)
                for p in range(NP2):
                    act.wait_ge(t2_ready.sem, t2_ready.at(i, p))
                    act.wait_ge(p_ready.sem, p_ready.at(i, p - 2))
                    act.activation(aot[:, p % 2].rearrange("p c t -> p (c t)"), t2_bank[:, :], ACT.Copy).then_inc(
                        t2_copied.sem, 1)
                for p in range(NP2):
                    act.wait_ge(t3_ready.sem, t3_ready.at(i, p))
                    act.wait_ge(l_ready.sem, l_ready.at(i, p - 2))
                    act.activation(xt[:, p % 2].rearrange("p c t -> p (c t)"), t3_bank[:, :], ACT.Copy).then_inc(
                        t3_copied.sem, 1)

        @block.vector
        def _(dve):
            dve.sem_inc(l_copied.sem, l_copied.start)
            dve.sem_inc(p_read.sem, p_read.start)
            dve.sem_inc(prod_read.sem, prod_read.start)
            dve.memset(sc[:], -BIG)
            dve.drain()
            with dve.Fori(0, NT) as i:
                def moments(which, src):
                    for s in range(N):
                        dve.bn_stats(st[:, s, :], src[:, s, :])
                    dve.drain()
                    for s in range(N):
                        ins = dve.bn_aggr(mv[:, which, s, :], st[:, s, :])
                    ins.then_inc(mv_done[which].sem, 1)
                    dve.wait_ge(rstd_done[which].sem, rstd_done[which].at(i))

                def normalise(which, dst, src, done):
                    for s in range(N):
                        ins = dve.tensor_scalar(dst[:, s, :], src[:, s, :], mv[:, which, s, 0:1],
                                                rstd[:, which, s:s + 1], ALU.subtract, ALU.mult)
                        if s % 2:
                            ins.then_inc(done.sem, 1)

                dve.wait_ge(x_in.sem, x_in.at(i))
                moments(0, x)
                normalise(0, n1, x, n1_done)
                dve.wait_ge(q_copied.sem, q_copied.at(i, N - 1))
                for s in range(N):
                    n = s + 1
                    dve.wait_ge(prod_ready.sem, prod_ready.at(i, s))
                    dve.tensor_reduce(sc[:, s * R:s * R + R, 0:n, :].rearrange("p r t g -> p r (t g)"),
                                      prod[:, s % 2, :, 0:n].rearrange("p r t g d -> p r (t g) d"), AX.X,
                                      ALU.add).then_inc(prod_read.sem, 1)
                dve.drain()
                dve.tensor_reduce(mx[:], sc[:].rearrange("p a t g -> p a g t"), AX.X, ALU.max)
                dve.drain()
                dve.tensor_tensor(sh[:], sc[:], mx[:].unsqueeze(2).broadcast_to([P, N * R, N, KV]),
                                  ALU.subtract).then_inc(sh_done.sem, 1)
                dve.wait_ge(exp_done.sem, exp_done.at(i))
                dve.tensor_reduce(sm[:], pe_[:].rearrange("p a t g -> p a g t"), AX.X, ALU.add)
                dve.drain()
                dve.reciprocal(rs[:], sm[:])
                dve.drain()
                dve.tensor_tensor(pn[:], pe_[:], rs[:].unsqueeze(2).broadcast_to([P, N * R, N, KV]),
                                  ALU.mult).then_inc(pn_done.sem, 1)
                for s in range(N):
                    dve.wait_ge(prod_ready.sem, prod_ready.at(i, N + s))
                    for r in range(R):
                        ins = dve.tensor_reduce(ao[:, s, :, r, :],
                                                prod[:, s % 2, r, 0:s + 1].rearrange("p t g d -> p g d t"), AX.X,
                                                ALU.add)
                    ins.then_inc(prod_read.sem, 1)
                for p in range(NP2):
                    hp = slice(2 * p, 2 * p + 2)
                    dve.wait_ge(p_ready.sem, p_ready.at(i, p))
                    dve.tensor_tensor(ha[:, hp, :], p_bank[:, :].rearrange("p (t d) -> p t d", t=2), x[:, hp, :],
                                      ALU.add).then_inc(p_read.sem, 1)
                dve.drain()
                dve.wait_ge(rr_out.sem, rr_out.at(i, -1))
                dve.tensor_tensor(rr[:], ha[:], x[:], ALU.add).then_inc(rr_done.sem, 1)
                dve.drain()
                moments(1, ha)
                normalise(1, n2, ha, n2_done)
                dve.wait_ge(l_ready.sem, l_ready.at(i, NP2 - 1))
                dve.wait_ge(lg_out.sem, lg_out.at(i, -1))
                dve.tensor_copy(lg[:].rearrange("p s e -> p (s e)"), l_bank[:, 0:N * E8]).then_inc(l_copied.sem, 1)

        @block.gpsimd
        def _(pool):
            pool.memset(neg_half[:, :], -0.5)
            pool.drain()
            pool.wait_ge(consts.sem, consts.at(0, 7))
            pool.sem_inc(pool_ticks.sem, 1)
            with pool.Fori(0, NT) as i:
                def inverse_std(which):
                    pool.wait_ge(mv_done[which].sem, mv_done[which].at(i))
                    pool.sem_inc(pool_ticks.sem, 1)
                    pool.tensor_scalar(var[:, which, :], mv[:, which, :, 1], EPS, None, ALU.add).then_inc(
                        eps_added[which].sem, 1)
                    pool.wait_ge(eps_added[which].sem, eps_added[which].at(i))
                    pool.tensor_tensor(rstd[:, which, :], var[:, which, :], neg_half[:, :], ALU.pow).then_inc(
                        rstd_done[which].sem, 1)

                def affine(dst, mid, src, k, ready, done):
                    for p in range(NP2):
                        hp = slice(2 * p, 2 * p + 2)
                        pool.wait_ge(ready.sem, ready.at(i, p))
                        pool.tensor_tensor(mid[:, hp, :], src[:, hp, :], ln[k][:], ALU.mult)
                        pool.drain()
                        pool.tensor_tensor(dst[:, hp, :], mid[:, hp, :], ln[k + 1][:], ALU.add).then_inc(done.sem, 1)

                inverse_std(0)
                affine(h1, n1w, n1, 0, n1_done, h1_done)
                pool.wait_ge(q_copied.sem, q_copied.at(i, N - 1))
                for s in range(2 * N):
                    if s == N:
                        pool.wait_ge(pn_done.sem, pn_done.at(i))
                    pool.wait_ge(prod_read.sem, prod_read.at(i, s - 2))
                    products = score_products if s < N else value_products
                    for r in range(R):
                        ins = products(pool, s % N, r)
                    ins.then_inc(prod_ready.sem, 1)
                inverse_std(1)
                pool.wait_ge(xn_out.sem, xn_out.at(i, -1))
                affine(h2, n2w, n2, 2, n2_done, h2_done)


EXPERTS = 8
FFN = 1024
CAP = -(-(T * 2 * 5) // (EXPERTS * 4))
SLOTS_ALL = EXPERTS * CAP


def route(nc, logits, before, iota, token_ids, gather_d, prob_d, scatter_d, slot_token):
    NTILE = T // P
    E8 = EXPERTS
    with ExitStack() as ctx:
        def sb(name, shape, dt=F32):
            return ctx.enter_context(nc.sbuf_tensor("r_" + name, shape, dt))

        def sem(name):
            return ctx.enter_context(nc.semaphore("r_" + name))

        lg = sb("lg", [P, NTILE, E8])
        tri = sb("tri", [P, P])
        ones = sb("ones", [P, P])
        io = sb("io", [P, NTILE, E8])
        oh = [sb(f"oh{k}", [P, NTILE, E8]) for k in range(2)]
        lg2 = sb("lg2", [P, NTILE, E8])
        eq = [sb(f"eq{k}", [P, NTILE, E8]) for k in range(2)]
        at = [sb(f"at{k}", [P, NTILE, E8]) for k in range(2)]
        best = [sb(f"best{k}", [P, NTILE]) for k in range(2)]
        first = [sb(f"first{k}", [P, NTILE]) for k in range(2)]
        gap = sb("gap", [P, NTILE])
        e2 = sb("e2", [P, NTILE])
        total = sb("total", [P, NTILE])
        prob = sb("prob", [P, 2, NTILE])
        chosen = sb("chosen", [P, NTILE, E8])
        scan = [sb(f"scan{k}", [P, NTILE, E8]) for k in range(7)]
        base = sb("base", [P, NTILE, E8])
        place = sb("place", [P, NTILE, E8])
        keep = sb("keep", [P, NTILE, E8])
        slot = sb("slot", [P, NTILE, E8])
        pick = [sb(f"pick{k}", [P, NTILE, E8]) for k in range(4)]
        slot_k = sb("slot_k", [P, 2, NTILE])
        keep_k = sb("keep_k", [P, 2, NTILE])
        weight = sb("weight", [P, 2, NTILE])
        gat_f = sb("gat_f", [P, 2, NTILE])
        out_f = sb("out_f", [P, 2, NTILE])
        sca_f = sb("sca_f", [P, 2, NTILE])
        gat = sb("gat", [P, 2, NTILE], U32)
        sca = sb("sca", [P, 2, NTILE], U32)
        tok_f = sb("tok_f", [P, NTILE])
        tok = sb("tok", [P, NTILE], U32)
        zero = sb("zero", [P, SLOTS_ALL // P], U32)
        count_bank = [ctx.enter_context(nc.psum_tensor(f"r_count{k}", [P, 512], F32)) for k in range(2)]
        loaded, ones_set, chosen_done, counted = (sem(k) for k in ("loaded", "ones_set", "chosen_done", "counted"))
        gap_done, exp_done, results, stored, zeroed, zero_set = (
            sem(k) for k in ("gap_done", "exp_done", "results", "stored", "zeroed", "zero_set"))
        block = ctx.enter_context(nc.Block())

        @block.sync
        def _(sp):
            lg_v = lg[:].rearrange("p (s t) e -> p s t e", s=N)
            for t in range(NT):
                sp.dma_start(lg_v[:, :, t, :], logits[t]).then_inc(loaded, 16)
            sp.dma_start(tri[:], before).then_inc(loaded, 16)
            sp.dma_start(io[:], iota).then_inc(loaded, 16)
            sp.dma_start(tok_f[:], token_ids).then_inc(loaded, 16)
            sp.wait_ge(zero_set, 1)
            sp.dma_start(slot_token.rearrange("(p n) o -> p (n o)", p=P), zero[:]).then_inc(zeroed, 16)
            sp.wait_ge(results, 4)
            sp.dma_start(gather_d, gat[:]).then_inc(stored, 16)
            sp.dma_start(prob_d, weight[:]).then_inc(stored, 16)
            sp.dma_start(scatter_d[:, 0:2, :], sca[:]).then_inc(stored, 16)
            sp.dma_start(scatter_d[:, 2, :], tok[:]).then_inc(stored, 16)
            sp.wait_ge(stored, 4 * 16)
            sp.wait_ge(zeroed, 16)

        @block.tensor
        def _(pe):
            pe.wait_ge(loaded, (NT + 3) * 16)
            pe.wait_ge(ones_set, 1)
            pe.wait_ge(chosen_done, 1)
            flat = chosen[:].rearrange("p t e -> p (t e)")
            pe.matmul(count_bank[0][:, :], tri[:, :], flat, start=True, stop=True)
            pe.matmul(count_bank[1][:, :], ones[:, :], flat, start=True, stop=True).then_inc(counted, 1)

        @block.scalar
        def _(act):
            act.wait_ge(gap_done, 1)
            act.activation(e2[:], gap[:], ACT.Exp).then_inc(exp_done, 1)

        @block.vector
        def _(dve):
            def step(ins):
                dve.drain()
                return ins

            def wide(a):
                return a.unsqueeze(2).broadcast_to([P, NTILE, E8])

            dve.memset(ones[:], 1.0).then_inc(ones_set, 1)
            dve.memset(zero[:], 0).then_inc(zero_set, 1)
            dve.wait_ge(loaded, (NT + 3) * 16)
            src = lg
            for k in range(2):
                step(dve.tensor_reduce(best[k][:], src[:], AX.X, ALU.max))
                step(dve.tensor_tensor(eq[k][:], src[:], wide(best[k][:]), ALU.is_equal))
                step(dve.tensor_tensor(at[k][:], eq[k][:], io[:], ALU.mult))
                step(dve.tensor_reduce(first[k][:], at[k][:], AX.X, ALU.min))
                step(dve.tensor_tensor(oh[k][:], io[:], wide(first[k][:]), ALU.is_equal))
                if k == 0:
                    step(dve.scalar_tensor_tensor(lg2[:], oh[0][:], -1e38, lg[:], ALU.mult, ALU.add))
                    src = lg2
            dve.tensor_tensor(chosen[:], oh[0][:], oh[1][:], ALU.add).then_inc(chosen_done, 1)
            dve.tensor_tensor(gap[:], best[1][:], best[0][:], ALU.subtract).then_inc(gap_done, 1)
            dve.wait_ge(exp_done, 1)
            step(dve.tensor_scalar(total[:], e2[:], 1.0, None, ALU.add))
            step(dve.reciprocal(prob[:, 0, :], total[:]))
            dve.tensor_tensor(prob[:, 1, :], prob[:, 0, :], e2[:], ALU.mult)
            dve.wait_ge(counted, 1)
            step(dve.tensor_copy(scan[0][:].rearrange("p t e -> p (t e)"), count_bank[1][:, :]))
            for n in range(6):
                d = 1 << n
                dve.tensor_copy(scan[n + 1][:, 0:d, :], scan[n][:, 0:d, :])
                step(dve.tensor_tensor(scan[n + 1][:, d:, :], scan[n][:, d:, :], scan[n][:, :NTILE - d, :], ALU.add))
            step(dve.tensor_tensor(base[:], scan[6][:], scan[0][:], ALU.subtract))
            step(dve.tensor_tensor(place[:].rearrange("p t e -> p (t e)"), count_bank[0][:, :],
                                   base[:].rearrange("p t e -> p (t e)"), ALU.add))
            dve.tensor_scalar(keep[:], place[:], float(CAP), None, ALU.is_lt)
            dve.scalar_tensor_tensor(slot[:], io[:], float(CAP), place[:], ALU.mult, ALU.add)
            dve.drain()
            for k in range(2):
                dve.tensor_tensor(pick[k][:], oh[k][:], slot[:], ALU.mult)
                dve.tensor_tensor(pick[2 + k][:], oh[k][:], keep[:], ALU.mult)
            dve.drain()
            for k in range(2):
                dve.tensor_reduce(slot_k[:, k, :], pick[k][:], AX.X, ALU.add)
                dve.tensor_reduce(keep_k[:, k, :], pick[2 + k][:], AX.X, ALU.add)
            dve.drain()
            dve.tensor_tensor(weight[:], prob[:], keep_k[:], ALU.mult).then_inc(results, 1)
            step(dve.scalar_tensor_tensor(gat_f[:], slot_k[:], float(EXPERTS * CAP), keep_k[:], ALU.add, ALU.mult))
            dve.tensor_copy(gat[:], gat_f[:]).then_inc(results, 1)
            step(dve.tensor_scalar(out_f[:], keep_k[:], -1.0, -float(1 << 20), ALU.add, ALU.mult))
            step(dve.tensor_tensor(sca_f[:], gat_f[:], out_f[:], ALU.add))
            dve.tensor_copy(sca[:], sca_f[:]).then_inc(results, 1)
            dve.tensor_copy(tok[:], tok_f[:]).then_inc(results, 1)


def fill_slots(nc, scatter_d, slot_token):
    PER = 8
    with ExitStack() as ctx:
        table = ctx.enter_context(nc.sbuf_tensor("f_table", [P, 3, T // P], U32))
        cols = ctx.enter_context(nc.sbuf_tensor("f_cols", [P, 3, PER], U32))
        loaded = ctx.enter_context(nc.semaphore("f_loaded"))
        written = Signal(ctx, nc, "f_written", 2 * PER, 0, 16)
        block = ctx.enter_context(nc.Block())

        @block.gpsimd
        def _(pool):
            pool.dma_start(table[:], scatter_d).then_inc(loaded, 16)
            pool.wait_ge(loaded, 16)
            with pool.Fori(0, T // P // PER) as i:
                pool.tensor_copy(cols[:], table[:, :, bass.ds(i * PER, PER)])
                pool.drain()
                for t in range(PER):
                    for k in range(2):
                        pool.indirect_dma_start(slot_token, bass.IndirectOffsetOnAxis(ap=cols[:, k, t:t + 1], axis=0),
                                                cols[:, 2, t:t + 1], None, bounds_check=SLOTS_ALL - 1,
                                                oob_is_err=False).then_inc(written.sem, 16)
                pool.wait_ge(written.sem, written.at(i, 2 * PER - 1))


def experts(nc, slot_token, xn, w1, w2, ident, slot_out):
    NB = 512
    BLOCKS = CAP // NB
    A = NB // P
    FC = FFN // P
    UNITS = 2 * BLOCKS
    H_BANKS = 4
    TURNS = EXPERTS // 2
    with ExitStack() as ctx:
        def sb(name, shape, dt=F32):
            return ctx.enter_context(nc.sbuf_tensor("e_" + name, shape, dt))

        def sig(name, per, prime=0, unit=1):
            return Signal(ctx, nc, "e_" + name, per, prime, unit)

        eye = sb("eye", [P, P])
        w1s = [sb(f"w1{k}", [P, DC, FFN]) for k in range(2)]
        w2s = [sb(f"w2{k}", [P, FC, D]) for k in range(2)]
        ids = sb("ids", [P, 2, A], U32)
        rows = sb("rows", [P, 2, A, D])
        xt = sb("xt", [P, 2, DC, NB])
        hid = sb("hid", [P, 2, FC, NB])
        out = sb("out", [P, 2, A, D])
        t_bank = [ctx.enter_context(nc.psum_tensor(f"e_t{k}", [P, 512], F32)) for k in range(2)]
        h_bank = [ctx.enter_context(nc.psum_tensor(f"e_h{k}", [P, 512], F32)) for k in range(H_BANKS)]
        o_bank = [ctx.enter_context(nc.psum_tensor(f"e_o{k}", [P, 512], F32)) for k in range(2)]
        consts = sig("consts", 1, 0, 16)
        w_in = [sig(f"w_in{k}", 2, 0, 16) for k in range(2)]
        ids_in = [sig(f"ids_in{k}", BLOCKS, 0, 16) for k in range(2)]
        rows_in = [sig(f"rows_in{k}", BLOCKS * A, 0, 16) for k in range(2)]
        t_ready = sig("t_ready", UNITS * 2, 4)
        t_copied = sig("t_copied", UNITS * 2, 2)
        h_ready = sig("h_ready", UNITS * FC, 2 * FC)
        gelu_done = sig("gelu_done", UNITS * FC, H_BANKS)
        o_ready = sig("o_ready", UNITS * 2, 4)
        o_copied = sig("o_copied", UNITS * 2, 2)
        stored = [sig(f"stored{k}", BLOCKS, 1, 16) for k in range(2)]
        ticks = sig("ticks", 1)
        ticks2 = sig("ticks2", 1)
        block = ctx.enter_context(nc.Block())

        def units():
            return [(u, u // BLOCKS, u % BLOCKS) for u in range(UNITS)]

        @block.sync
        def _(sp):
            sp.dma_start(eye[:], ident).then_inc(consts.sem, 16)
            for s in stored:
                sp.sem_inc(s.sem, s.start)

            def weights(e, k):
                a, b = (w1[e], w2[e]) if isinstance(e, int) else (
                    w1[bass.ds(e, 1)].rearrange("o d f -> (o d) f"), w2[bass.ds(e, 1)].rearrange("o f d -> (o f) d"))
                sp.dma_start(w1s[k][:], a.rearrange("(c p) f -> p c f", p=P)).then_inc(w_in[k].sem, 16)
                sp.dma_start(w2s[k][:], b.rearrange("(c p) d -> p c d", p=P)).then_inc(w_in[k].sem, 16)

            def store(i, u):
                sp.wait_ge(o_copied.sem, o_copied.at(i, 2 * u + 1))
                sp.sem_inc(ticks.sem, 1)
                sp.dma_start(slot_out[bass.ds((i * UNITS + u) * NB, NB), :].rearrange("(p a) d -> p (a d)", a=A),
                             out[:, u % 2].rearrange("p a d -> p (a d)")).then_inc(stored[u % 2].sem, 16)

            weights(0, 0)
            weights(1, 1)

            def turn(i, last):
                for u, k, b in units():
                    store(i, u)
                    if b == BLOCKS - 1 and not last:
                        weights(i * 2 + 2 + k, k)
            with sp.Fori(0, TURNS - 1) as i:
                turn(i, False)
            turn(TURNS - 1, True)
            for k in range(2):
                sp.wait_ge(stored[k].sem, stored[k].at(TURNS - 1, BLOCKS - 1))

        @block.gpsimd
        def _(pool):
            pool.sem_inc(t_ready.sem, t_ready.start)

            def gather(i, u):
                n = u // 2
                pool.wait_ge(t_ready.sem, t_ready.at(i, 2 * u - 3))
                pool.sem_inc(ticks2.sem, 1)
                pool.dma_start(ids[:, u % 2, :], slot_token[bass.ds((i * UNITS + u) * NB, NB), :].rearrange(
                    "(p a) o -> p (a o)", a=A)).then_inc(ids_in[u % 2].sem, 16)
                pool.wait_ge(ids_in[u % 2].sem, ids_in[u % 2].at(i, n))
                pool.sem_inc(ticks2.sem, 1)
                for a in range(A):
                    pool.indirect_dma_start(rows[:, u % 2, a, :], None, xn,
                                            bass.IndirectOffsetOnAxis(ap=ids[:, u % 2, a:a + 1], axis=0),
                                            bounds_check=T - 1, oob_is_err=False).then_inc(rows_in[u % 2].sem, 16)

            with pool.Fori(0, TURNS) as i:
                for u, _, _ in units():
                    gather(i, u)

        @block.tensor
        def _(pe):
            pe.wait_ge(consts.sem, consts.at(0))
            pe.sem_inc(h_ready.sem, h_ready.start)
            pe.sem_inc(o_ready.sem, o_ready.start)

            def turned(i, u):
                pe.wait_ge(rows_in[u % 2].sem, rows_in[u % 2].at(i, (u // 2) * A + A - 1))
                for k in range(DC):
                    pe.wait_ge(t_copied.sem, t_copied.at(i, 2 * u + k - 2))
                    for a in range(A):
                        mm = pe.transpose(t_bank[k][:, a * P:a * P + P], rows[:, u % 2, a, k * P:k * P + P], eye[:, :])
                    mm.then_inc(t_ready.sem, 1)

            def up(i, u, e):
                if u % BLOCKS == 0:
                    pe.wait_ge(w_in[e].sem, w_in[e].at(i, 1))
                pe.wait_ge(t_copied.sem, t_copied.at(i, 2 * u + 1))
                for f in range(FC):
                    n = u * FC + f
                    pe.wait_ge(gelu_done.sem, gelu_done.at(i, n - H_BANKS))
                    bank = h_bank[n % H_BANKS]
                    for k in range(DC):
                        mm = pe.matmul(bank[:, :], w1s[e][:, k, f * P:f * P + P], xt[:, u % 2, k, :], start=(k == 0),
                                       stop=(k == DC - 1))
                    mm.then_inc(h_ready.sem, 1)

            def down(i, u, e):
                pe.wait_ge(gelu_done.sem, gelu_done.at(i, u * FC + FC - 1))
                for pair in range(2):
                    pe.wait_ge(o_copied.sem, o_copied.at(i, 2 * u + pair - 2))
                    for a in (2 * pair, 2 * pair + 1):
                        for f in range(FC):
                            mm = pe.matmul(o_bank[pair][:, (a % 2) * D:(a % 2) * D + D],
                                           hid[:, u % 2, f, a * P:a * P + P], w2s[e][:, f, :], start=(f == 0),
                                           stop=(f == FC - 1))
                    mm.then_inc(o_ready.sem, 1)

            with pe.Fori(0, TURNS) as i:
                turned(i, 0)
                for u, e, _ in units():
                    if u + 1 < UNITS:
                        turned(i, u + 1)
                    up(i, u, e)
                    if u:
                        down(i, u - 1, (u - 1) // BLOCKS)
                down(i, UNITS - 1, 1)

        @block.scalar
        def _(act):
            act.sem_inc(gelu_done.sem, gelu_done.start)
            with act.Fori(0, TURNS) as i:
                for u, _, _ in units():
                    for f in range(FC):
                        n = u * FC + f
                        act.wait_ge(h_ready.sem, h_ready.at(i, n))
                        if f == 0:
                            act.wait_ge(o_ready.sem, o_ready.at(i, 2 * u - 3))
                        act.activation(hid[:, u % 2, f, :], h_bank[n % H_BANKS][:, :], ACT.Gelu).then_inc(gelu_done.sem, 1)

        @block.vector
        def _(dve):
            dve.sem_inc(t_copied.sem, t_copied.start)
            dve.sem_inc(o_copied.sem, o_copied.start)

            def copy_turned(i, u):
                for k in range(DC):
                    dve.wait_ge(t_ready.sem, t_ready.at(i, 2 * u + k))
                    if k == 0:
                        dve.wait_ge(h_ready.sem, h_ready.at(i, (u - 1) * FC - 1))
                    dve.tensor_copy(xt[:, u % 2, k, :], t_bank[k][:, :]).then_inc(t_copied.sem, 1)

            def copy_out(i, u):
                for pair in range(2):
                    dve.wait_ge(o_ready.sem, o_ready.at(i, 2 * u + pair))
                    if pair == 0:
                        dve.wait_ge(stored[u % 2].sem, stored[u % 2].at(i, u // 2 - 1))
                    dve.tensor_copy(out[:, u % 2, 2 * pair:2 * pair + 2, :].rearrange("p a d -> p (a d)"),
                                    o_bank[pair][:, :]).then_inc(o_copied.sem, 1)

            with dve.Fori(0, TURNS) as i:
                copy_turned(i, 0)
                for u, _, _ in units():
                    if u + 1 < UNITS:
                        copy_turned(i, u + 1)
                    if u:
                        copy_out(i, u - 1)
                copy_out(i, UNITS - 1)


def combine(nc, resid, slot_out, gather_d, prob_d, out):
    with ExitStack() as ctx:
        def sb(name, shape, dt=F32):
            return ctx.enter_context(nc.sbuf_tensor("o_" + name, shape, dt))

        def sig(name, per, prime=0, unit=1):
            return Signal(ctx, nc, "o_" + name, per, prime, unit)

        idx_all = sb("idx_all", [P, 2, T // P], U32)
        prob_all = sb("prob_all", [P, 2, T // P])
        idx = sb("idx", [P, 2, NT], U32)
        prob = sb("prob", [P, 2, NT])
        neg_half = sb("neg_half", [P, NT])
        r = sb("r", [P, NT, D])
        y = sb("y", [P, NT, 2, D])
        s1 = sb("s1", [P, NT, D])
        s2 = sb("s2", [P, NT, D])
        st = sb("st", [P, NT, 6])
        mv = sb("mv", [P, NT, 2])
        var = sb("var", [P, NT])
        rstd = sb("rstd", [P, NT])
        res = sb("res", [P, NT, D])
        tables = sig("tables", 2, 0, 16)
        r_in = sig("r_in", 1, 0, 16)
        y_in = [sig(f"y_in{t}", 2, 0, 16) for t in range(NT)]
        prob_set = sig("prob_set", 1)
        summed = sig("summed", NT, NT)
        mv_done = sig("mv_done", 1)
        eps_added = sig("eps_added", 1)
        rstd_done = sig("rstd_done", 1)
        res_done = sig("res_done", 1)
        res_out = sig("res_out", 1, 1, 16)
        ticks = sig("ticks", 1)
        pool_ticks = sig("pool_ticks", 1)
        block = ctx.enter_context(nc.Block())

        @block.sync
        def _(sp):
            sp.dma_start(idx_all[:], gather_d).then_inc(tables.sem, 16)
            sp.dma_start(prob_all[:], prob_d).then_inc(tables.sem, 16)
            sp.sem_inc(res_out.sem, res_out.start)
            sp.dma_start(r[:], resid[0].rearrange("(t p) d -> p t d", p=P)).then_inc(r_in.sem, 16)

            def turn(i, last):
                sp.wait_ge(summed.sem, summed.at(i, NT - 1))
                sp.sem_inc(ticks.sem, 1)
                if not last:
                    sp.dma_start(r[:], resid[bass.ds(i + 1, 1)].rearrange("o (t p) d -> p (o t) d", p=P)).then_inc(
                        r_in.sem, 16)
                sp.wait_ge(res_done.sem, res_done.at(i))
                sp.sem_inc(ticks.sem, 1)
                sp.dma_start(out[bass.ds(i, 1)].rearrange("o (t p) d -> p (o t) d", p=P), res[:]).then_inc(
                    res_out.sem, 16)
            with sp.Fori(0, N - 1) as i:
                turn(i, False)
            turn(N - 1, True)
            sp.wait_ge(res_out.sem, res_out.at(N - 1))

        @block.gpsimd
        def _(pool):
            pool.wait_ge(tables.sem, tables.at(0, 1))
            pool.sem_inc(pool_ticks.sem, 1)
            pool.memset(neg_half[:, :], -0.5)
            pool.drain()

            def gathers(i):
                pool.wait_ge(summed.sem, summed.at(i, -1))
                pool.sem_inc(pool_ticks.sem, 1)
                pool.tensor_copy(idx[:], idx_all[:, :, bass.ds(i * NT, NT)])
                pool.tensor_copy(prob[:], prob_all[:, :, bass.ds(i * NT, NT)]).then_inc(prob_set.sem, 1)
                pool.drain()
                for t in range(NT):
                    for k in range(2):
                        pool.indirect_dma_start(y[:, t, k, :], None, slot_out,
                                                bass.IndirectOffsetOnAxis(ap=idx[:, k, t:t + 1], axis=0),
                                                bounds_check=SLOTS_ALL - 1, oob_is_err=False).then_inc(y_in[t].sem, 16)

            with pool.Fori(0, N) as i:
                gathers(i)
                pool.wait_ge(mv_done.sem, mv_done.at(i))
                pool.sem_inc(pool_ticks.sem, 1)
                pool.tensor_scalar(var[:, :], mv[:, :, 1], EPS, None, ALU.add).then_inc(eps_added.sem, 1)
                pool.wait_ge(eps_added.sem, eps_added.at(i))
                pool.tensor_tensor(rstd[:, :], var[:, :], neg_half[:, :], ALU.pow).then_inc(rstd_done.sem, 1)

        @block.vector
        def _(dve):
            dve.sem_inc(summed.sem, summed.start)
            with dve.Fori(0, N) as i:
                dve.wait_ge(r_in.sem, r_in.at(i))
                dve.wait_ge(prob_set.sem, prob_set.at(i))
                for t in range(NT):
                    dve.wait_ge(y_in[t].sem, y_in[t].at(i, 1))
                    dve.scalar_tensor_tensor(s1[:, t, :], y[:, t, 0, :], prob[:, 0, t:t + 1], r[:, t, :], ALU.mult,
                                             ALU.add)
                    dve.drain()
                    dve.scalar_tensor_tensor(s2[:, t, :], y[:, t, 1, :], prob[:, 1, t:t + 1], s1[:, t, :], ALU.mult,
                                             ALU.add).then_inc(summed.sem, 1)
                dve.drain()
                for t in range(NT):
                    dve.bn_stats(st[:, t, :], s2[:, t, :])
                dve.drain()
                for t in range(NT):
                    ins = dve.bn_aggr(mv[:, t, :], st[:, t, :])
                ins.then_inc(mv_done.sem, 1)
                dve.wait_ge(rstd_done.sem, rstd_done.at(i))
                dve.wait_ge(res_out.sem, res_out.at(i, -1))
                for t in range(NT):
                    ins = dve.tensor_scalar(res[:, t, :], s2[:, t, :], mv[:, t, 0:1], rstd[:, t:t + 1], ALU.subtract,
                                            ALU.mult)
                ins.then_inc(res_done.sem, 1)
                dve.drain()


def program(nc, a, out):
    def scratch(name, shape, dt=F32):
        return nc.dram_tensor("d_" + name, shape, dt, kind="Internal").ap()

    spectral = scratch("spectral", [D, D])
    x2 = scratch("x2", [N, S, D])
    x3 = scratch("x3", [N, S, D])
    split = scratch("split", [4 * N, 3, P, S], BF16)
    v_d = scratch("v", [N, P, 2 * NT * 8 * 32])
    guard_d = scratch("guard_d", [2, 3, 32, P], BF16)
    resid = scratch("resid", [N, S, D])
    xn = scratch("xn", [N, S, D])
    logits = scratch("logits", [NT, P, N, EXPERTS])
    gather_d = scratch("gather_d", [P, 2, T // P], U32)
    prob_d = scratch("prob_d", [P, 2, T // P])
    scatter_d = scratch("scatter_d", [P, 3, T // P], U32)
    slot_token = scratch("slot_token", [SLOTS_ALL, 1], U32)
    slot_out = scratch("slot_out", [SLOTS_ALL, D])

    spectral_matrix(nc, a["w_real"], a["w_imag"], a["cos"], a["nsin"], a["cos_n"], a["nsin_n"], spectral)
    linear_attention_and_spectral(nc, a["xT"], a["x"], a["wq"], a["bq"], a["wk"], a["bk"], a["wv"], a["bv"], a["wo"],
                                  a["bo"], a["ffn_bias"], a["w_kqv"], a["ident"], spectral, x2, split, v_d)
    causal_attention(nc, x2, split, v_d, a["ident"], a["above"], a["ramp_q"], a["ramp_k"], a["sel_q"], a["sel_k"],
                     a["m_rows"], guard_d, x3)
    position_attention(nc, x3, a["ln1_w"], a["ln1_b"], a["ln2_w"], a["ln2_b"], a["w_qkv"], a["w_proj"],
                       a["w_router"], a["ident"], resid, xn, logits)
    route(nc, logits, a["before"], a["iota"], a["token_ids"], gather_d, prob_d, scatter_d, slot_token)
    fill_slots(nc, scatter_d, slot_token)
    experts(nc, slot_token, xn.rearrange("n s d -> (n s) d"), a["w1"], a["w2"], a["ident"], slot_out)
    combine(nc, resid, slot_out, gather_d, prob_d, out)


def shape_constants():
    d = np.arange(D)
    angle = 2 * np.pi * (np.outer(d, d) % D) / D
    q = np.arange(P)
    pos = np.arange(S)
    high, low, zero, one = ((pos // P) * P, pos % P, 0 * pos, 0 * pos + 1)
    sel_q = np.zeros((15, 3))
    sel_k = np.zeros((15, 3))
    for part in range(3):
        sel_q[4 * part:4 * part + 2, part] = 1
        sel_k[4 * part + 2:4 * part + 4, part] = 1
    c = {
        "cos": np.cos(angle), "nsin": -np.sin(angle), "cos_n": np.cos(angle) / D, "nsin_n": -np.sin(angle) / D,
        "ident": np.eye(P),
        "above": np.stack([np.where(q[None, :] > q[:, None], -BIG, 0), np.where(q[None, :] < q[:, None], -BIG, 0)]),
        "ramp_q": np.stack([zero, zero, -high, -low] * 3 + [zero] * 3),
        "ramp_k": np.stack([high, low, zero, zero] * 3 + [-one] * 3),
        "sel_q": sel_q, "sel_k": sel_k,
        "before": q[:, None] < q[None, :],
        "iota": np.broadcast_to(np.arange(-EXPERTS, 0), (P, T // P, EXPERTS)),
        "token_ids": np.arange(T // P)[None, :] * P + q[:, None],
    }
    return {k: np.ascontiguousarray(v, dtype=np.float32) for k, v in c.items()}


def kernel(**inputs):
    import concourse.bacc as bacc
    from concourse.bass_utils import run_bass_kernel_spmd

    t = {k: np.asarray(v) for k, v in inputs.items()}

    def by_partition(v):
        return v.reshape(DC, P).T

    def on_all(v):
        return np.broadcast_to(v, (P, 2, D))

    arrays = {
        "x": t["L0_attn_x"], "xT": t["L0_attn_x"].transpose(0, 2, 1),
        "wq": t["L0_attn_Wq"], "wk": t["L0_attn_Wk"], "wv": t["L0_attn_Wv"], "wo": t["L0_attn_Wo"],
        "bq": by_partition(t["L0_attn_bq"]), "bk": by_partition(t["L0_attn_bk"]), "bv": by_partition(t["L0_attn_bv"]),
        "bo": on_all(t["L0_attn_bo"]), "ffn_bias": on_all(t["L0_ffn_bias"]),
        "w_real": t["L0_ffn_w_freq_real"], "w_imag": t["L0_ffn_w_freq_imag"],
        "w_kqv": t["L1_attn_W_kqv"], "m_rows": np.broadcast_to(t["L1_attn_m"].reshape(1, 16), (15, 16)),
        "ln1_w": on_all(t["L1_ffn_ln1_weight"]), "ln1_b": on_all(t["L1_ffn_ln1_bias"]),
        "ln2_w": on_all(t["L1_ffn_ln2_weight"]), "ln2_b": on_all(t["L1_ffn_ln2_bias"]),
        "w_qkv": t["L1_ffn_qkv_weight"].T, "w_proj": t["L1_ffn_proj_weight"].T,
        "w_router": t["L1_ffn_router_weight"], "w1": t["L1_ffn_moe_w1"], "w2": t["L1_ffn_moe_w2"],
    }
    arrays = {k: np.ascontiguousarray(v) for k, v in arrays.items()}
    arrays.update(shape_constants())
    nc = bacc.Bacc("TRN2", target_bir_lowering=False, num_devices=1)
    a = {k: nc.dram_tensor("in_" + k, v.shape, mybir.dt.from_np(v.dtype), kind="ExternalInput").ap()
         for k, v in arrays.items()}
    out = nc.dram_tensor("out", (N, S, D), F32, kind="ExternalOutput").ap()
    program(nc, a, out)
    r = run_bass_kernel_spmd(nc, [{"in_" + k: v for k, v in arrays.items()}], core_ids=[0])
    return r.results[0]["out"]
```

```python
from contextlib import ExitStack

import numpy as np
import concourse.bass as bass
from concourse import mybir

F32 = mybir.dt.float32
F32R = mybir.dt.float32r
BF16 = mybir.dt.bfloat16
U32 = mybir.dt.uint32
ALU = mybir.AluOpType
ACT = mybir.ActivationFunctionType
AX = mybir.AxisListType

P = 128
N, S, D = 8, 1024, 256
DC = D // P
NT = S // P
NPAIR = NT // 2
T = N * S
EPS = 1e-5
BIG = 1e30


class Signal:

    def __init__(self, ctx, nc, name, per, prime=0, unit=1):
        self.sem = ctx.enter_context(nc.semaphore(name))
        self.per, self.prime, self.unit = per, prime, unit
        self.start = prime * unit

    def at(self, i, k=0):
        return i * (self.per * self.unit) + (k + 1 + self.prime) * self.unit


def spectral_matrix(nc, w_real, w_imag, cos, nsin, spectral):
    with ExitStack() as ctx:
        def sb(name, shape, dt=F32):
            return ctx.enter_context(nc.sbuf_tensor("m_" + name, shape, dt))

        wr = sb("wr", [P, DC, D])
        wi = sb("wi", [P, DC, D])
        c = sb("c", [P, DC, D])
        ns = sb("ns", [P, DC, D])
        ps = sb("ps", [P, DC, D])
        re_t = sb("re_t", [P, DC, D])
        im_t = sb("im_t", [P, DC, D])
        m = sb("m", [P, DC, D])
        bank = [ctx.enter_context(nc.psum_tensor(f"m_bank{i}", [P, 512], F32)) for i in range(6)]
        loaded = ctx.enter_context(nc.semaphore("m_loaded"))
        sin_ready = ctx.enter_context(nc.semaphore("m_sin_ready"))
        product = ctx.enter_context(nc.semaphore("m_product"))
        copied = ctx.enter_context(nc.semaphore("m_copied"))
        stored = ctx.enter_context(nc.semaphore("m_stored"))
        block = ctx.enter_context(nc.Block())

        @block.sync
        def _(sp):
            for dst, src in ((wr, w_real), (wi, w_imag), (c, cos), (ns, nsin)):
                sp.dma_start(dst[:], src.rearrange("(c p) n -> p c n", p=P)).then_inc(loaded, 16)
            sp.wait_ge(copied, 6)
            sp.dma_start(spectral.rearrange("(c p) n -> p c n", p=P), m[:]).then_inc(stored, 16)
            sp.wait_ge(stored, 16)

        @block.tensor
        def _(pe):
            pe.wait_ge(loaded, 4 * 16)
            pe.wait_ge(sin_ready, 1)
            for oc in range(DC):
                cols = slice(oc * P, oc * P + P)
                for n, (a, b) in enumerate(((wi, ps), (wr, ns))):
                    main = wr if n == 0 else wi
                    out = bank[2 * oc + n][:, 0:D]
                    for k in range(DC):
                        pe.matmul(out, main[:, k, cols], c[:, k, :], start=(k == 0), stop=False)
                    for k in range(DC):
                        mm = pe.matmul(out, a[:, k, cols], b[:, k, :], start=False, stop=(k == DC - 1))
                    mm.then_inc(product, 1)
            pe.wait_ge(copied, 4)
            for dc in range(DC):
                cols = slice(dc * P, dc * P + P)
                out = bank[4 + dc][:, 0:D]
                for k in range(DC):
                    pe.matmul(out, re_t[:, k, cols], c[:, k, :], start=(k == 0), stop=False)
                for k in range(DC):
                    mm = pe.matmul(out, im_t[:, k, cols], ns[:, k, :], start=False, stop=(k == DC - 1))
                mm.then_inc(product, 1)

        @block.vector
        def _(dve):
            dve.wait_ge(loaded, 4 * 16)
            dve.tensor_scalar(ps[:], ns[:], -1.0, None, ALU.mult).then_inc(sin_ready, 1)
            for n, dst in enumerate((re_t[:, 0, :], im_t[:, 0, :], re_t[:, 1, :], im_t[:, 1, :])):
                dve.wait_ge(product, n + 1)
                dve.tensor_copy(dst, bank[n][:, 0:D]).then_inc(copied, 1)
            for n in range(DC):
                dve.wait_ge(product, 4 + n + 1)
                dve.tensor_scalar(m[:, n, :], bank[4 + n][:, 0:D], 1.0 / D, None, ALU.mult).then_inc(copied, 1)


def linear_attention_and_spectral(nc, xT, x, wq, bq, wk, bk, wv, bv, wo, bo2, bias2, w_kqv, ident, spectral, x2,
                                  split, v_d, ticks, pool_ticks):
    SLOTS = 10
    FRONT = {
        0: ("k0", "v0"),
        1: ("k1",),
        2: ("v1", "k2", "v2"),
        4: ("k3", "v3"),
        5: ("q4",),
        6: ("q5",),
        7: ("q6",),
        8: ("q7",),
    }
    NEXT = {
        6: ((0, 0, 0), (0, 1, 0)),
        7: ((1, 0, 0), (1, 1, 0), ("v", 0), ("v", 1)),
        8: ((0, 0, 1), (0, 1, 1), (1, 0, 1), (1, 1, 1)),
        9: (("v", 2), ("v", 3)),
    }
    ORDER = {
        "tensor": ("project_out", "front", "times_m", "turn_x1", "turn_x2", "project_next"),
        "scalar": ("front", "copy_x1", "gelu", "copy_x2", "next_parts"),
        "vector": ("front_k", "norm_x1", "norm_x2", "front_q", "residual_1", "residual_2", "next_rests", "add_bias"),
        "pool": ("x1_and_bias", "rstd_1", "rstd_2", "next_lows"),
    }
    NEXT_ORDER = [u for s in sorted(NEXT) for u in NEXT[s]]
    SPLIT_ORDER = [u for u in NEXT_ORDER if u[0] != "v"]
    TURNED = [(w, s - 2 - 2 * w) for s in range(SLOTS) for w in (0, 1) if 0 <= s - 2 - 2 * w < NPAIR]
    HEADS, HD, VW = 16, 16, 32
    HH = HEADS // 2
    with ExitStack() as ctx:
        def sb(name, shape, dt=F32):
            return ctx.enter_context(nc.sbuf_tensor("a_" + name, shape, dt))

        def sig(name, per, prime=0, unit=1):
            return Signal(ctx, nc, "a_" + name, per, prime, unit)

        def psum(name):
            return ctx.enter_context(nc.psum_tensor("a_" + name, [P, 512], F32))

        w = {k: sb("w" + k, [P, DC, D]) for k in "qkvom"}
        w_next = sb("w_next", [P, DC, 3 * D])
        b = {k: sb("b" + k, [P, DC]) for k in "qkv"}
        minus_b = {k: sb("minus_b" + k, [P, DC]) for k in "qk"}
        bo_b = sb("bo_b", [P, 2, D])
        bias_b = sb("bias_b", [P, 2, D])
        eye = sb("eye", [P, P])
        neg_half = sb("neg_half", [P, 2])
        xt = sb("xt", [P, DC, S])
        xs = sb("xs", [P, NT, D])
        n_t = sb("n_t", [P, 2, 512])
        e_t = sb("e_t", [P, 2, 512])
        r_t = sb("r_t", [P, 2, 512])
        keys = sb("keys", [P, DC, S])
        q_t = sb("q_t", [P, 2, 512])
        z_t = sb("z_t", [P, 2, 512])
        junk = sb("junk", [P, 512])
        ksum2 = sb("ksum2", [P, DC, 2])
        kv2 = sb("kv2", [P, DC, 2])
        ksum = sb("ksum", [P, DC])
        kv = sb("kv", [P, DC])
        vp = sb("vp", [P, DC, S])
        pre = sb("pre", [P, 2, 2, D])
        g = sb("g", [P, 2, 2, D])
        h = sb("h", [P, NT, D])
        x1 = sb("x1", [P, NT, D])
        x1b = sb("x1b", [P, NT, D])
        h2 = sb("h2", [P, NT, D])
        x2s = sb("x2s", [P, NT, D])
        st = sb("st", [P, NT, 2, 6])
        mv = sb("mv", [P, 2, NT, 2])
        var = sb("var", [P, 2, NT])
        rstd = sb("rstd", [P, 2, NT])
        x1t = sb("x1t", [P, 2, DC, 2 * P])
        x2t = sb("x2t", [P, DC, S])
        parts = sb("parts", [P, 2, 3, 512], BF16)
        rest = sb("rest", [P, 2, 512])
        vs = sb("vs", [P, 2, NT, HH, VW])
        act_bank = [psum(f"act{k}") for k in range(2)]
        v_bank, o_bank, t_bank, m_bank = (psum(k) for k in ("v", "o", "t", "mb"))
        next_bank = [psum(f"next{k}") for k in range(2)]

        consts = sig("consts", 1, 0, 16)
        xt_in = sig("xt_in", 1, 0, 16)
        xs_in = sig("xs_in", 1, 0, 16)
        kq_ready = sig("kq_ready", 8)
        v_ready = sig("v_ready", 4)
        er_ready = sig("er_ready", 8, 2)
        er_read = sig("er_read", 8, 2)
        v_done = sig("v_done", 4, 1)
        vp_done = sig("vp_done", 4)
        o_ready = sig("o_ready", NPAIR)
        o_added = sig("o_added", NPAIR, 1)
        gelu_done = sig("gelu_done", NPAIR, 2)
        h_done = sig("h_done", NPAIR, 2)
        mv_done = [sig(f"mv_done{k}", NPAIR) for k in range(2)]
        eps_added = [sig(f"eps_added{k}", NPAIR) for k in range(2)]
        rstd_done = [sig(f"rstd_done{k}", NPAIR) for k in range(2)]
        x1_done = sig("x1_done", NPAIR)
        x1b_done = sig("x1b_done", NPAIR)
        turned = sig("turned", 2 * NPAIR)
        turned_read = sig("turned_read", 2 * NPAIR, 1)
        m_ready = sig("m_ready", NPAIR, 2)
        h2_done = sig("h2_done", NPAIR, 1)
        x2_done = sig("x2_done", NPAIR)
        next_ready = sig("next_ready", 12)
        high_done = sig("high_done", 8)
        rest_done = sig("rest_done", 8)
        middle_done = sig("middle_done", 8)
        v_copied = sig("v_copied", 4)
        split_done = sig("split_done", 8, 2)
        split_out = [sig(f"split_out{k}", 4, 1, 16) for k in range(2)]
        v_set = sig("v_set", 1)
        v_out = sig("v_out", 1, 1, 16)
        x2_out = sig("x2_out", 1, 1, 16)
        block = ctx.enter_context(nc.Block())

        def turns(eng, turn, front):
            for s in range(SLOTS + 1):
                front(0, s)
            with eng.Fori(0, N - 1) as i:
                turn(i, lambda s, *kinds: front(i + 1, s, *kinds))
            turn(N - 1, lambda s, *kinds: None)

        def front_units(s, kinds):
            return [(u[0], int(u[1])) for u in FRONT.get(s, ()) if u[0] in kinds]

        def bank_read(at):
            u = NEXT_ORDER[at]
            if u[0] == "v":
                return v_copied, u[1]
            return rest_done, SPLIT_ORDER.index(u)

        @block.sync
        def _(sp):
            for k, src in zip("qkvom", (wq, wk, wv, wo, spectral)):
                sp.dma_start(w[k][:], src.rearrange("(c p) n -> p c n", p=P)).then_inc(consts.sem, 16)
            for k, src in zip("qkv", (bq, bk, bv)):
                sp.dma_start(b[k][:], src).then_inc(consts.sem, 16)
            sp.dma_start(w_next[:], w_kqv.rearrange("(c p) n -> p c n", p=P)).then_inc(consts.sem, 16)
            sp.dma_start(bo_b[:], bo2).then_inc(consts.sem, 16)
            sp.dma_start(bias_b[:], bias2).then_inc(consts.sem, 16)
            sp.dma_start(eye[:], ident).then_inc(consts.sem, 16)
            sp.sem_inc(x2_out.sem, x2_out.start)
            sp.sem_inc(v_out.sem, v_out.start)
            for k in range(2):
                sp.sem_inc(split_out[k].sem, split_out[k].start)
            sp.dma_start(xt[:], xT[0].rearrange("(c p) s -> p c s", p=P)).then_inc(xt_in.sem, 16)
            sp.dma_start(xs[:], x[0].rearrange("(t p) d -> p t d", p=P)).then_inc(xs_in.sem, 16)
            sp.wait_ge(kq_ready.sem, kq_ready.at(0, 7))
            sp.wait_ge(v_ready.sem, v_ready.at(0, 3))
            sp.dma_start(xt[:], xT[1].rearrange("(c p) s -> p c s", p=P)).then_inc(xt_in.sem, 16)

            def turn(i, more_x, more_xt):
                sp.wait_ge(h_done.sem, h_done.at(i, NPAIR - 1))
                sp.sem_inc(ticks.sem, 1)
                if more_x:
                    sp.dma_start(xs[:], x[bass.ds(i + 1, 1)].rearrange("o (t p) d -> p (o t) d", p=P)).then_inc(
                        xs_in.sem, 16)
                for n, (kind, half, c) in enumerate(SPLIT_ORDER):
                    if n == 4:
                        sp.wait_ge(x2_done.sem, x2_done.at(i, NPAIR - 1))
                        sp.sem_inc(ticks.sem, 1)
                        sp.dma_start(x2[bass.ds(i, 1)].rearrange("o (t p) d -> p (o t) d", p=P), x2s[:]).then_inc(
                            x2_out.sem, 16)
                        if more_xt:
                            sp.wait_ge(kq_ready.sem, kq_ready.at(i + 1, 7))
                            sp.wait_ge(v_ready.sem, v_ready.at(i + 1, 3))
                            sp.sem_inc(ticks.sem, 1)
                            sp.dma_start(xt[:], xT[bass.ds(i + 2, 1)].rearrange("o (c p) s -> p (o c) s", p=P)
                                         ).then_inc(xt_in.sem, 16)
                    sp.wait_ge(split_done.sem, split_done.at(i, n))
                    sp.sem_inc(ticks.sem, 1)
                    sp.dma_start(split[bass.ds((i * 2 + half) * 2 + kind, 1), :, :, c * 512:c * 512 + 512].rearrange(
                        "o r p s -> p (o r) s"), parts[:, n % 2]).then_inc(split_out[n % 2].sem, 16)
                sp.wait_ge(v_copied.sem, v_copied.at(i, 3))
                sp.sem_inc(ticks.sem, 1)
                sp.dma_start(v_d[bass.ds(i, 1)].rearrange("o p n -> p (o n)"),
                             vs[:].rearrange("p a t h w -> p (a t h w)")).then_inc(v_out.sem, 16)

            with sp.Fori(0, N - 2) as i:
                turn(i, True, True)
            turn(N - 2, True, False)
            turn(N - 1, False, False)
            sp.wait_ge(x2_out.sem, x2_out.at(N - 1))
            sp.wait_ge(v_out.sem, v_out.at(N - 1))
            for k in range(2):
                sp.wait_ge(split_out[k].sem, split_out[k].at(N - 1, 3))

        @block.tensor
        def _(pe):
            pe.wait_ge(consts.sem, 12 * 16)
            pe.sem_inc(m_ready.sem, m_ready.start)

            def front(i, s):
                for kind, n in front_units(s, "kvq"):
                    hc, c = (n % 2, (n - 4) // 2) if kind == "q" else (n // 2, n % 2)
                    if (kind, n) == ("k", 0):
                        pe.wait_ge(xt_in.sem, xt_in.at(i))
                    if kind == "v":
                        pe.wait_ge(v_done.sem, v_done.at(i, n - 1))
                        bank = v_bank
                    else:
                        pe.wait_ge(er_ready.sem, er_ready.at(i, n - 2))
                        bank = act_bank[n % 2]
                    for k in range(DC):
                        mm = pe.matmul(bank[:, :], w[kind][:, k, hc * P:hc * P + P], xt[:, k, c * 512:c * 512 + 512],
                                       start=(k == 0), stop=(k == DC - 1))
                    mm.then_inc(v_ready.sem if kind == "v" else kq_ready.sem, 1)

            def transpose_pair(i, which, p):
                at = TURNED.index((which, p))
                src, done = ((x1, x1_done), (x2s, x2_done))[which]
                pe.wait_ge(done.sem, done.at(i, p))
                pe.wait_ge(turned_read.sem, turned_read.at(i, at - 1))
                for k in range(DC):
                    for t in (2 * p, 2 * p + 1):
                        c0 = k * 256 + (t % 2) * P
                        mm = pe.transpose(t_bank[:, c0:c0 + P], src[:, t, k * P:k * P + P], eye[:, :])
                mm.then_inc(turned.sem, 1)

            def turn(i, next_front):
                def project_out(s):
                    if s < NPAIR:
                        p = s
                        pe.wait_ge(vp_done.sem, vp_done.at(i, (2 * p // 4) * 2 + 1))
                        pe.wait_ge(o_added.sem, o_added.at(i, p - 1))
                        for t in (2 * p, 2 * p + 1):
                            for k in range(DC):
                                mm = pe.matmul(o_bank[:, (t % 2) * D:(t % 2) * D + D], vp[:, k, t * P:t * P + P],
                                               w["o"][:, k, :], start=(k == 0), stop=(k == DC - 1))
                        mm.then_inc(o_ready.sem, 1)

                def turn_x1(s):
                    if 0 <= s - 2 < NPAIR:
                        transpose_pair(i, 0, s - 2)

                def times_m(s):
                    if 0 <= s - 3 < NPAIR:
                        p = s - 3
                        pe.wait_ge(turned_read.sem, turned_read.at(i, TURNED.index((0, p))))
                        pe.wait_ge(h2_done.sem, h2_done.at(i, p - 1))
                        for t in (2 * p, 2 * p + 1):
                            for k in range(DC):
                                mm = pe.matmul(m_bank[:, (t % 2) * D:(t % 2) * D + D],
                                               x1t[:, p % 2, k, (t % 2) * P:(t % 2) * P + P], w["m"][:, k, :],
                                               start=(k == 0), stop=(k == DC - 1))
                        mm.then_inc(m_ready.sem, 1)

                def turn_x2(s):
                    if 0 <= s - 4 < NPAIR:
                        transpose_pair(i, 1, s - 4)

                def project_next(s):
                    for u in NEXT.get(s, ()):
                        at = NEXT_ORDER.index(u)
                        half_of_tokens = u[1] // 2 if u[0] == "v" else u[2]
                        pe.wait_ge(turned_read.sem, turned_read.at(i, TURNED.index((1, 2 * half_of_tokens + 1))))
                        if at >= 2:
                            sig_, n = bank_read(at - 2)
                            pe.wait_ge(sig_.sem, sig_.at(i, n))
                        bank = next_bank[at % 2]
                        if u[0] == "v":
                            for t in (2 * u[1], 2 * u[1] + 1):
                                for k in range(DC):
                                    mm = pe.matmul(bank[:, (t % 2) * D:(t % 2) * D + D], x2t[:, k, t * P:t * P + P],
                                                   w_next[:, k, 2 * D:3 * D], start=(k == 0), stop=(k == DC - 1))
                        else:
                            kind, half, c = u
                            col = (1 - kind) * D + half * P
                            for k in range(DC):
                                mm = pe.matmul(bank[:, :], w_next[:, k, col:col + P], x2t[:, k, c * 512:c * 512 + 512],
                                               start=(k == 0), stop=(k == DC - 1))
                        mm.then_inc(next_ready.sem, 1)

                work = {"project_out": project_out, "front": next_front, "turn_x1": turn_x1, "times_m": times_m,
                        "turn_x2": turn_x2, "project_next": project_next}
                for s in range(SLOTS):
                    for name in ORDER["tensor"]:
                        work[name](s)

            turns(pe, turn, front)

        @block.scalar
        def _(act):
            act.sem_inc(er_ready.sem, er_ready.start)
            act.sem_inc(gelu_done.sem, gelu_done.start)
            act.sem_inc(turned_read.sem, turned_read.start)
            act.wait_ge(consts.sem, 12 * 16)
            for kind in "kq":
                act.activation(minus_b[kind][:, :], b[kind][:, :], ACT.Copy, scale=-1.0)
            act.drain()

            def front(i, s):
                for kind, n in front_units(s, "kq"):
                    hc = n // 2 if kind == "k" else n % 2
                    act.wait_ge(kq_ready.sem, kq_ready.at(i, n))
                    act.wait_ge(er_read.sem, er_read.at(i, n - 2))
                    act.activation(n_t[:, n % 2, :], act_bank[n % 2][:, :], ACT.Relu, scale=-1.0,
                                   bias=minus_b[kind][:, hc:hc + 1])
                    act.activation(r_t[:, n % 2, :], act_bank[n % 2][:, :], ACT.Relu, bias=b[kind][:, hc:hc + 1])
                    act.drain()
                    act.activation(e_t[:, n % 2, :], n_t[:, n % 2, :], ACT.Exp, scale=-1.0).then_inc(er_ready.sem, 1)

            def copy_turned(i, which, p):
                at = TURNED.index((which, p))
                act.wait_ge(turned.sem, turned.at(i, at))
                if which == 0:
                    act.wait_ge(m_ready.sem, m_ready.at(i, p - 2))
                    dst = x1t[:, p % 2]
                else:
                    dst = x2t[:, :, 2 * p * P:2 * p * P + 2 * P]
                act.activation(dst, t_bank[:, :].rearrange("p (c t) -> p c t", c=DC), ACT.Copy).then_inc(
                    turned_read.sem, 1)

            def turn(i, next_front):
                def copy_x1(s):
                    if 0 <= s - 2 < NPAIR:
                        copy_turned(i, 0, s - 2)

                def copy_x2(s):
                    if 0 <= s - 4 < NPAIR:
                        copy_turned(i, 1, s - 4)

                def gelu(s):
                    if s < NPAIR:
                        p = s
                        act.wait_ge(o_added.sem, o_added.at(i, p))
                        act.wait_ge(h_done.sem, h_done.at(i, p - 2))
                        act.activation(g[:, p % 2], pre[:, p % 2], ACT.Gelu_apprx_tanh).then_inc(gelu_done.sem, 1)

                def next_parts(s):
                    for u in NEXT.get(s, ()):
                        at = NEXT_ORDER.index(u)
                        act.wait_ge(next_ready.sem, next_ready.at(i, at))
                        if u[0] == "v":
                            if u[1] == 0:
                                act.wait_ge(v_set.sem, 1)
                                act.wait_ge(v_out.sem, v_out.at(i, -1))
                            for half in range(2):
                                ins = act.activation(
                                    vs[:, half, 2 * u[1]:2 * u[1] + 2, :, 0:HD],
                                    next_bank[at % 2][:, :].rearrange("p (t a h d) -> p a t h d", t=2, a=2,
                                                                      d=HD)[:, half], ACT.Copy)
                            ins.then_inc(v_copied.sem, 1)
                        else:
                            n = SPLIT_ORDER.index(u)
                            act.wait_ge(split_out[n % 2].sem, split_out[n % 2].at(i, n // 2 - 1))
                            act.activation(parts[:, n % 2, 0, :], next_bank[at % 2][:, :], ACT.Copy,
                                           scale=1.0 if u[0] else 1.0 / 16).then_inc(high_done.sem, 1)

                work = {"front": next_front, "copy_x1": copy_x1, "copy_x2": copy_x2, "gelu": gelu,
                        "next_parts": next_parts}
                for s in range(SLOTS):
                    for name in ORDER["scalar"]:
                        work[name](s)

            turns(act, turn, front)

        @block.vector
        def _(dve):
            dve.memset(vs[:], 0.0)
            dve.drain()
            dve.memset(vs[:].rearrange("p a t h w -> p (a t h) w")[:, :, HD:HD + 1], 1.0).then_inc(v_set.sem, 1)
            for s in (er_read, v_done, o_added, h_done, h2_done):
                dve.sem_inc(s.sem, s.start)
            dve.wait_ge(consts.sem, 12 * 16)

            def front(i, s, kinds="kq"):
                for kind, n in front_units(s - 1, kinds):
                    hc, c = (n % 2, (n - 4) // 2) if kind == "q" else (n // 2, n % 2)
                    dve.wait_ge(er_ready.sem, er_ready.at(i, n))
                    dve.tensor_scalar(e_t[:, n % 2, :], e_t[:, n % 2, :], -1.0, None, ALU.add)
                    dve.drain()
                    if kind == "k":
                        chunk = keys[:, hc, c * 512:c * 512 + 512]
                        dve.scalar_tensor_tensor(chunk, e_t[:, n % 2, :], 1.0, r_t[:, n % 2, :], ALU.add, ALU.add,
                                                 accum_out=ksum2[:, hc, c:c + 1]).then_inc(er_read.sem, 1)
                        dve.drain()
                        dve.wait_ge(v_ready.sem, v_ready.at(i, n))
                        dve.scalar_tensor_tensor(junk[:, :], v_bank[:, :], b["v"][:, hc:hc + 1], chunk, ALU.add,
                                                 ALU.mult, accum_out=kv2[:, hc, c:c + 1]).then_inc(v_done.sem, 1)
                        if n == 3:
                            dve.drain()
                            dve.tensor_tensor(ksum[:, :], ksum2[:, :, 0], ksum2[:, :, 1], ALU.add)
                            dve.tensor_tensor(kv[:, :], kv2[:, :, 0], kv2[:, :, 1], ALU.add)
                            dve.drain()
                    else:
                        dve.scalar_tensor_tensor(q_t[:, n % 2, :], e_t[:, n % 2, :], 1.0, r_t[:, n % 2, :], ALU.add,
                                                 ALU.add).then_inc(er_read.sem, 1)
                        dve.drain()
                        dve.tensor_scalar(z_t[:, n % 2, :], q_t[:, n % 2, :], ksum[:, hc:hc + 1], 1e-6, ALU.mult,
                                          ALU.add)
                        dve.drain()
                        dve.reciprocal(z_t[:, n % 2, :], z_t[:, n % 2, :])
                        dve.drain()
                        dve.scalar_tensor_tensor(vp[:, hc, c * 512:c * 512 + 512], q_t[:, n % 2, :], kv[:, hc:hc + 1],
                                                 z_t[:, n % 2, :], ALU.mult, ALU.mult).then_inc(vp_done.sem, 1)

            def residual_stats(which, p, dst, a, c, done):
                hp = slice(2 * p, 2 * p + 2)
                dve.tensor_tensor(dst[:, hp, :], a, c[:, hp, :], ALU.add).then_inc(done.sem, 1)
                dve.drain()
                for t in (2 * p, 2 * p + 1):
                    dve.bn_stats(st[:, t, which, :], dst[:, t, :])
                dve.drain()
                for t in (2 * p, 2 * p + 1):
                    ins = dve.bn_aggr(mv[:, which, t, :], st[:, t, which, :])
                ins.then_inc(mv_done[which].sem, 1)

            def turn(i, next_front):
                def add_bias(s):
                    if s < NPAIR:
                        p = s
                        dve.wait_ge(o_ready.sem, o_ready.at(i, p))
                        dve.wait_ge(gelu_done.sem, gelu_done.at(i, p - 2))
                        dve.tensor_tensor(pre[:, p % 2].rearrange("p t d -> p (t d)"), o_bank[:, :],
                                          bo_b[:].rearrange("p t d -> p (t d)"), ALU.add).then_inc(o_added.sem, 1)

                def norm_x1(s):
                    if 0 <= s - 2 < NPAIR:
                        p = s - 2
                        dve.wait_ge(rstd_done[0].sem, rstd_done[0].at(i, p))
                        for t in (2 * p, 2 * p + 1):
                            ins = dve.tensor_scalar(x1[:, t, :], h[:, t, :], mv[:, 0, t, 0:1], rstd[:, 0, t:t + 1],
                                                    ALU.subtract, ALU.mult)
                        ins.then_inc(x1_done.sem, 1)

                def norm_x2(s):
                    if 0 <= s - 4 < NPAIR:
                        p = s - 4
                        dve.wait_ge(rstd_done[1].sem, rstd_done[1].at(i, p))
                        if p == 0:
                            dve.wait_ge(x2_out.sem, x2_out.at(i, -1))
                        for t in (2 * p, 2 * p + 1):
                            ins = dve.tensor_scalar(x2s[:, t, :], h2[:, t, :], mv[:, 1, t, 0:1], rstd[:, 1, t:t + 1],
                                                    ALU.subtract, ALU.mult)
                        ins.then_inc(x2_done.sem, 1)

                def residual_1(s):
                    if 0 <= s - 1 < NPAIR:
                        p = s - 1
                        if p == 0:
                            dve.wait_ge(xs_in.sem, xs_in.at(i))
                        dve.wait_ge(gelu_done.sem, gelu_done.at(i, p))
                        residual_stats(0, p, h, g[:, p % 2], xs, h_done)

                def residual_2(s):
                    if 0 <= s - 3 < NPAIR:
                        p = s - 3
                        dve.wait_ge(m_ready.sem, m_ready.at(i, p))
                        dve.wait_ge(x1b_done.sem, x1b_done.at(i, p))
                        residual_stats(1, p, h2, m_bank[:, :].rearrange("p (t d) -> p t d", t=2), x1b, h2_done)

                def next_rests(s):
                    for u in NEXT.get(s, ()):
                        if u[0] == "v":
                            continue
                        at, n = NEXT_ORDER.index(u), SPLIT_ORDER.index(u)
                        dve.wait_ge(high_done.sem, high_done.at(i, n))
                        dve.wait_ge(split_done.sem, split_done.at(i, n - 2))
                        dve.scalar_tensor_tensor(rest[:, n % 2, :], next_bank[at % 2][:, :], 1.0 if u[0] else 1.0 / 16,
                                                 parts[:, n % 2, 0, :], ALU.mult, ALU.subtract).then_inc(
                                                     rest_done.sem, 1)
                        dve.drain()
                        dve.tensor_copy(parts[:, n % 2, 1, :], rest[:, n % 2, :]).then_inc(middle_done.sem, 1)

                work = {"add_bias": add_bias, "norm_x1": norm_x1, "norm_x2": norm_x2,
                        "front_k": lambda s: next_front(s, "k"), "front_q": lambda s: next_front(s, "q"),
                        "residual_1": residual_1, "residual_2": residual_2, "next_rests": next_rests}
                for s in range(SLOTS):
                    for name in ORDER["vector"]:
                        work[name](s)
                next_front(SLOTS)

            turns(dve, turn, front)

        @block.gpsimd
        def _(pool):
            pool.sem_inc(split_done.sem, split_done.start)
            pool.memset(neg_half[:, :], -0.5)
            pool.wait_ge(consts.sem, 12 * 16)
            pool.sem_inc(pool_ticks.sem, 1)
            pool.drain()

            def inverse_std(i, which, p):
                c = slice(2 * p, 2 * p + 2)
                pool.wait_ge(mv_done[which].sem, mv_done[which].at(i, p))
                pool.sem_inc(pool_ticks.sem, 1)
                pool.tensor_scalar(var[:, which, c], mv[:, which, c, 1], EPS, None, ALU.add).then_inc(
                    eps_added[which].sem, 1)
                pool.wait_ge(eps_added[which].sem, eps_added[which].at(i, p))
                pool.tensor_tensor(rstd[:, which, c], var[:, which, c], neg_half[:, :], ALU.pow).then_inc(
                    rstd_done[which].sem, 1)

            def turn(i, next_front):
                def x1_and_bias(s):
                    if 0 <= s - 2 < NPAIR:
                        p = s - 2
                        pool.wait_ge(x1_done.sem, x1_done.at(i, p))
                        hp = slice(2 * p, 2 * p + 2)
                        pool.tensor_tensor(x1b[:, hp, :], x1[:, hp, :], bias_b[:], ALU.add).then_inc(x1b_done.sem, 1)

                def rstd_1(s):
                    if 0 <= s - 1 < NPAIR:
                        inverse_std(i, 0, s - 1)

                def rstd_2(s):
                    if 0 <= s - 3 < NPAIR:
                        inverse_std(i, 1, s - 3)

                def next_lows(s):
                    for u in NEXT.get(s, ()):
                        if u[0] == "v":
                            continue
                        n = SPLIT_ORDER.index(u)
                        pool.wait_ge(middle_done.sem, middle_done.at(i, n))
                        pool.sem_inc(pool_ticks.sem, 1)
                        pool.tensor_tensor(parts[:, n % 2, 2, :], rest[:, n % 2, :], parts[:, n % 2, 1, :],
                                           ALU.subtract).then_inc(split_done.sem, 1)

                work = {"x1_and_bias": x1_and_bias, "rstd_1": rstd_1, "rstd_2": rstd_2, "next_lows": next_lows}
                for s in range(SLOTS):
                    for name in ORDER["pool"]:
                        work[name](s)

            turns(pool, turn, lambda i, s: None)


def causal_attention(nc, x2, split, v_d, ident, above, ramp_q, ramp_k, sel_q, sel_k, m_rows, guard_d, x3,
                     ticks, pool_ticks):
    H, HD = 16, 16
    HH = H // 2
    G = HH // 2
    PARTS = 3
    PROD = 6 * HD
    SCORE_ROWS = PROD + 4 * PARTS
    ROWS = SCORE_ROWS + PARTS
    VW = 32
    VH = NT * HH * VW
    STEPS = [(g, c, j) for g in range(2) for c in range(2) for j in range(4 * c + 4)]
    NS = len(STEPS)
    MAX_UNITS = [[(hd, t, kc) for hd in range(g * G, g * G + G) for t in range(NT) for kc in range(1 + (t >= 4))]
                 for g in range(2)]
    NM = len(MAX_UNITS[0])
    def ring_uses(more):
        steps, n = [], 0
        for k in range(NS + 2):
            gaps = [[] for _ in range(5)]
            if more:
                for gap in range(MAX_COUNTS[k]):
                    gaps[gap].append(("max", n))
                    n += 1
            if k == 1:
                gaps[0].insert(0, ("guard", 0, 1))
            if k == 14 and more:
                gaps[0].insert(0, ("guard", 1, 0))
            if k >= 2 and STEPS[k - 2][2] == 4 * STEPS[k - 2][1] + 3:
                gaps[2].insert(0, ("out", STEPS[k - 2][0] * 2 + STEPS[k - 2][1]))
            steps.append(gaps)
        return steps

    MAX_COUNTS = [4] * (NS - 2) + [2] * 4
    RING_USES = [ring_uses(more) for more in (False, True)]
    PROLOGUE_ORDER = [("max", n) for n in range(2 * NM)]
    PROLOGUE_ORDER.insert(NM + 1, ("guard", 1, 0))
    ORDER = [[use for gaps in steps for gap in gaps for use in gap] for steps in RING_USES]
    PROLOGUE_USES, USES = len(PROLOGUE_ORDER), len(ORDER[1])
    assert USES % 3 == 0

    with ExitStack() as ctx:
        def sb(name, shape, dt=F32):
            return ctx.enter_context(nc.sbuf_tensor("b_" + name, shape, dt))

        def sig(name, per, prime=0, unit=1):
            return Signal(ctx, nc, "b_" + name, per, prime, unit)

        eye = sb("eye", [P, P])
        eye_b = sb("eye_b", [P, P], BF16)
        mask_f = sb("mask_f", [P, 2, P])
        mask = sb("mask", [P, 2, P], BF16)
        ramp = {"q": sb("ramp_q", [P, S]), "k": sb("ramp_k", [P, S])}
        sel = {"q": sb("sel_q", [P, PARTS]), "k": sb("sel_k", [P, PARTS])}
        m_all = sb("m_all", [P, H])
        m_part = sb("m_part", [P, PARTS, H], BF16)
        m_rest = sb("m_rest", [P, 2, H])
        m_sel = {"q": sb("m_sel_q", [P, 3, H]), "k": sb("m_sel_k", [P, 3, H])}
        neg_half = sb("neg_half", [P, NT])
        xs = sb("xs", [P, NT, D])
        aug = {k: [sb(f"aug_{k}{i}", [P, HH, S], BF16) for i in range(2)] for k in "qk"}
        v = [sb(f"v{i}", [P, NT, HH, VW]) for i in range(2)]
        cmax = sb("cmax", [P, 2, G, NT, 2])
        guard = sb("guard", [P, 2, G * NT])
        g_full = sb("g_full", [G * NT, 2, P])
        g_rest = sb("g_rest", [G * NT, 2, P])
        g_part = sb("g_part", [G * NT, 2, PARTS, P], BF16)
        pt = sb("pt", [P, 3, G, 512])
        ot = sb("ot", [P, 512])
        rc = sb("rc", [P, 4, G])
        att = sb("att", [P, 2, 4, G, HD])
        h3 = sb("h3", [P, NT, D])
        st = sb("st", [P, NT, 6])
        mv = sb("mv", [P, NT, 2])
        var = sb("var", [P, NT])
        rstd = sb("rstd", [P, NT])
        x3s = sb("x3s", [P, NT, D])
        s_bank = [ctx.enter_context(nc.psum_tensor(f"b_s{i}", [P, 2, 512], F32)) for i in range(2)]
        ring_bank = [ctx.enter_context(nc.psum_tensor(f"b_ring{i}", [P, 512], F32)) for i in range(3)]
        av_bank = ctx.enter_context(nc.psum_tensor("b_av", [P, 512], F32))

        consts = sig("consts", 1, 0, 16)
        const_cast = sig("const_cast", 1)
        m_sel_done = sig("m_sel_done", 1)
        rows_set = sig("rows_set", 2)
        rows_set_2 = sig("rows_set_2", 1)
        xs_in = sig("xs_in", 1, 0, 16)
        aug_in = [[sig(f"aug_in{g}{half}", 12, 0, 16) for half in range(2)] for g in range(2)]
        v_in = sig("v_in", 2, 0, 16)
        ring_ready = sig("ring_ready", 2 * USES)
        ring_read = sig("ring_read", 2 * USES, 3)
        guard_done = sig("guard_done", 2 * 2)
        guard_copied = sig("guard_copied", 2 * 2)
        g_parts_done = sig("g_parts_done", 2 * 2)
        guard_out = sig("guard_out", 2 * 2, 0, 16)
        guard_in = [sig(f"guard_in{g}", 2, 0, 16) for g in range(2)]
        s_ready = sig("s_ready", 2 * NS * 2, 1)
        exp_done = sig("exp_done", 2 * NS * 2, 2)
        av_done = sig("av_done", 2 * NS, 3)
        ot_copied = sig("ot_copied", 2 * 4, 1)
        att_done = sig("att_done", 2 * 4, 1)
        h3_added = sig("h3_added", 2 * 4, 2)
        mv_done = sig("mv_done", 2)
        eps_added = sig("eps_added", 2)
        rstd_done = sig("rstd_done", 2)
        x3_done = sig("x3_done", 2)
        x3_out = sig("x3_out", 1, 1, 16)
        block = ctx.enter_context(nc.Block())

        def width(c, j):
            lo = max(512 * c, P * j)
            return lo, 512 * (c + 1) - lo

        def finished(k):
            g, c, j = STEPS[k]
            return g * 2 + c if j == 4 * c + 3 else None

        def turns(eng, half_turn, prologue=None):
            if prologue:
                prologue()
            with eng.Fori(0, N - 1) as i:
                for half in range(2):
                    half_turn(i, half, True)
            half_turn(N - 1, 0, True)
            half_turn(N - 1, 1, False)

        def number(half, more, use):
            return PROLOGUE_USES + half * USES + ORDER[more].index(use)

        @block.sync
        def _(sp):
            for dst, src in ((eye[:], ident), (mask_f[:], above.rearrange("k p n -> p k n")),
                             (ramp["q"][PROD:ROWS, :], ramp_q), (ramp["k"][PROD:ROWS, :], ramp_k),
                             (sel["q"][PROD:ROWS, :], sel_q), (sel["k"][PROD:ROWS, :], sel_k),
                             (m_all[PROD:ROWS, :], m_rows)):
                sp.dma_start(dst, src).then_inc(consts.sem, 16)

            sp.sem_inc(x3_out.sem, x3_out.start)

            def load_operands(h, hb, g):
                for kind in range(2):
                    dst = aug["qk"[kind]][hb]
                    row = 0
                    for a, count in ((0, 3), (1, 2), (2, 1)):
                        for r in range(count):
                            part = a if kind == 0 else r
                            src = split[bass.ds(h * 2 + kind, 1), part, g * G * HD:g * G * HD + G * HD]
                            sp.dma_start(dst[row:row + HD, g * G:g * G + G, :],
                                         src.rearrange("o (h d) s -> d (o h) s", d=HD)).then_inc(aug_in[g][hb].sem, 16)
                            row += HD

            def load_values(i, half):
                sp.dma_start(v[half][:].rearrange("p t h w -> p (t h w)"),
                             v_d[bass.ds(i, 1), :, half * VH:half * VH + VH].rearrange("o p n -> p (o n)")).then_inc(
                    v_in.sem, 16)

            def guard_rows(i, h, g):
                sp.wait_ge(g_parts_done.sem, g_parts_done.at(i, h * 2 + g))
                sp.dma_start(guard_d[g].rearrange("r p n -> p r n"), g_part[:, g]).then_inc(guard_out.sem, 16)
                sp.wait_ge(guard_out.sem, guard_out.at(i, h * 2 + g))
                sp.sem_inc(ticks.sem, 1)
                sp.dma_start(aug["q"][h % 2][SCORE_ROWS:ROWS, g * G:g * G + G, :],
                             guard_d[g].rearrange("r (h t) n -> r h (t n)", h=G)).then_inc(guard_in[g].sem, 16)

            def half_turn(i, half, more):
                if more:
                    sp.wait_ge(s_ready.sem, s_ready.at(i, half * NS * 2 - 1))
                    sp.sem_inc(ticks.sem, 1)
                    load_operands(i * 2 + half + 1, 1 - half, 1)
                guard_rows(i, half, 1)
                if more:
                    sp.wait_ge(av_done.sem, av_done.at(i, half * NS - 1))
                    sp.sem_inc(ticks.sem, 1)
                    load_values(i + half, 1 - half)
                if not isinstance(i, int):
                    sp.wait_ge(s_ready.sem, s_ready.at(i, half * NS * 2 + NS - 1))
                    sp.sem_inc(ticks.sem, 1)
                    load_operands(i * 2 + half + 2, half, 0)
                if more:
                    guard_rows(i, half + 1, 0)
                if half == 1:
                    sp.wait_ge(x3_done.sem, x3_done.at(i, 1))
                    sp.sem_inc(ticks.sem, 1)
                    sp.dma_start(x3[bass.ds(i, 1)].rearrange("o (t p) d -> p (o t) d", p=P), x3s[:]).then_inc(
                        x3_out.sem, 16)

            def prologue():
                load_operands(0, 0, 0)
                sp.wait_ge(aug_in[0][0].sem, aug_in[0][0].at(0, 11))
                load_operands(0, 0, 1)
                sp.wait_ge(aug_in[1][0].sem, aug_in[1][0].at(0, 11))
                load_values(0, 0)
                load_operands(1, 1, 0)
                guard_rows(0, 0, 0)

            turns(sp, half_turn, prologue)
            sp.wait_ge(x3_out.sem, x3_out.at(N - 1))

        @block.tensor
        def _(pe):
            pe.wait_ge(consts.sem, consts.at(0, 6))
            pe.wait_ge(const_cast.sem, const_cast.at(0))
            pe.sem_inc(av_done.sem, av_done.start)
            pe.sem_inc(s_ready.sem, s_ready.start)

            def row_max(i, at, hb, n):
                g, u = n // NM, n % NM
                q, k = aug["q"][hb], aug["k"][hb]
                hd, t, kc = MAX_UNITS[g][u]
                n_keys = min(512, P * (t + 1) - 512 * kc)
                diagonal = n_keys == P * (t + 1) - 512 * kc
                bank = ring_bank[at % 3]
                pe.wait_ge(ring_read.sem, ring_read.at(i, at - 3))
                mm = pe.matmul(bank[:, 0:n_keys], q[0:SCORE_ROWS, hd, t * P:t * P + P],
                               k[0:SCORE_ROWS, hd, 512 * kc:512 * kc + n_keys], start=True, stop=not diagonal)
                if diagonal:
                    mm = pe.matmul(bank[:, n_keys - P:n_keys], eye_b[:, :], mask[:, 0, :], start=False, stop=True)
                mm.then_inc(ring_ready.sem, 1)

            def turn_guard(i, at, h, g):
                pe.wait_ge(guard_done.sem, guard_done.at(i, h * 2 + g))
                pe.wait_ge(ring_read.sem, ring_read.at(i, at - 3))
                pe.transpose(ring_bank[at % 3][0:G * NT, 0:P], guard[:, g, :], eye[:, :]).then_inc(ring_ready.sem, 1)

            def turn_output(i, at, half, o):
                pe.wait_ge(ot_copied.sem, ot_copied.at(i, half * 4 + o))
                pe.wait_ge(ring_read.sem, ring_read.at(i, at - 3))
                for t in range(4):
                    mm = pe.transpose(ring_bank[at % 3][:, t * P:t * P + P], ot[:, t * P:t * P + P], eye[:, :])
                mm.then_inc(ring_ready.sem, 1)

            def scores(i, half, k, head):
                g, c, j = STEPS[k]
                lo, n = width(c, j)
                pair, hh = head // 2, head % 2
                hd = g * G + head
                diagonal = j >= 4 * c
                if k % 12 == 0 and head == 0:
                    pe.wait_ge(guard_in[g].sem, guard_in[g].at(i, half))
                bank = s_bank[pair]
                if hh == 0:
                    pe.wait_ge(exp_done.sem, exp_done.at(i, (half * NS + k - 1) * 2 + pair))
                mm = pe.matmul(bank[:, hh, 0:n], aug["k"][half][0:ROWS, hd, j * P:j * P + P],
                               aug["q"][half][0:ROWS, hd, lo:lo + n], start=True, stop=not diagonal)
                if diagonal:
                    mm = pe.matmul(bank[:, hh, 0:P], eye_b[:, :], mask[:, 1, :], start=False, stop=True)
                if hh == 1:
                    mm.then_inc(s_ready.sem, 1)

            def values(i, half, k):
                g, c, j = STEPS[k]
                lo, n = width(c, j)
                if k == 0:
                    pe.wait_ge(v_in.sem, v_in.at(i, half))
                pe.wait_ge(exp_done.sem, exp_done.at(i, (half * NS + k) * 2 + 1))
                if j == 0:
                    pe.wait_ge(ot_copied.sem, ot_copied.at(i, half * 4 + g * 2 + c - 1))
                for hh in range(G):
                    mm = pe.matmul(av_bank[hh * VW:hh * VW + VW, lo - 512 * c:512], v[half][:, j, g * G + hh, :],
                                   pt[:, k % 3, hh, 0:n], start=(j == 0), stop=(j == 4 * c + 3))
                mm.then_inc(av_done.sem, 1)

            def half_turn(i, half, more):
                for k in range(NS + 2):
                    for gap, uses in enumerate(RING_USES[more][k]):
                        if gap < 4 and k < NS:
                            scores(i, half, k, gap)
                        for use in uses:
                            at = number(half, more, use)
                            if use[0] == "max":
                                h, g = half + 1, use[1] // NM
                                if use[1] % NM == 0:
                                    pe.wait_ge(aug_in[g][h % 2].sem, aug_in[g][h % 2].at(i, h // 2 * 12 + 11))
                                row_max(i, at, h % 2, use[1])
                            elif use[0] == "guard":
                                turn_guard(i, at, half + use[1], use[2])
                            else:
                                turn_output(i, at, half, use[1])
                    if 1 <= k <= NS:
                        values(i, half, k - 1)

            def prologue():
                for at, use in enumerate(PROLOGUE_ORDER):
                    if use[0] == "guard":
                        turn_guard(0, at, 0, 0)
                    else:
                        if use[1] % NM == 0:
                            g = use[1] // NM
                            pe.wait_ge(aug_in[g][0].sem, aug_in[g][0].at(0, 11))
                            pe.wait_ge(rows_set.sem, rows_set.at(0, g))
                        row_max(0, at, 0, use[1])
                pe.wait_ge(rows_set_2.sem, rows_set_2.at(0))

            turns(pe, half_turn, prologue)

        @block.scalar
        def _(act):
            act.sem_inc(exp_done.sem, exp_done.start)
            act.sem_inc(ot_copied.sem, ot_copied.start)
            r = slice(PROD, ROWS)
            act.wait_ge(m_sel_done.sem, m_sel_done.at(0))
            for kind in "qk":
                for hd in range(HH):
                    ins = act.activation(aug[kind][1][r, hd, :], ramp[kind][r, :], ACT.Identity,
                                         bias=m_sel[kind][r, 2, HH + hd:HH + hd + 1])
            ins.then_inc(rows_set_2.sem, 1)

            def half_turn(i, half, more):
                for k in range(NS + 1):
                    if k < NS:
                        g, c, j = STEPS[k]
                        lo, n = width(c, j)
                        for pair in range(2):
                            act.wait_ge(s_ready.sem, s_ready.at(i, (half * NS + k) * 2 + pair))
                            if pair == 0:
                                act.wait_ge(av_done.sem, av_done.at(i, half * NS + k - 3))
                            act.activation(pt[:, k % 3, 2 * pair:2 * pair + 2, 0:n], s_bank[pair][:, :, 0:n],
                                           ACT.Exp).then_inc(exp_done.sem, 1)
                    if k >= 1 and finished(k - 1) is not None:
                        o = finished(k - 1)
                        act.wait_ge(av_done.sem, av_done.at(i, half * NS + k - 1))
                        act.wait_ge(att_done.sem, att_done.at(i, half * 4 + o - 1))
                        act.activation(ot[:, :], av_bank[:, :], ACT.Copy).then_inc(ot_copied.sem, 1)

            turns(act, half_turn)

        @block.vector
        def _(dve):
            dve.sem_inc(ring_read.sem, ring_read.start)
            dve.sem_inc(att_done.sem, att_done.start)
            dve.wait_ge(consts.sem, consts.at(0, 6))
            def row_max(i, at, n):
                g, u = n // NM, n % NM
                hd, t, kc = MAX_UNITS[g][u]
                n_keys = min(512, P * (t + 1) - 512 * kc)
                dve.wait_ge(ring_ready.sem, ring_ready.at(i, at))
                dve.tensor_reduce(cmax[:, g, hd % G, t, kc:kc + 1], ring_bank[at % 3][:, 0:n_keys], AX.X,
                                  ALU.max).then_inc(ring_read.sem, 1)
                if u == NM - 1:
                    dve.drain()
                    flat = cmax[:, g].rearrange("p h t k -> p (h t) k")
                    dve.tensor_tensor(guard[:, g, :], flat[:, :, 0], flat[:, :, 1], ALU.max).then_inc(
                        guard_done.sem, 1)

            def copy_guard(i, at, h, g):
                dve.wait_ge(ring_ready.sem, ring_ready.at(i, at))
                dve.tensor_copy(g_full[:, g, :], ring_bank[at % 3][0:G * NT, 0:P]).then_inc(ring_read.sem, 1)
                dve.drain()
                dve.sem_inc(guard_copied.sem, 1)

            def output(i, at, half, o):
                dve.wait_ge(ring_ready.sem, ring_ready.at(i, at))
                turned = ring_bank[at % 3][:, :].rearrange("p (t h d) -> p t h d", t=4, h=G)
                dve.reciprocal(rc[:, :, :], turned[:, :, :, HD])
                dve.drain()
                dve.wait_ge(h3_added.sem, h3_added.at(i, half * 4 + o - 2))
                dve.tensor_tensor(att[:, o % 2], turned[:, :, :, 0:HD],
                                  rc[:, :, :].unsqueeze(3).broadcast_to([P, 4, G, HD]), ALU.mult).then_inc(
                    ring_read.sem, 1)
                dve.drain()
                dve.sem_inc(att_done.sem, 1)

            def statistics(i, c):
                dve.wait_ge(h3_added.sem, h3_added.at(i, 6 + c))
                for t in range(4 * c, 4 * c + 4):
                    dve.bn_stats(st[:, t, :], h3[:, t, :])
                dve.drain()
                for t in range(4 * c, 4 * c + 4):
                    ins = dve.bn_aggr(mv[:, t, :], st[:, t, :])
                ins.then_inc(mv_done.sem, 1)

            def half_turn(i, half, more):
                for k in range(NS + 2):
                    for uses in RING_USES[more][k]:
                        for use in uses:
                            at = number(half, more, use)
                            if use[0] == "max":
                                row_max(i, at, use[1])
                            elif use[0] == "guard":
                                copy_guard(i, at, half + use[1], use[2])
                            else:
                                output(i, at, half, use[1])
                    if half == 1 and k in (19, NS + 1):
                        statistics(i, int(k == NS + 1))

            def prologue():
                for at, use in enumerate(PROLOGUE_ORDER):
                    if use[0] == "guard":
                        copy_guard(0, at, 0, 0)
                    else:
                        row_max(0, at, use[1])

            dve.memset(cmax[:], -3e38)
            dve.tensor_copy(eye_b[:], eye[:])
            dve.tensor_copy(mask[:], mask_f[:]).then_inc(const_cast.sem, 1)
            r = slice(PROD, ROWS)
            dve.tensor_copy(m_part[r, 0, :], m_all[r, :])
            dve.drain()
            dve.tensor_tensor(m_rest[r, 0, :], m_all[r, :], m_part[r, 0, :], ALU.subtract)
            dve.drain()
            dve.tensor_copy(m_part[r, 1, :], m_rest[r, 0, :])
            dve.drain()
            dve.tensor_tensor(m_part[r, 2, :], m_rest[r, 0, :], m_part[r, 1, :], ALU.subtract)
            dve.drain()
            for kind in "qk":
                ms = m_sel[kind]
                dve.tensor_scalar(ms[r, 0, :], m_part[r, 0, :], sel[kind][r, 0:1], None, ALU.mult)
                for p in (1, 2):
                    dve.drain()
                    dve.scalar_tensor_tensor(ms[r, p, :], m_part[r, p, :], sel[kind][r, p:p + 1], ms[r, p - 1, :],
                                             ALU.mult, ALU.add)
                dve.drain()
            dve.sem_inc(m_sel_done.sem, 1)
            for g in range(2):
                for kind in "qk":
                    for hd in range(g * G, g * G + G):
                        ins = dve.tensor_scalar(aug[kind][0][r, hd, :], ramp[kind][r, :], m_sel[kind][r, 2, hd:hd + 1],
                                                None, ALU.add)
                ins.then_inc(rows_set.sem, 1)
            prologue()
            turns(dve, half_turn)

        @block.gpsimd
        def _(pool):
            pool.sem_inc(h3_added.sem, h3_added.start)
            pool.memset(neg_half[:, :], -0.5)
            pool.drain()
            pool.dma_start(xs[:], x2[0].rearrange("(t p) d -> p t d", p=P)).then_inc(xs_in.sem, 16)

            def split_guard(i, h, g):
                full, rest, part = g_full[:, g, :], g_rest[:, g, :], g_part[:, g]
                pool.wait_ge(guard_copied.sem, guard_copied.at(i, h * 2 + g))
                pool.sem_inc(pool_ticks.sem, 1)
                pool.tensor_copy(part[:, 0, :], full)
                pool.drain()
                pool.tensor_tensor(rest, full, part[:, 0, :], ALU.subtract)
                pool.drain()
                pool.tensor_copy(part[:, 1, :], rest)
                pool.drain()
                pool.tensor_tensor(part[:, 2, :], rest, part[:, 1, :], ALU.subtract).then_inc(g_parts_done.sem, 1)

            def add_residual(i, half, o):
                g, c = o // 2, o % 2
                if half == 0 and o == 0:
                    pool.wait_ge(xs_in.sem, xs_in.at(i))
                pool.wait_ge(att_done.sem, att_done.at(i, half * 4 + o))
                pool.sem_inc(pool_ticks.sem, 1)
                d0 = half * P + g * G * HD
                tiles = slice(4 * c, 4 * c + 4)
                pool.tensor_tensor(h3[:, tiles, d0:d0 + G * HD], xs[:, tiles, d0:d0 + G * HD],
                                   att[:, o % 2].rearrange("p t h d -> p t (h d)"), ALU.add).then_inc(h3_added.sem, 1)

            def normalise(i, c):
                tiles = slice(4 * c, 4 * c + 4)
                if c == 0:
                    pool.wait_ge(x3_out.sem, x3_out.at(i, -1))
                pool.wait_ge(mv_done.sem, mv_done.at(i, c))
                pool.sem_inc(pool_ticks.sem, 1)
                pool.tensor_scalar(var[:, tiles], mv[:, tiles, 1], EPS, None, ALU.add).then_inc(eps_added.sem, 1)
                pool.wait_ge(eps_added.sem, eps_added.at(i, c))
                pool.tensor_tensor(rstd[:, tiles], var[:, tiles], neg_half[:, tiles], ALU.pow).then_inc(
                    rstd_done.sem, 1)
                pool.wait_ge(rstd_done.sem, rstd_done.at(i, c))
                pool.sem_inc(pool_ticks.sem, 1)
                for t in range(4 * c, 4 * c + 4):
                    ins = pool.tensor_scalar(x3s[:, t, :], h3[:, t, :], mv[:, t, 0:1], rstd[:, t:t + 1],
                                             ALU.subtract, ALU.mult)
                ins.then_inc(x3_done.sem, 1)

            def turn(i, more):
                for half in range(2):
                    split_guard(i, half, 1)
                    add_residual(i, half, 0)
                    add_residual(i, half, 1)
                    if more or half == 0:
                        split_guard(i, half + 1, 0)
                    add_residual(i, half, 2)
                    if half == 1:
                        normalise(i, 0)
                    add_residual(i, half, 3)
                if more:
                    pool.wait_ge(h3_added.sem, h3_added.at(i, 7))
                    pool.sem_inc(pool_ticks.sem, 1)
                    pool.dma_start(xs[:], x2[bass.ds(i + 1, 1)].rearrange("o (t p) d -> p (o t) d", p=P)).then_inc(
                        xs_in.sem, 16)
                normalise(i, 1)

            split_guard(0, 0, 0)
            with pool.Fori(0, N - 1) as i:
                turn(i, True)
            turn(N - 1, False)


def position_attention(nc, x3, ln1_w, ln1_b, ln2_w, ln2_b, w_qkv, w_proj, w_router, ident, resid, xn, logits,
                       ticks, pool_ticks):
    KV, R, HD = 8, 2, 16
    GW = (R + 2) * HD
    E8 = 8
    NP2 = N // 2
    GROUPS = ((0, 4), (4, 8))
    UNITS = 2 * N - 1
    ORDER = {
        "vector": (("front", 0), ("scores", 0), ("add", 0), ("scores", 1), ("add", 1), ("scores", 2), ("add", 2),
            ("scores", 3), ("add", 3), ("less_max", 0), ("scores", 4), ("scores", 5), ("moments", 0), ("scores", 6),
            ("probabilities", 0), ("scores", 7), ("less_max", 1), ("values", 0), ("values", 1), ("values", 2),
            ("probabilities", 1), ("values", 3), ("last_products", 0), ("values", 4), ("values", 5), ("values", 6),
            ("values", 7)),
        "scalar": (("front", 0), ("copies", 0), ("exponentials", 0), ("copies", 1), ("copies", 2),
            ("exponentials", 1), ("tail", 0), ("copies", 3), ("turned", 0)),
        "pool": (("products", 0), ("products", 1), ("products", 2), ("front", 0), ("products", 3), ("products", 4),
            ("products", 5), ("products", 6), ("products", 7), ("tail", 0), ("products", 8), ("products", 9),
            ("products", 10), ("products", 11), ("products", 12), ("products", 13), ("products", 14)),
        "tensor": (("front", 0), ("tail", 0), ("project", 0)),
    }
    OF_NEXT, OF_LAST = ("front", "copies"), ("tail", "add", "moments")
    BUFS = 3
    assert UNITS % BUFS == 0
    with ExitStack() as ctx:
        def sb(name, shape, dt=F32):
            return ctx.enter_context(nc.sbuf_tensor("c_" + name, shape, dt))

        def sig(name, per, prime=0, unit=1):
            return Signal(ctx, nc, "c_" + name, per, prime, unit)

        wq = sb("wq", [P, DC, KV * GW])
        wp = sb("wp", [P, DC, D])
        wr = sb("wr", [P, DC, E8])
        eye = sb("eye", [P, P])
        ln = [sb(f"ln{k}", [P, DC]) for k in range(4)]
        neg_half = sb("neg_half", [P, N])
        x_front = sb("x_front", [P, N, D])
        x_back = sb("x_back", [P, N, D])
        st = sb("st", [P, 2, N, 6])
        mv = sb("mv", [P, 2, N, 2])
        var = sb("var", [P, 2, N])
        rstd = sb("rstd", [P, 2, N])
        minus_mean = sb("minus_mean", [P, 2, N])
        shift = sb("shift", [P, 2, N])
        n1 = sb("n1", [P, N, D])
        ht = sb("ht", [P, 2, DC, 2 * P])
        qkv = [sb(f"qkv{k}", [P, N, KV * GW]) for k in range(2)]
        prod = sb("prod", [P, BUFS, R, N, KV, HD])
        prod_last = sb("prod_last", [P, R, N, KV, HD])
        sc = sb("sc", [P, N * R, N, KV])
        mx = sb("mx", [P, N * R, KV])
        sh = sb("sh", [P, N * R, N, KV])
        ex = sb("ex", [P, N * R, N, KV])
        sm = sb("sm", [P, N * R, KV])
        rs = sb("rs", [P, N * R, KV])
        pn = sb("pn", [P, N * R, N, KV])
        ao = sb("ao", [P, N, KV, R, HD])
        aot = sb("aot", [P, 2, DC, 2 * P])
        ha = sb("ha", [P, N, D])
        rr = sb("rr", [P, N, D])
        n2 = sb("n2", [P, N, D])
        xt = sb("xt", [P, 2, DC, 2 * P])
        lg = sb("lg", [P, N, E8])

        def bank(name):
            return ctx.enter_context(nc.psum_tensor("c_" + name, [P, 512], F32))

        t_bank, p_bank, q_bank = ([bank(f"{name}{k}") for k in range(2)] for name in "tpq")
        l_bank = bank("l")

        consts = sig("consts", 1, 0, 16)
        xf_in = sig("xf_in", 1, 0, 16)
        xb_in = sig("xb_in", 1, 0, 16)
        mv_done = [sig(f"mv_done{k}", 1) for k in range(2)]
        pool_step = [sig(f"pool_step{k}", 2) for k in range(2)]
        shift_done = [sig(f"shift_done{k}", 1) for k in range(2)]
        n1_done = sig("n1_done", NP2)
        t1_ready = sig("t1_ready", NP2)
        t1_copied = sig("t1_copied", NP2, 1)
        q_ready = sig("q_ready", N, 3)
        q_copied = sig("q_copied", N, 2)
        prod_ready = sig("prod_ready", UNITS)
        prod_read = sig("prod_read", UNITS, BUFS)
        sh_done = sig("sh_done", 2)
        exp_done = sig("exp_done", 2)
        pn_done = sig("pn_done", 2)
        ao_done = sig("ao_done", N)
        t2_ready = sig("t2_ready", NP2, 1)
        t2_copied = sig("t2_copied", NP2, 1)
        p_ready = sig("p_ready", NP2, 2)
        p_read = sig("p_read", NP2, 2)
        rr_done = sig("rr_done", 1)
        n2_done = sig("n2_done", NP2, 1)
        t3_ready = sig("t3_ready", NP2, 1)
        t3_copied = sig("t3_copied", NP2, 1)
        l_ready = sig("l_ready", NP2, 2)
        l_copied = sig("l_copied", 1, 1)
        rr_out = sig("rr_out", 1, 1, 16)
        xn_out = sig("xn_out", 1, 1, 16)
        lg_out = sig("lg_out", 1, 1, 16)
        block = ctx.enter_context(nc.Block())

        def turns(eng, turn, front, tail):
            front(0, 0)
            turn(0, 0, False, True)
            turn(1, 1, True, True)
            with eng.Fori(1, NT // 2 - 1) as i:
                for parity in range(2):
                    turn(i * 2 + parity, parity, True, True)
            turn(NT - 2, 0, True, True)
            turn(NT - 1, 1, True, False)
            tail(NT - 1)

        def in_order(engine, work, has_tail, has_front):
            for name, arg in ORDER[engine]:
                if (has_tail or name not in OF_LAST) and (has_front or name not in OF_NEXT):
                    work[name](arg)

        def q_of(kqv, s, r):
            return kqv[:, s, :].rearrange("p (g w) -> p g w", g=KV)[:, :, r * HD:r * HD + HD]

        def kv_of(kqv, s, which):
            at = (R + which) * HD
            return kqv[:, 0:s + 1, :].rearrange("p t (g w) -> p t g w", g=KV)[:, :, :, at:at + HD]

        def score_products(eng, dst, kqv, s, r):
            n = s + 1
            return eng.tensor_tensor(dst[:, r, 0:n], q_of(kqv, s, r).unsqueeze(1).broadcast_to([P, n, KV, HD]),
                                     kv_of(kqv, s, 0), ALU.mult)

        def value_products(eng, dst, kqv, s, r):
            n = s + 1
            return eng.tensor_tensor(dst[:, r, 0:n], pn[:, s * R + r, 0:n, :].unsqueeze(3).broadcast_to([P, n, KV, HD]),
                                     kv_of(kqv, s, 1), ALU.mult)

        def at_positions(dram, j):
            return dram[:, bass.ds(j * P, P), :].rearrange("s p d -> p s d")

        @block.sync
        def _(sp):
            for dst, src in ((wq[:], w_qkv.rearrange("(c p) n -> p c n", p=P)),
                             (wp[:], w_proj.rearrange("(c p) n -> p c n", p=P)),
                             (wr[:], w_router.rearrange("(c p) n -> p c n", p=P)), (eye[:], ident),
                             (ln[0][:], ln1_w), (ln[1][:], ln1_b), (ln[2][:], ln2_w), (ln[3][:], ln2_b)):
                sp.dma_start(dst, src).then_inc(consts.sem, 16)
            for s in (rr_out, xn_out, lg_out):
                sp.sem_inc(s.sem, s.start)

            def load_front(j):
                sp.wait_ge(n1_done.sem, n1_done.at(j - 1, NP2 - 1))
                sp.sem_inc(ticks.sem, 1)
                sp.dma_start(x_front[:], at_positions(x3, j)).then_inc(xf_in.sem, 16)

            def front(j, parity):
                sp.dma_start(x_front[:], at_positions(x3, 0)).then_inc(xf_in.sem, 16)
                sp.dma_start(x_back[:], at_positions(x3, 0)).then_inc(xb_in.sem, 16)
                load_front(1)

            def store_sum(j):
                sp.wait_ge(rr_done.sem, rr_done.at(j))
                sp.sem_inc(ticks.sem, 1)
                sp.dma_start(at_positions(resid, j), rr[:]).then_inc(rr_out.sem, 16)

            def store_tail(j):
                sp.wait_ge(n2_done.sem, n2_done.at(j, NP2 - 1))
                sp.sem_inc(ticks.sem, 1)
                sp.dma_start(at_positions(xn, j), n2[:]).then_inc(xn_out.sem, 16)
                sp.wait_ge(l_copied.sem, l_copied.at(j))
                sp.sem_inc(ticks.sem, 1)
                sp.dma_start(logits[bass.ds(j, 1)].rearrange("o p s e -> p o (s e)"),
                             lg[:].rearrange("p (o s) e -> p o (s e)", o=1)).then_inc(lg_out.sem, 16)

            def turn(j, parity, has_tail, has_front):
                if has_tail:
                    store_sum(j - 1)
                    sp.dma_start(x_back[:], at_positions(x3, j)).then_inc(xb_in.sem, 16)
                if has_front and not (isinstance(j, int) and j == NT - 2):
                    load_front(j + 2)
                if has_tail:
                    store_tail(j - 1)

            def tail(j):
                store_sum(j)
                store_tail(j)

            turns(sp, turn, front, tail)
            for s in (rr_out, xn_out, lg_out):
                sp.wait_ge(s.sem, s.at(NT - 1))

        @block.tensor
        def _(pe):
            pe.wait_ge(consts.sem, consts.at(0, 7))
            pe.sem_inc(q_ready.sem, q_ready.start)
            pe.sem_inc(t2_ready.sem, t2_ready.start)
            pe.sem_inc(p_ready.sem, p_ready.start)
            pe.sem_inc(t3_ready.sem, t3_ready.start)
            pe.sem_inc(l_ready.sem, l_ready.start)

            def turned(src, ready, copied, j, products):
                def turn_pair(p):
                    for k in range(DC):
                        for s in (2 * p, 2 * p + 1):
                            c0 = k * 256 + (s % 2) * P
                            mm = pe.transpose(t_bank[p % 2][:, c0:c0 + P], src(s, k), eye[:, :])
                    mm.then_inc(ready.sem, 1)

                for p in range(NP2 + 1):
                    if p < NP2:
                        source_wait(j, ready, p)
                        turn_pair(p)
                    if p:
                        pe.wait_ge(copied.sem, copied.at(j, p - 1))
                        products(p - 1)

            def source_wait(j, ready, p):
                if ready is t1_ready:
                    pe.wait_ge(n1_done.sem, n1_done.at(j, p))
                elif ready is t2_ready:
                    pe.wait_ge(ao_done.sem, ao_done.at(j, 2 * p + 1))
                else:
                    pe.wait_ge(n2_done.sem, n2_done.at(j, p))

            def front(j, parity):
                def products(p):
                    for s in (2 * p, 2 * p + 1):
                        pe.wait_ge(q_copied.sem, q_copied.at(j, s - 2))
                        for k in range(DC):
                            mm = pe.matmul(q_bank[s % 2][:, :], ht[:, p % 2, k, (s % 2) * P:(s % 2) * P + P],
                                           wq[:, k, :], start=(k == 0), stop=(k == DC - 1))
                        mm.then_inc(q_ready.sem, 1)

                turned(lambda s, k: n1[:, s, k * P:k * P + P], t1_ready, t1_copied, j, products)

            def tail(j):
                def products(p):
                    if p == 0:
                        pe.wait_ge(l_copied.sem, l_copied.at(j, -1))
                    for s in (2 * p, 2 * p + 1):
                        for k in range(DC):
                            mm = pe.matmul(l_bank[:, s * E8:s * E8 + E8], xt[:, p % 2, k, (s % 2) * P:(s % 2) * P + P],
                                           wr[:, k, :], start=(k == 0), stop=(k == DC - 1))
                    mm.then_inc(l_ready.sem, 1)

                turned(lambda s, k: n2[:, s, k * P:k * P + P], t3_ready, t3_copied, j, products)

            def turn(j, parity, has_tail, has_front):
                def products(p):
                    pe.wait_ge(p_read.sem, p_read.at(j, p - 2))
                    for s in (2 * p, 2 * p + 1):
                        for k in range(DC):
                            mm = pe.matmul(p_bank[p % 2][:, (s % 2) * D:(s % 2) * D + D],
                                           aot[:, p % 2, k, (s % 2) * P:(s % 2) * P + P], wp[:, k, :],
                                           start=(k == 0), stop=(k == DC - 1))
                    mm.then_inc(p_ready.sem, 1)

                def project(_):
                    turned(lambda s, k: ao[:, s].rearrange("p g r d -> p (g r d)")[:, k * P:k * P + P], t2_ready,
                           t2_copied, j, products)

                in_order("tensor", {"front": lambda _: front(j + 1, 1 - parity), "tail": lambda _: tail(j - 1),
                                    "project": project}, has_tail, has_front)

            turns(pe, turn, front, tail)

        @block.scalar
        def _(act):
            for s in (t1_copied, t2_copied, t3_copied, q_copied, l_copied, n2_done):
                act.sem_inc(s.sem, s.start)
            act.wait_ge(consts.sem, consts.at(0, 7))

            def normalise(j, which, dst, src, done):
                act.wait_ge(shift_done[which].sem, shift_done[which].at(j))
                for s in range(N):
                    ins = act.activation(dst[:, s, :], src[:, s, :], ACT.Identity, bias=shift[:, which, s:s + 1],
                                         scale=rstd[:, which, s:s + 1])
                    if s % 2:
                        ins.then_inc(done.sem, 1)

            def copy_turned(dst, bank_, k, done):
                for c in range(DC):
                    ins = act.activation(dst[:, c, :], bank_[:, c * 2 * P:c * 2 * P + 2 * P], ACT.Identity,
                                         bias=ln[k + 1][:, c:c + 1], scale=ln[k][:, c:c + 1])
                ins.then_inc(done.sem, 1)

            def norm_front(j):
                if not (isinstance(j, int) and j == 0):
                    act.wait_ge(t1_ready.sem, t1_ready.at(j, -1))
                normalise(j, 0, n1, x_front, n1_done)

            def front_turned(j, p):
                act.wait_ge(t1_ready.sem, t1_ready.at(j, p))
                act.wait_ge(q_ready.sem, q_ready.at(j, 2 * p - 3))
                copy_turned(ht[:, p % 2], t_bank[p % 2], 0, t1_copied)

            def front_pairs(j, parity, pairs):
                for p in pairs:
                    if p == 0:
                        front_turned(j, 0)
                    if p + 1 < NP2:
                        front_turned(j, p + 1)
                    for s in (2 * p, 2 * p + 1):
                        act.wait_ge(q_ready.sem, q_ready.at(j, s))
                        if s == 0 and not (isinstance(j, int) and j < 2):
                            act.wait_ge(ao_done.sem, ao_done.at(j - 2, N - 1))
                        act.activation(qkv[parity][:, s, :], q_bank[s % 2][:, :], ACT.Copy).then_inc(q_copied.sem, 1)

            def front(j, parity):
                norm_front(j)
                front_pairs(j, parity, range(NP2))

            def tail(j):
                act.wait_ge(t3_ready.sem, t3_ready.at(j, -1))
                act.wait_ge(xn_out.sem, xn_out.at(j, -1))
                normalise(j, 1, n2, ha, n2_done)
                for p in range(NP2):
                    act.wait_ge(t3_ready.sem, t3_ready.at(j, p))
                    act.wait_ge(l_ready.sem, l_ready.at(j, p - 2))
                    copy_turned(xt[:, p % 2], t_bank[p % 2], 2, t3_copied)
                act.wait_ge(l_ready.sem, l_ready.at(j, NP2 - 1))
                act.wait_ge(lg_out.sem, lg_out.at(j, -1))
                act.activation(lg[:].rearrange("p s e -> p (s e)"), l_bank[:, 0:N * E8], ACT.Copy).then_inc(
                    l_copied.sem, 1)

            def exponentials(j, group):
                a, b = GROUPS[group]
                act.wait_ge(sh_done.sem, sh_done.at(j, group))
                act.activation(ex[:, a * R:b * R, 0:b], sh[:, a * R:b * R, 0:b], ACT.Exp, scale=0.25).then_inc(
                    exp_done.sem, 1)

            def turn(j, parity, has_tail, has_front):
                def turned(_):
                    for p in range(NP2):
                        act.wait_ge(t2_ready.sem, t2_ready.at(j, p))
                        act.wait_ge(p_ready.sem, p_ready.at(j, p - 2))
                        act.activation(aot[:, p % 2].rearrange("p c t -> p (c t)"), t_bank[p % 2][:, :],
                                       ACT.Copy).then_inc(t2_copied.sem, 1)

                in_order("scalar", {"front": lambda _: norm_front(j + 1), "tail": lambda _: tail(j - 1),
                                    "copies": lambda p: front_pairs(j + 1, 1 - parity, (p,)),
                                    "exponentials": lambda group: exponentials(j, group), "turned": turned},
                         has_tail, has_front)

            turns(act, turn, front, tail)

        @block.vector
        def _(dve):
            for s in (p_read, prod_read):
                dve.sem_inc(s.sem, s.start)
            dve.memset(sc[:], -BIG)
            dve.drain()

            def moments(which, src):
                for s in range(N):
                    dve.bn_stats(st[:, which, s, :], src[:, s, :])
                dve.drain()
                for s in range(N):
                    ins = dve.bn_aggr(mv[:, which, s, :], st[:, which, s, :])
                ins.then_inc(mv_done[which].sem, 1)

            def front(j, parity):
                dve.wait_ge(xf_in.sem, xf_in.at(j))
                moments(0, x_front)

            def sum_scores(j, parity, s):
                n = s + 1
                dve.wait_ge(prod_ready.sem, prod_ready.at(j, s))
                dve.tensor_reduce(sc[:, s * R:s * R + R, 0:n, :].rearrange("p r t g -> p r (t g)"),
                                  prod[:, s % BUFS, :, 0:n].rearrange("p r t g d -> p r (t g) d"), AX.X,
                                  ALU.add).then_inc(prod_read.sem, 1)

            def less_max(j, group):
                a, b = GROUPS[group]
                rows = slice(a * R, b * R)
                dve.drain()
                dve.tensor_reduce(mx[:, rows], sc[:, rows, 0:b].rearrange("p a t g -> p a g t"), AX.X, ALU.max)
                dve.drain()
                dve.tensor_tensor(sh[:, rows, 0:b], sc[:, rows, 0:b],
                                  mx[:, rows].unsqueeze(2).broadcast_to([P, (b - a) * R, b, KV]),
                                  ALU.subtract).then_inc(sh_done.sem, 1)

            def probabilities(j, group):
                a, b = GROUPS[group]
                rows = slice(a * R, b * R)
                dve.wait_ge(exp_done.sem, exp_done.at(j, group))
                dve.tensor_reduce(sm[:, rows], ex[:, rows, 0:b].rearrange("p a t g -> p a g t"), AX.X, ALU.add)
                dve.drain()
                dve.reciprocal(rs[:, rows], sm[:, rows])
                dve.drain()
                dve.tensor_tensor(pn[:, rows, 0:b], ex[:, rows, 0:b],
                                  rs[:, rows].unsqueeze(2).broadcast_to([P, (b - a) * R, b, KV]),
                                  ALU.mult).then_inc(pn_done.sem, 1)

            def sum_values(j, parity, s):
                if s == 0:
                    dve.wait_ge(t2_ready.sem, t2_ready.at(j, -1))
                if s < N - 1:
                    dve.wait_ge(prod_ready.sem, prod_ready.at(j, N + s))
                    src = prod[:, (N + s) % BUFS]
                else:
                    dve.drain()
                    src = prod_last
                for r in range(R):
                    ins = dve.tensor_reduce(ao[:, s, :, r, :], src[:, r, 0:s + 1].rearrange("p t g d -> p g d t"), AX.X,
                                            ALU.add)
                if s < N - 1:
                    ins.then_inc(prod_read.sem, 1)
                    dve.drain()
                    ins = dve.sem_inc(ao_done.sem, 1)
                else:
                    ins.then_inc(ao_done.sem, 1)

            def add_residual(j, p):
                hp = slice(2 * p, 2 * p + 2)
                if p == 0:
                    dve.wait_ge(xb_in.sem, xb_in.at(j))
                    dve.wait_ge(n2_done.sem, n2_done.at(j, -1))
                    dve.wait_ge(rr_out.sem, rr_out.at(j, -1))
                dve.wait_ge(p_ready.sem, p_ready.at(j, p))
                dve.tensor_tensor(ha[:, hp, :], p_bank[p % 2][:, :].rearrange("p (t d) -> p t d", t=2),
                                  x_back[:, hp, :], ALU.add).then_inc(p_read.sem, 1)
                dve.drain()
                ins = dve.tensor_tensor(rr[:, hp, :], ha[:, hp, :], x_back[:, hp, :], ALU.add)
                if p == NP2 - 1:
                    ins.then_inc(rr_done.sem, 1)

            def turn(j, parity, has_tail, has_front):
                def last_products(_):
                    dve.drain()
                    for r in range(R):
                        value_products(dve, prod_last, qkv[parity], N - 1, r)

                in_order("vector", {"front": lambda _: front(j + 1, 1 - parity),
                                    "scores": lambda s: sum_scores(j, parity, s),
                                    "less_max": lambda group: less_max(j, group),
                                    "probabilities": lambda group: probabilities(j, group),
                                    "values": lambda s: sum_values(j, parity, s), "last_products": last_products,
                                    "add": lambda p: add_residual(j - 1, p),
                                    "moments": lambda _: second_moments(j - 1)}, has_tail, has_front)

            def second_moments(j):
                dve.drain()
                moments(1, ha)

            def tail(j):
                for p in range(NP2):
                    add_residual(j, p)
                second_moments(j)

            turns(dve, turn, front, tail)

        @block.gpsimd
        def _(pool):
            pool.memset(neg_half[:, :], -0.5)
            pool.drain()

            def inverse_std(j, which):
                pool.wait_ge(mv_done[which].sem, mv_done[which].at(j))
                pool.sem_inc(pool_ticks.sem, 1)
                pool.tensor_scalar(minus_mean[:, which, :], mv[:, which, :, 0], -1.0, None, ALU.mult)
                pool.tensor_scalar(var[:, which, :], mv[:, which, :, 1], EPS, None, ALU.add).then_inc(
                    pool_step[which].sem, 1)
                pool.wait_ge(pool_step[which].sem, pool_step[which].at(j, 0))
                pool.tensor_tensor(rstd[:, which, :], var[:, which, :], neg_half[:, :], ALU.pow).then_inc(
                    pool_step[which].sem, 1)
                pool.wait_ge(pool_step[which].sem, pool_step[which].at(j, 1))
                pool.tensor_tensor(shift[:, which, :], minus_mean[:, which, :], rstd[:, which, :], ALU.mult).then_inc(
                    shift_done[which].sem, 1)

            def products(j, parity, u):
                s = u % N
                if u == 0:
                    pool.wait_ge(q_copied.sem, q_copied.at(j, N - 1))
                if u == N or u == N + GROUPS[1][0]:
                    pool.wait_ge(pn_done.sem, pn_done.at(j, int(u > N)))
                pool.wait_ge(prod_read.sem, prod_read.at(j, u - BUFS))
                for r in range(R):
                    ins = (score_products if u < N else value_products)(
                        pool, prod[:, u % BUFS], qkv[parity], s, r)
                ins.then_inc(prod_ready.sem, 1)

            def turn(j, parity, has_tail, has_front):
                in_order("pool", {"front": lambda _: inverse_std(j + 1, 0), "tail": lambda _: inverse_std(j - 1, 1),
                                  "products": lambda u: products(j, parity, u)}, has_tail, has_front)

            turns(pool, turn, lambda j, parity: inverse_std(j, 0), lambda j: inverse_std(j, 1))


EXPERTS = 8
FFN = 1024
CAP = -(-(T * 2 * 5) // (EXPERTS * 4))
CHUNKS = CAP // P
ROWS_ALL = T + CAP
DX = D + EXPERTS
TILES = T // P


def route(nc, logits, before, iota, tile_start, ident, xw, rank_d, bounds_d, spare_rows):
    NTILE = T // P
    E8 = EXPERTS
    with ExitStack() as ctx:
        def sb(name, shape, dt=F32):
            return ctx.enter_context(nc.sbuf_tensor("r_" + name, shape, dt))

        def sem(name):
            return ctx.enter_context(nc.semaphore("r_" + name))

        lg = sb("lg", [P, NTILE, E8])
        tri = sb("tri", [P, P])
        ones = sb("ones", [P, P])
        io = sb("io", [P, NTILE, E8])
        oh = [sb(f"oh{k}", [P, NTILE, E8]) for k in range(2)]
        lg2 = sb("lg2", [P, NTILE, E8])
        eq = [sb(f"eq{k}", [P, NTILE, E8]) for k in range(2)]
        at = [sb(f"at{k}", [P, NTILE, E8]) for k in range(2)]
        best = [sb(f"best{k}", [P, NTILE]) for k in range(2)]
        first = [sb(f"first{k}", [P, NTILE]) for k in range(2)]
        gap = sb("gap", [P, NTILE])
        e2 = sb("e2", [P, NTILE])
        total = sb("total", [P, NTILE])
        prob = sb("prob", [P, 2, NTILE])
        chosen = sb("chosen", [P, NTILE, E8])
        scan = [sb(f"scan{k}", [P, NTILE, E8]) for k in range(7)]
        base = sb("base", [P, NTILE, E8])
        place = sb("place", [P, NTILE, E8])
        pick = [sb(f"pick{k}", [P, NTILE, E8]) for k in range(2)]
        weight = sb("weight", [P, NTILE, E8])
        value = sb("value", [P, NTILE, E8])
        value_u, rest_u = (sb(k, [P, NTILE, E8], U32) for k in ("value_u", "rest_u"))
        parts = sb("parts", [P, 2, NTILE, E8])
        eye = sb("eye", [P, P])
        first_token = sb("first_token", [NTILE, E8])
        rank = sb("rank", [NTILE, E8, 2, P + 1], BF16)
        bounds = sb("bounds", [NTILE, E8, 2])
        zero = sb("zero", [P, CAP // P * D])
        count_bank = [ctx.enter_context(nc.psum_tensor(f"r_count{k}", [P, 512], F32)) for k in range(2)]
        turned_bank = [ctx.enter_context(nc.psum_tensor(f"r_turned{k}", [P, 512], F32)) for k in range(4)]
        bounds_bank = ctx.enter_context(nc.psum_tensor("r_bounds_bank", [P, 512], F32))
        split_done, turned, bounds_ready, rank_done = (
            sem(k) for k in ("split_done", "turned", "bounds_ready", "rank_done"))
        loaded, ones_set, chosen_done, counted = (sem(k) for k in ("loaded", "ones_set", "chosen_done", "counted"))
        gap_done, exp_done, results, stored, zero_set = (
            sem(k) for k in ("gap_done", "exp_done", "results", "stored", "zero_set"))
        block = ctx.enter_context(nc.Block())

        @block.sync
        def _(sp):
            lg_v = lg[:].rearrange("p (s t) e -> p s t e", s=N)
            for t in range(NT):
                sp.dma_start(lg_v[:, :, t, :], logits[t]).then_inc(loaded, 16)
            sp.dma_start(tri[:], before).then_inc(loaded, 16)
            sp.dma_start(io[:], iota).then_inc(loaded, 16)
            sp.dma_start(eye[:], ident).then_inc(loaded, 16)
            sp.dma_start(first_token[:], tile_start).then_inc(loaded, 16)
            sp.wait_ge(zero_set, 1)
            sp.dma_start(spare_rows.rearrange("(p n) d -> p (n d)", p=P), zero[:]).then_inc(stored, 16)
            sp.dma_start(xw[T:T + 1, :], zero[0:1, 0:DX]).then_inc(stored, 16)
            sp.wait_ge(results, 1)
            sp.dma_start(xw[0:T, D:DX].rearrange("(t p) e -> p t e", p=P), weight[:]).then_inc(stored, 16)
            sp.wait_ge(results, 2)
            sp.dma_start(bounds_d, bounds[:].rearrange("t e k -> t (e k)")).then_inc(stored, 16)
            sp.wait_ge(rank_done, 5)
            sp.dma_start(rank_d, rank[:].rearrange("t e k n -> t (e k n)")).then_inc(stored, 16)
            sp.wait_ge(stored, 5 * 16)

        @block.tensor
        def _(pe):
            pe.wait_ge(loaded, (NT + 4) * 16)
            pe.wait_ge(ones_set, 1)
            pe.wait_ge(chosen_done, 1)
            flat = chosen[:].rearrange("p t e -> p (t e)")
            pe.matmul(count_bank[0][:, :], tri[:, :], flat, start=True, stop=True)
            pe.matmul(count_bank[1][:, :], ones[:, :], flat, start=True, stop=True).then_inc(counted, 1)
            pe.wait_ge(split_done, 1)
            for k in range(2):
                for e in range(E8):
                    mm = pe.transpose(turned_bank[2 * k + e // 4][0:NTILE, (e % 4) * P:(e % 4) * P + P],
                                      parts[:, k, :, e], eye[:, :])
                    if e % 4 == 3:
                        mm.then_inc(turned, 1)
            for k, src in enumerate((base, scan[6])):
                for e in range(E8):
                    mm = pe.matmul(bounds_bank[0:NTILE, 2 * e + k:2 * e + k + 1], src[:, :, e], eye[:, 0:1], start=True,
                                   stop=True)
            mm.then_inc(bounds_ready, 1)

        @block.scalar
        def _(act):
            act.wait_ge(gap_done, 1)
            act.activation(e2[:], gap[:], ACT.Exp).then_inc(exp_done, 1)
            for n in range(4):
                act.wait_ge(turned, n + 1)
                half = n % 2
                act.activation(rank[:, 4 * half:4 * half + 4, n // 2, 0:P],
                               turned_bank[n][0:NTILE, :].rearrange("t (e n) -> t e n", e=4), ACT.Copy).then_inc(
                    rank_done, 1)

        @block.vector
        def _(dve):
            def step(ins):
                dve.drain()
                return ins

            def wide(a):
                return a.unsqueeze(2).broadcast_to([P, NTILE, E8])

            dve.memset(ones[:], 1.0).then_inc(ones_set, 1)
            dve.memset(zero[:], 0).then_inc(zero_set, 1)
            dve.wait_ge(loaded, (NT + 4) * 16)
            src = lg
            for k in range(2):
                step(dve.tensor_reduce(best[k][:], src[:], AX.X, ALU.max))
                step(dve.tensor_tensor(eq[k][:], src[:], wide(best[k][:]), ALU.is_equal))
                step(dve.tensor_tensor(at[k][:], eq[k][:], io[:], ALU.mult))
                step(dve.tensor_reduce(first[k][:], at[k][:], AX.X, ALU.min))
                step(dve.tensor_tensor(oh[k][:], io[:], wide(first[k][:]), ALU.is_equal))
                if k == 0:
                    step(dve.scalar_tensor_tensor(lg2[:], oh[0][:], -1e38, lg[:], ALU.mult, ALU.add))
                    src = lg2
            dve.tensor_tensor(chosen[:], oh[0][:], oh[1][:], ALU.add).then_inc(chosen_done, 1)
            dve.tensor_tensor(gap[:], best[1][:], best[0][:], ALU.subtract).then_inc(gap_done, 1)
            dve.wait_ge(exp_done, 1)
            step(dve.tensor_scalar(total[:], e2[:], 1.0, None, ALU.add))
            step(dve.reciprocal(prob[:, 0, :], total[:]))
            dve.tensor_tensor(prob[:, 1, :], prob[:, 0, :], e2[:], ALU.mult)
            dve.wait_ge(counted, 1)
            step(dve.tensor_copy(scan[0][:].rearrange("p t e -> p (t e)"), count_bank[1][:, :]))
            for n in range(6):
                d = 1 << n
                dve.tensor_copy(scan[n + 1][:, 0:d, :], scan[n][:, 0:d, :])
                step(dve.tensor_tensor(scan[n + 1][:, d:, :], scan[n][:, d:, :], scan[n][:, :NTILE - d, :], ALU.add))
            step(dve.tensor_tensor(base[:], scan[6][:], scan[0][:], ALU.subtract))
            step(dve.tensor_tensor(place[:].rearrange("p t e -> p (t e)"), count_bank[0][:, :],
                                   base[:].rearrange("p t e -> p (t e)"), ALU.add))
            step(dve.scalar_tensor_tensor(value[:].rearrange("p t e -> p (t e)"),
                                          place[:].rearrange("p t e -> p (t e)"), 1.0,
                                          chosen[:].rearrange("p t e -> p (t e)"), ALU.add, ALU.mult))
            step(dve.tensor_copy(value_u[:], value[:]))
            step(dve.tensor_scalar(rest_u[:], value_u[:], P - 1, None, ALU.bitwise_and))
            step(dve.tensor_copy(parts[:, 1], rest_u[:]))
            dve.tensor_tensor(parts[:, 0], value[:], parts[:, 1], ALU.subtract).then_inc(split_done, 1)
            for k in range(2):
                dve.tensor_tensor(pick[k][:], oh[k][:], wide(prob[:, k, :]), ALU.mult)
            dve.drain()
            dve.tensor_tensor(weight[:], pick[0][:], pick[1][:], ALU.add).then_inc(results, 1)
            dve.tensor_copy(rank[:, :, 0, P], first_token[:])
            dve.memset(rank[:, :, 1, P:P + 1], 0.0).then_inc(rank_done, 1)
            dve.wait_ge(bounds_ready, 1)
            dve.tensor_copy(bounds[:].rearrange("t e k -> t (e k)"), bounds_bank[0:NTILE, 0:2 * E8]).then_inc(
                results, 1)


def slot_rows(nc, rank_d, bounds_d, slot_numbers, place_numbers, token_numbers, spare_numbers, rows_d,
              pool_ticks):
    BLOCK = 512
    BLOCKS = CAP // BLOCK
    PER = BLOCK // P
    PAIRS = EXPERTS // 2
    BANKS = 4
    USES = 2 * BLOCKS * PER // 2
    with ExitStack() as ctx:
        def sb(name, shape, dt=F32):
            return ctx.enter_context(nc.sbuf_tensor("s_" + name, shape, dt))

        def sig(name, per, prime=0, unit=1):
            return Signal(ctx, nc, "s_" + name, per, prime, unit)

        rank_all = sb("rank_all", [P, PAIRS, 2 * (P + 1)], BF16)
        bounds_all = sb("bounds_all", [P, PAIRS, 2])
        rank = sb("rank", [P, 2, 2 * (P + 1)], BF16)
        bounds = sb("bounds", [P, 2])
        slot = sb("slot", [P, CAP])
        place = sb("place", [P, CHUNKS])
        token = sb("token", [P, P])
        spare = sb("spare", [P, 2, CHUNKS])
        beyond = sb("beyond", [P, BLOCKS, BLOCK])
        ends = sb("ends", [P, 1])
        within = sb("within", [P, 2, BLOCK], BF16)
        junk = sb("junk", [P, 2 * PER, P])
        found = sb("found", [P, 2, CHUNKS])
        tile = sb("tile", [P, 2, CHUNKS])
        none = sb("none", [P, 2, CHUNKS])
        row = sb("row", [P, 2, CHUNKS])
        rows = sb("rows", [P, EXPERTS * CHUNKS], U32)
        bank = [ctx.enter_context(nc.psum_tensor(f"s_bank{k}", [P, 512], F32)) for k in range(BANKS)]
        loaded = sig("loaded", 1, 0, 16)
        beyond_done = sig("beyond_done", BLOCKS)
        within_done = sig("within_done", BLOCKS, 1)
        found_ready = sig("found_ready", USES, 2 * PER)
        found_read = sig("found_read", USES, BANKS)
        rows_done = sig("rows_done", 1)
        stored = sig("stored", 1, 0, 16)
        block = ctx.enter_context(nc.Block())

        @block.sync
        def _(sp):
            for k in range(2):
                half = slice(k * TILES, k * TILES + TILES)
                sp.dma_start(rank_all[half], rank_d.rearrange("t (i k n) -> t k i n", k=2, i=PAIRS)[:, k]).then_inc(
                    loaded.sem, 16)
                sp.dma_start(bounds_all[half], bounds_d.rearrange("t (i k n) -> t k i n", k=2, i=PAIRS)[:, k]).then_inc(
                    loaded.sem, 16)
            for dst, src in ((slot[:], slot_numbers), (place[:], place_numbers), (token[:], token_numbers),
                             (spare[:], spare_numbers)):
                sp.dma_start(dst, src).then_inc(loaded.sem, 16)
            sp.wait_ge(rows_done.sem, rows_done.at(PAIRS - 1))
            sp.dma_start(rows_d, rows[:]).then_inc(stored.sem, 16)
            sp.wait_ge(stored.sem, stored.at(0))

        @block.tensor
        def _(pe):
            pe.sem_inc(found_ready.sem, found_ready.start)
            with pe.Fori(0, PAIRS) as i:
                for b in range(BLOCKS):
                    pe.wait_ge(within_done.sem, within_done.at(i, b))
                    for k in range(2):
                        half = slice(k * TILES, k * TILES + TILES)
                        for a in range(PER):
                            use = (b * 2 * PER + k * PER + a) // 2
                            if a % 2 == 0:
                                pe.wait_ge(found_read.sem, found_read.at(i, use - BANKS))
                            for part in range(2):
                                mm = pe.matmul(bank[use % BANKS][:, (a % 2) * (P + 1):(a % 2) * (P + 1) + P + 1],
                                               within[half, b % 2, a * P:a * P + P],
                                               rank[half, 0, part * (P + 1):part * (P + 1) + P + 1],
                                               start=(part == 0), stop=(part == 1))
                            if a % 2 == 1:
                                mm.then_inc(found_ready.sem, 1)

        @block.gpsimd
        def _(pool):
            pool.wait_ge(loaded.sem, loaded.at(0, 7))
            with pool.Fori(0, PAIRS) as i:
                pool.tensor_copy(ends[:].rearrange("p (o k) -> p o k", o=1), bounds_all[:, bass.ds(i, 1), 1:2])
                pool.drain()
                pool.wait_ge(within_done.sem, within_done.at(i, -1))
                pool.sem_inc(pool_ticks.sem, 1)
                for b in range(BLOCKS):
                    pool.tensor_scalar(beyond[:, b, :], slot[:, b * BLOCK:b * BLOCK + BLOCK], ends[:, 0:1], None,
                                       ALU.is_ge).then_inc(beyond_done.sem, 1)
                pool.drain()

        @block.vector
        def _(dve):
            dve.sem_inc(found_read.sem, found_read.start)
            dve.sem_inc(within_done.sem, within_done.start)
            dve.wait_ge(loaded.sem, loaded.at(0, 7))

            def which_slots(i, b):
                numbers = slot[:, b * BLOCK:b * BLOCK + BLOCK]
                dve.wait_ge(found_ready.sem, found_ready.at(i, (b - 1) * PER - 1))
                dve.wait_ge(beyond_done.sem, beyond_done.at(i, b))
                dve.scalar_tensor_tensor(within[:, b % 2, :], numbers, bounds[:, 0:1], beyond[:, b, :], ALU.is_ge,
                                         ALU.subtract).then_inc(within_done.sem, 1)

            def find(i, b):
                for k in range(2):
                    for a in range(PER):
                        use = (b * 2 * PER + k * PER + a) // 2
                        c = b * PER + a
                        at = (a % 2) * (P + 1)
                        if a % 2 == 0:
                            dve.wait_ge(found_ready.sem, found_ready.at(i, use))
                        dve.scalar_tensor_tensor(junk[:, k * PER + a], bank[use % BANKS][:, at:at + P],
                                                 place[:, c:c + 1], token[:], ALU.is_equal, ALU.mult,
                                                 accum_out=found[:, k, c:c + 1])
                        if a % 2 == 1:
                            both = bank[use % BANKS][:, 0:2 * (P + 1)].rearrange("p (c n) -> p c n", c=2)
                            dve.tensor_copy(tile[:, k, c - 1:c + 1], both[:, :, P]).then_inc(found_read.sem, 1)
                dve.drain()

            with dve.Fori(0, PAIRS) as i:
                dve.tensor_copy(rank[:, 0:1, :], rank_all[:, bass.ds(i, 1), :])
                dve.tensor_copy(bounds[:].rearrange("p (o k) -> p o k", o=1), bounds_all[:, bass.ds(i, 1), :])
                dve.drain()
                which_slots(i, 0)
                for b in range(BLOCKS):
                    if b + 1 < BLOCKS:
                        which_slots(i, b + 1)
                    find(i, b)
                dve.scalar_tensor_tensor(none[:], found[:], 0.0, spare[:], ALU.is_equal, ALU.mult)
                dve.tensor_tensor(row[:], found[:], tile[:], ALU.add)
                dve.drain()
                dve.scalar_tensor_tensor(row[:], row[:], -1.0, none[:], ALU.add, ALU.add)
                dve.drain()
                dve.tensor_copy(rows[:, bass.ds(i * (2 * CHUNKS), 2 * CHUNKS)],
                                row[:].rearrange("p k c -> p (k c)")).then_inc(rows_done.sem, 1)
                dve.drain()


def experts(nc, rows_d, xw, ln2_w, ln2_b, w1, w2, ident, rows_all, ticks, pool_ticks):
    NB = 512
    BLOCKS = CAP // NB
    A = NB // P
    FC = FFN // P
    UNITS = 2 * BLOCKS
    H_BANKS = 4
    HID = 4
    TURNS = EXPERTS // 2
    LAG = 4
    RING = LAG + 1
    assert UNITS % RING == 0 and A * 2 == FC
    with ExitStack() as ctx:
        def sb(name, shape, dt=F32):
            return ctx.enter_context(nc.sbuf_tensor("e_" + name, shape, dt))

        def sig(name, per, prime=0, unit=1):
            return Signal(ctx, nc, "e_" + name, per, prime, unit)

        eye = sb("eye", [P, P])
        ln_w = sb("ln_w", [P, DC])
        ln_b = sb("ln_b", [P, DC])
        w1_full = sb("w1_full", [P, DC, FFN])
        w2_full = sb("w2_full", [P, FC, D])
        w1_high, w1_low = (sb("w1_" + part, [P, DC, FFN], F32R) for part in ("high", "low"))
        w2_high, w2_low = (sb("w2_" + part, [P, FC, D], F32R) for part in ("high", "low"))
        row_all = sb("row_all", [P, EXPERTS * CHUNKS], U32)
        weight = sb("weight", [P, RING, A])
        token = sb("token", [P, RING, A], U32)
        row = sb("row", [P, RING, A], U32)
        rows = sb("rows", [P, 2, A, DX])
        xt = sb("xt", [P, 2, NB])
        xt_high, xt_low = (sb("xt_" + part, [P, 2, DC, NB], F32R) for part in ("high", "low"))
        hid = sb("hid", [P, HID, NB])
        hid_high, hid_low = (sb("hid_" + part, [P, 2, FC, NB], F32R) for part in ("high", "low"))
        out = sb("out", [P, 2, A, D])
        t_bank = [ctx.enter_context(nc.psum_tensor(f"e_t{k}", [P, 512], F32)) for k in range(2)]
        h_bank = [ctx.enter_context(nc.psum_tensor(f"e_h{k}", [P, 512], F32)) for k in range(H_BANKS)]
        o_bank = [ctx.enter_context(nc.psum_tensor(f"e_o{k}", [P, 512], F32)) for k in range(2)]
        consts = sig("consts", 1, 0, 16)
        w1_in = sig("w1_in", 2, 0, 16)
        w2_in = sig("w2_in", 2, 0, 16)
        w1_split = sig("w1_split", 2)
        w2_split = sig("w2_split", 2)
        indices = sig("indices", UNITS)
        rows_in = [sig(f"rows_in{k}", BLOCKS * A, 0, 16) for k in range(2)]
        t_ready = sig("t_ready", UNITS * 2)
        t_copied = sig("t_copied", UNITS * 2, 4)
        xt_split = sig("xt_split", UNITS * 2, 2)
        h_ready = sig("h_ready", UNITS * FC, 2 * FC)
        gelu_done = sig("gelu_done", UNITS * FC, H_BANKS)
        hid_split = sig("hid_split", UNITS * FC, HID)
        o_ready = sig("o_ready", UNITS * 2, 4)
        o_copied = sig("o_copied", UNITS * 2, 2)
        added = [sig(f"added{k}", BLOCKS * A, 0, 16) for k in range(2)]
        block = ctx.enter_context(nc.Block())

        def units():
            return [(u, u // BLOCKS, u % BLOCKS) for u in range(UNITS)]

        @block.sync
        def _(sp):
            for dst, src in ((eye, ident), (ln_w, ln2_w), (ln_b, ln2_b), (row_all, rows_d)):
                sp.dma_start(dst[:], src).then_inc(consts.sem, 16)

            def load_w1(e):
                sp.dma_start(w1_full[:], w1[bass.ds(e, 1)].rearrange("o (c p) f -> p (o c) f", p=P)).then_inc(
                    w1_in.sem, 16)

            def load_w2(e):
                sp.dma_start(w2_full[:], w2[bass.ds(e, 1)].rearrange("o (c p) d -> p (o c) d", p=P)).then_inc(
                    w2_in.sem, 16)

            load_w1(0)
            load_w2(0)

            def turn(i, last):
                for u, k, b in units():
                    if b == 0 and not (last and k == 1):
                        sp.wait_ge(w1_split.sem, w1_split.at(i, k))
                        sp.sem_inc(ticks.sem, 1)
                        load_w1(i * 2 + k + 1)
                        sp.wait_ge(w2_split.sem, w2_split.at(i, k))
                        sp.sem_inc(ticks.sem, 1)
                        load_w2(i * 2 + k + 1)

            with sp.Fori(0, TURNS - 1) as i:
                turn(i, False)
            turn(TURNS - 1, True)

        @block.gpsimd
        def _(pool):
            pool.wait_ge(consts.sem, consts.at(0, 3))
            pool.sem_inc(pool_ticks.sem, 1)

            def gather(i, u):
                ring = u % RING
                pool.wait_ge(t_copied.sem, t_copied.at(i, 2 * u - 3))
                if not (isinstance(i, int) and i == 0 and u < RING):
                    v = u - RING
                    pool.wait_ge(added[v % 2].sem, added[v % 2].at(i, (v // 2) * A + A - 1))
                pool.sem_inc(pool_ticks.sem, 1)
                pool.tensor_copy(row[:, ring, :], row_all[:, bass.ds((i * UNITS + u) * A, A)])
                pool.drain()
                pool.tensor_scalar(token[:, ring, :], row[:, ring, :], T, None, ALU.min).then_inc(indices.sem, 1)
                pool.wait_ge(indices.sem, indices.at(i, u))
                pool.sem_inc(pool_ticks.sem, 1)
                for a in range(A):
                    pool.indirect_dma_start(rows[:, u % 2, a, :], None, xw,
                                            bass.IndirectOffsetOnAxis(ap=token[:, ring, a:a + 1], axis=0),
                                            bounds_check=T, oob_is_err=False).then_inc(rows_in[u % 2].sem, 16)

            def add(i, u):
                pool.wait_ge(o_copied.sem, o_copied.at(i, 2 * u + 1))
                if u % BLOCKS == 0 and not (isinstance(i, int) and i * UNITS + u == 0):
                    for v in (u - 1, u - 2):
                        pool.wait_ge(added[v % 2].sem, added[v % 2].at(i, (v // 2) * A + A - 1))
                pool.sem_inc(pool_ticks.sem, 1)
                for a in range(A):
                    pool.indirect_dma_start(rows_all, bass.IndirectOffsetOnAxis(ap=row[:, u % RING, a:a + 1], axis=0),
                                            out[:, u % 2, a, :], None, bounds_check=ROWS_ALL - 1, oob_is_err=True,
                                            compute_op=ALU.add).then_inc(added[u % 2].sem, 16)

            for u, _, _ in units():
                gather(0, u)
                if u >= LAG:
                    add(0, u - LAG)
            with pool.Fori(1, TURNS) as i:
                for u, _, _ in units():
                    gather(i, u)
                    add(i, u - LAG)
            for u in range(UNITS - LAG, UNITS):
                add(TURNS - 1, u)
            for k in range(2):
                pool.wait_ge(added[k].sem, added[k].at(TURNS - 1, BLOCKS * A - 1))

        @block.tensor
        def _(pe):
            pe.wait_ge(consts.sem, consts.at(0, 3))
            pe.sem_inc(h_ready.sem, h_ready.start)
            pe.sem_inc(o_ready.sem, o_ready.start)

            def turned(i, u):
                pe.wait_ge(rows_in[u % 2].sem, rows_in[u % 2].at(i, (u // 2) * A + A - 1))
                for k in range(DC):
                    pe.wait_ge(t_copied.sem, t_copied.at(i, 2 * u + k - 2))
                    for a in range(A):
                        mm = pe.transpose(t_bank[k][:, a * P:a * P + P], rows[:, u % 2, a, k * P:k * P + P], eye[:, :])
                    mm.then_inc(t_ready.sem, 1)

            def up(i, u, e):
                if u % BLOCKS == 0:
                    pe.wait_ge(w1_split.sem, w1_split.at(i, e))
                pe.wait_ge(xt_split.sem, xt_split.at(i, 2 * u + 1))
                for f in range(FC):
                    n = u * FC + f
                    pe.wait_ge(gelu_done.sem, gelu_done.at(i, n - H_BANKS))
                    terms = [(w, x, k) for k in range(DC) for w, x in ((w1_high, xt_high), (w1_high, xt_low),
                                                                      (w1_low, xt_high))]
                    for m, (w, x, k) in enumerate(terms):
                        mm = pe.matmul(h_bank[n % H_BANKS][:, :], w[:, k, f * P:f * P + P], x[:, u % 2, k, :],
                                       start=(m == 0), stop=(m == len(terms) - 1))
                    mm.then_inc(h_ready.sem, 1)

            def down(i, u, e):
                if u % BLOCKS == 0:
                    pe.wait_ge(w2_split.sem, w2_split.at(i, e))
                pe.wait_ge(hid_split.sem, hid_split.at(i, u * FC + FC - 1))
                for pair in range(2):
                    pe.wait_ge(o_copied.sem, o_copied.at(i, 2 * u + pair - 2))
                    for a in (2 * pair, 2 * pair + 1):
                        terms = [(h, w, f) for f in range(FC) for h, w in ((hid_high, w2_high), (hid_high, w2_low),
                                                                          (hid_low, w2_high))]
                        for m, (h, w, f) in enumerate(terms):
                            mm = pe.matmul(o_bank[pair][:, (a % 2) * D:(a % 2) * D + D],
                                           h[:, u % 2, f, a * P:a * P + P], w[:, f, :], start=(m == 0),
                                           stop=(m == len(terms) - 1))
                    mm.then_inc(o_ready.sem, 1)

            def turn(i, first, last):
                for u, e, _ in units():
                    if not (last and u == UNITS - 1):
                        turned(i, u + 1)
                    up(i, u, e)
                    if not (first and u == 0):
                        down(i, u - 1, (u - 1) // BLOCKS)

            turned(0, 0)
            turn(0, True, False)
            with pe.Fori(1, TURNS - 1) as i:
                turn(i, False, False)
            turn(TURNS - 1, False, True)
            down(TURNS - 1, UNITS - 1, 1)

        @block.scalar
        def _(act):
            act.sem_inc(gelu_done.sem, gelu_done.start)
            with act.Fori(0, TURNS) as i:
                for u, _, _ in units():
                    for f in range(FC):
                        n = u * FC + f
                        act.wait_ge(h_ready.sem, h_ready.at(i, n))
                        act.wait_ge(hid_split.sem, hid_split.at(i, n - HID))
                        act.activation(hid[:, n % HID, :], h_bank[n % H_BANKS][:, :], ACT.Gelu).then_inc(
                            gelu_done.sem, 1)

        @block.vector
        def _(dve):
            dve.sem_inc(t_copied.sem, t_copied.start)
            dve.sem_inc(xt_split.sem, xt_split.start)
            dve.sem_inc(hid_split.sem, hid_split.start)
            dve.sem_inc(o_copied.sem, o_copied.start)
            dve.wait_ge(consts.sem, consts.at(0, 3))

            def copy_turned(i, u):
                for k in range(DC):
                    dve.wait_ge(t_ready.sem, t_ready.at(i, 2 * u + k))
                    if k == 0:
                        dve.wait_ge(h_ready.sem, h_ready.at(i, (u - 1) * FC - 1))
                    dve.tensor_scalar(xt[:, k, :], t_bank[k][:, :], ln_w[:, k:k + 1], ln_b[:, k:k + 1], ALU.mult,
                                      ALU.add).then_inc(t_copied.sem, 1)
                    dve.drain()
                    split(xt_high[:, u % 2, k, :], xt_low[:, u % 2, k, :], xt[:, k, :]).then_inc(xt_split.sem, 1)
                    if k == 0:
                        dve.tensor_copy(weight[:, u % RING, :].rearrange("p (a o) -> p a o", o=1),
                                        rows[:, u % 2, :, bass.ds(i * 2 + (D + u // BLOCKS), 1)])

            def split(high, low, full):
                dve.tensor_copy(high, full)
                dve.drain()
                return dve.tensor_tensor(low, full, high, ALU.subtract)

            def split_hidden(i, u):
                for f in range(FC):
                    n = u * FC + f
                    dve.wait_ge(gelu_done.sem, gelu_done.at(i, n))
                    if f == 0:
                        dve.wait_ge(o_ready.sem, o_ready.at(i, 2 * u - 3))
                    split(hid_high[:, u % 2, f, :], hid_low[:, u % 2, f, :], hid[:, n % HID, :]).then_inc(
                        hid_split.sem, 1)

            def split_w1(i, e):
                dve.wait_ge(w1_in.sem, w1_in.at(i, e))
                if not (isinstance(i, int) and i == 0 and e == 0):
                    dve.wait_ge(h_ready.sem, h_ready.at(i, e * BLOCKS * FC - 1))
                split(w1_high[:], w1_low[:], w1_full[:]).then_inc(w1_split.sem, 1)

            def split_w2(i, e):
                dve.wait_ge(w2_in.sem, w2_in.at(i, e))
                if not (isinstance(i, int) and i == 0 and e == 0):
                    dve.wait_ge(o_ready.sem, o_ready.at(i, e * BLOCKS * 2 - 1))
                split(w2_high[:], w2_low[:], w2_full[:]).then_inc(w2_split.sem, 1)

            def copy_out(i, u):
                for pair in range(2):
                    dve.wait_ge(o_ready.sem, o_ready.at(i, 2 * u + pair))
                    if pair == 0 and not (isinstance(i, int) and i == 0 and u < 2):
                        dve.wait_ge(added[u % 2].sem, added[u % 2].at(i, (u // 2) * A - 1))
                    for a in (2 * pair, 2 * pair + 1):
                        ins = dve.tensor_scalar(out[:, u % 2, a, :], o_bank[pair][:, (a % 2) * D:(a % 2) * D + D],
                                                weight[:, u % RING, a:a + 1], None, ALU.mult)
                    ins.then_inc(o_copied.sem, 1)

            def turn(i, first, last):
                for u, e, b in units():
                    if not (last and u == UNITS - 1):
                        copy_turned(i, u + 1)
                    split_hidden(i, u)
                    if b == BLOCKS - 1 and not (last and e == 1):
                        split_w1(i, e + 1)
                    if not (first and u == 0):
                        copy_out(i, u - 1)
                    if b == 0:
                        split_w2(i, e)

            split_w1(0, 0)
            copy_turned(0, 0)
            turn(0, True, False)
            with dve.Fori(1, TURNS - 1) as i:
                turn(i, False, False)
            turn(TURNS - 1, False, True)
            copy_out(TURNS - 1, UNITS - 1)


def final_norm(nc, rows_all, out, ticks, pool_ticks):
    with ExitStack() as ctx:
        def sb(name, shape, dt=F32):
            return ctx.enter_context(nc.sbuf_tensor("o_" + name, shape, dt))

        def sig(name, per, prime=0, unit=1):
            return Signal(ctx, nc, "o_" + name, per, prime, unit)

        neg_half = sb("neg_half", [P, NT])
        r = sb("r", [P, 2, NT, D])
        st = sb("st", [P, NT, 6])
        mv = sb("mv", [P, 2, NT, 2])
        var = sb("var", [P, NT])
        rstd = sb("rstd", [P, 2, NT])
        shift = sb("shift", [P, 2, NT])
        res = sb("res", [P, 2, NT, D])
        r_in = [sig(f"r_in{k}", 1, 0, 16) for k in range(2)]
        mv_done = sig("mv_done", 2)
        pool_step = sig("pool_step", 4)
        shift_done = sig("shift_done", 2)
        res_done = sig("res_done", 2, 2)
        res_out = [sig(f"res_out{k}", 1, 1, 16) for k in range(2)]
        block = ctx.enter_context(nc.Block())

        def sequence(dram, i, k):
            return dram[bass.ds((i * 2 + k) * S, S), :].rearrange("(t p) d -> p t d", p=P)

        def turns(eng, turn):
            with eng.Fori(0, N // 2) as i:
                for k in range(2):
                    turn(i, k)

        @block.sync
        def _(sp):
            for k in range(2):
                sp.sem_inc(res_out[k].sem, res_out[k].start)

            def turn(i, k):
                sp.wait_ge(res_done.sem, res_done.at(i, k - 2))
                sp.sem_inc(ticks.sem, 1)
                sp.dma_start(r[:, k], sequence(rows_all, i, k)).then_inc(r_in[k].sem, 16)

            turns(sp, turn)

        @block.vector
        def _(dve):
            def turn(i, k):
                dve.wait_ge(res_done.sem, res_done.at(i, k - 2))
                dve.wait_ge(r_in[k].sem, r_in[k].at(i))
                for t in range(NT):
                    dve.bn_stats(st[:, t, :], r[:, k, t, :])
                dve.drain()
                for t in range(NT):
                    ins = dve.bn_aggr(mv[:, k, t, :], st[:, t, :])
                ins.then_inc(mv_done.sem, 1)
                dve.drain()

            turns(dve, turn)

        @block.gpsimd
        def _(pool):
            pool.memset(neg_half[:, :], -0.5)
            pool.drain()

            def turn(i, k):
                pool.wait_ge(mv_done.sem, mv_done.at(i, k))
                pool.sem_inc(pool_ticks.sem, 1)
                pool.tensor_scalar(var[:, :], mv[:, k, :, 1], EPS, None, ALU.add).then_inc(pool_step.sem, 1)
                pool.wait_ge(pool_step.sem, pool_step.at(i, 2 * k))
                pool.tensor_tensor(rstd[:, k, :], var[:, :], neg_half[:, :], ALU.pow).then_inc(pool_step.sem, 1)
                pool.wait_ge(pool_step.sem, pool_step.at(i, 2 * k + 1))
                pool.sem_inc(pool_ticks.sem, 1)
                pool.tensor_tensor(var[:, :], mv[:, k, :, 0], rstd[:, k, :], ALU.mult)
                pool.drain()
                pool.tensor_scalar(shift[:, k, :], var[:, :], -1.0, None, ALU.mult).then_inc(shift_done.sem, 1)
                pool.drain()

            turns(pool, turn)

        @block.scalar
        def _(act):
            act.sem_inc(res_done.sem, res_done.start)

            def turn(i, k):
                act.wait_ge(shift_done.sem, shift_done.at(i, k))
                act.wait_ge(res_out[k].sem, res_out[k].at(i, -1))
                for t in range(NT):
                    ins = act.activation(res[:, k, t, :], r[:, k, t, :], ACT.Identity, bias=shift[:, k, t:t + 1],
                                         scale=rstd[:, k, t:t + 1])
                ins.then_inc(res_done.sem, 1)
                act.wait_ge(res_done.sem, res_done.at(i, k))
                act.dma_start(sequence(out, i, k), res[:, k]).then_inc(res_out[k].sem, 16)

            turns(act, turn)
            for k in range(2):
                act.wait_ge(res_out[k].sem, res_out[k].at(N // 2 - 1))


def program(nc, a, out):
    def scratch(name, shape, dt=F32):
        return nc.dram_tensor("d_" + name, shape, dt, kind="Internal").ap()

    spectral = scratch("spectral", [D, D])
    x2 = scratch("x2", [N, S, D])
    x3 = scratch("x3", [N, S, D])
    split = scratch("split", [4 * N, 3, P, S], BF16)
    v_d = scratch("v", [N, P, 2 * NT * 8 * 32])
    guard_d = scratch("guard_d", [2, 3, 32, P], BF16)
    rows_all = scratch("rows_all", [ROWS_ALL, D])
    xw = scratch("xw", [T + 1, DX])
    logits = scratch("logits", [NT, P, N, EXPERTS])
    rank_d = scratch("rank", [TILES, EXPERTS * 2 * (P + 1)], BF16)
    bounds_d = scratch("bounds", [TILES, EXPERTS * 2])
    rows_d = scratch("rows", [P, EXPERTS * CHUNKS], U32)

    with ExitStack() as ctx:
        ticks = [Signal(ctx, nc, name, 1) for name in ("sp_ticks", "pool_ticks")]
        spectral_matrix(nc, a["w_real"], a["w_imag"], a["cos"], a["nsin"], spectral)
        linear_attention_and_spectral(nc, a["xT"], a["x"], a["wq"], a["bq"], a["wk"], a["bk"], a["wv"], a["bv"],
                                      a["wo"], a["bo"], a["ffn_bias"], a["w_kqv"], a["ident"], spectral, x2, split,
                                      v_d, *ticks)
        causal_attention(nc, x2, split, v_d, a["ident"], a["above"], a["ramp_q"], a["ramp_k"], a["sel_q"], a["sel_k"],
                         a["m_rows"], guard_d, x3, *ticks)
        position_attention(nc, x3, a["ln1_w"], a["ln1_b"], a["ln2_w"], a["ln2_b"], a["w_qkv"], a["w_proj"],
                           a["w_router"], a["ident"], rows_all[0:T, :].rearrange("(n s) d -> n s d", n=N),
                           xw[0:T, 0:D].rearrange("(n s) d -> n s d", n=N), logits, *ticks)
        route(nc, logits, a["before"], a["iota"], a["tile_start"], a["ident"], xw, rank_d, bounds_d,
              rows_all[T:ROWS_ALL, :])
        slot_rows(nc, rank_d, bounds_d, a["slot_numbers"], a["place_numbers"], a["token_numbers"],
                  a["spare_numbers"], rows_d, ticks[1])
        experts(nc, rows_d, xw, a["ln2_w"], a["ln2_b"], a["w1"], a["w2"], a["ident"], rows_all, *ticks)
        final_norm(nc, rows_all, out.rearrange("n s d -> (n s) d"), *ticks)


def shape_constants():
    d = np.arange(D)
    angle = 2 * np.pi * (np.outer(d, d) % D) / D
    q = np.arange(P)
    pos = np.arange(S)
    high, low, zero, one = ((pos // P) * P, pos % P, 0 * pos, 0 * pos + 1)
    sel_q = np.zeros((15, 3))
    sel_k = np.zeros((15, 3))
    for part in range(3):
        sel_q[4 * part:4 * part + 2, part] = 1
        sel_k[4 * part + 2:4 * part + 4, part] = 1
    slot = np.arange(CAP)
    by_chunk = slot.reshape(CHUNKS, P).T
    c = {
        "tile_start": np.broadcast_to((np.arange(TILES) * P)[:, None], (TILES, EXPERTS)),
        "slot_numbers": np.broadcast_to(slot, (P, CAP)), "place_numbers": by_chunk + 1,
        "token_numbers": np.broadcast_to(q + 1, (P, P)),
        "spare_numbers": np.stack([T + by_chunk + 1] * 2, axis=1),
        "cos": np.cos(angle), "nsin": -np.sin(angle),
        "ident": np.eye(P),
        "above": np.stack([np.where(q[None, :] > q[:, None], -BIG, 0), np.where(q[None, :] < q[:, None], -BIG, 0)]),
        "ramp_q": np.stack([zero, zero, -high, -low] * 3 + [zero] * 3),
        "ramp_k": np.stack([high, low, zero, zero] * 3 + [-one] * 3),
        "sel_q": sel_q, "sel_k": sel_k,
        "before": q[:, None] < q[None, :],
        "iota": np.broadcast_to(np.arange(-EXPERTS, 0), (P, T // P, EXPERTS)),
    }
    return {k: np.ascontiguousarray(v, dtype=np.float32) for k, v in c.items()}


def kernel(**inputs):
    import concourse.bacc as bacc
    from concourse.bass_utils import run_bass_kernel_spmd

    t = {k: np.asarray(v) for k, v in inputs.items()}

    def by_partition(v):
        return v.reshape(DC, P).T

    def on_all(v):
        return np.broadcast_to(v, (P, 2, D))

    arrays = {
        "x": t["L0_attn_x"], "xT": t["L0_attn_x"].transpose(0, 2, 1),
        "wq": t["L0_attn_Wq"], "wk": t["L0_attn_Wk"], "wv": t["L0_attn_Wv"], "wo": t["L0_attn_Wo"],
        "bq": by_partition(t["L0_attn_bq"]), "bk": by_partition(t["L0_attn_bk"]), "bv": by_partition(t["L0_attn_bv"]),
        "bo": on_all(t["L0_attn_bo"]), "ffn_bias": on_all(t["L0_ffn_bias"]),
        "w_real": t["L0_ffn_w_freq_real"], "w_imag": t["L0_ffn_w_freq_imag"],
        "w_kqv": t["L1_attn_W_kqv"], "m_rows": np.broadcast_to(t["L1_attn_m"].reshape(1, 16), (15, 16)),
        "ln1_w": by_partition(t["L1_ffn_ln1_weight"]), "ln1_b": by_partition(t["L1_ffn_ln1_bias"]),
        "ln2_w": by_partition(t["L1_ffn_ln2_weight"]), "ln2_b": by_partition(t["L1_ffn_ln2_bias"]),
        "w_qkv": t["L1_ffn_qkv_weight"].T, "w_proj": t["L1_ffn_proj_weight"].T,
        "w_router": t["L1_ffn_router_weight"], "w1": t["L1_ffn_moe_w1"], "w2": t["L1_ffn_moe_w2"],
    }
    arrays = {k: np.ascontiguousarray(v) for k, v in arrays.items()}
    arrays.update(shape_constants())
    nc = bacc.Bacc("TRN2", target_bir_lowering=False, num_devices=1)
    a = {k: nc.dram_tensor("in_" + k, v.shape, mybir.dt.from_np(v.dtype), kind="ExternalInput").ap()
         for k, v in arrays.items()}
    out = nc.dram_tensor("out", (N, S, D), F32, kind="ExternalOutput").ap()
    program(nc, a, out)
    r = run_bass_kernel_spmd(nc, [{"in_" + k: v for k, v in arrays.items()}], core_ids=[0])
    return r.results[0]["out"]
```
